# Optimizing a Trainium2 kernel written in Bass

```python
import numpy as np
import jax
import jax.numpy as jnp

def _softmax(x, axis=-1):
    return jax.nn.softmax(x, axis=axis)

def _gelu(x):
    return jax.nn.gelu(x, approximate=True)

def _silu(x):
    return jax.nn.silu(x)

def _sigmoid(x):
    return jax.nn.sigmoid(x)

def _layernorm(x, axis=-1, eps=1e-05):
    m = jnp.mean(x, axis=axis, keepdims=True)
    v = jnp.var(x, axis=axis, keepdims=True)
    return (x - m) / jnp.sqrt(v + eps)

def _scatter_add(tgt, idx, src, axis=0):
    return tgt.at[idx].add(src)

def _segment_sum(src, seg, n):
    return jax.ops.segment_sum(src, seg, n)
kernel_name = 'mk_xattn_ffn_d2_seqx_r4_96589d'

def setup_inputs(seed: int=0):
    np.random.seed(seed)
    _w = jnp.asarray

    def _rec_inputs():
        import jax
        import jax.numpy as jnp
        _rk = jax.random.key(seed)
        x = -0.0002928 + 1 * jax.random.normal(jax.random.fold_in(_rk, 1), (4, 1024, 256), jnp.float32)
        _lenS = 1024 - jax.random.randint(jax.random.fold_in(_rk, 7), (4,), 0, max(1, 1024 // 4) + 1, jnp.int32)
        _lenS2 = 77 - jax.random.randint(jax.random.fold_in(_rk, 8), (4,), 0, max(1, 77 // 4) + 1, jnp.int32)
        _ctx_1024P = jax.random.normal(jax.random.fold_in(_rk, 11), (4, 16, 256), jnp.float32)
        _ctx_1024c = jax.random.dirichlet(jax.random.fold_in(_rk, 511), 0.3 * jnp.ones((16,), jnp.float32), (4, 77))
        _ctx_1024t = jnp.einsum('bsk,bkd->bsd', _ctx_1024c, _ctx_1024P)
        _ctx_1024t = _ctx_1024t * jax.lax.rsqrt(jnp.mean(jnp.square(_ctx_1024t)) + 1e-12) * 0.953939
        ctx_1024 = -1.39393e-06 + 0.999914 * (_ctx_1024t + 0.3 * jax.random.normal(jax.random.fold_in(_rk, 611), (4, 77, 256), jnp.float32))
        return (x, ctx_1024)
    x, ctx_1024 = _rec_inputs()

    def _L0_xattn_setup():
        import jax, jax.numpy as jnp
        import numpy as np
        import math
        D_MODEL = 256
        N_HEADS = 16
        D_HEAD = D_MODEL // N_HEADS
        key = jax.random.key(seed)
        ks = jax.random.split(key, 11)
        N, L, S = (2, 512, 512)
        inp = {'queries': jax.random.normal(ks[0], (N, L, D_MODEL), dtype=jnp.float32), 'keys': jax.random.normal(ks[1], (N, S, D_MODEL), dtype=jnp.float32), 'values': jax.random.normal(ks[2], (N, S, D_MODEL), dtype=jnp.float32), 'Wq': jax.random.normal(ks[3], (D_MODEL, N_HEADS * D_HEAD), dtype=jnp.float32) / math.sqrt(D_MODEL), 'bq': jnp.zeros((N_HEADS * D_HEAD,), dtype=jnp.float32), 'Wk': jax.random.normal(ks[4], (D_MODEL, N_HEADS * D_HEAD), dtype=jnp.float32) / math.sqrt(D_MODEL), 'bk': jnp.zeros((N_HEADS * D_HEAD,), dtype=jnp.float32), 'Wv': jax.random.normal(ks[5], (D_MODEL, N_HEADS * D_HEAD), dtype=jnp.float32) / math.sqrt(D_MODEL), 'bv': jnp.zeros((N_HEADS * D_HEAD,), dtype=jnp.float32), 'Wo': jax.random.normal(ks[6], (N_HEADS * D_HEAD, D_MODEL), dtype=jnp.float32) / math.sqrt(N_HEADS * D_HEAD), 'bo': jnp.zeros((D_MODEL,), dtype=jnp.float32)}
        return inp
    _L0_xattn_all = _L0_xattn_setup()
    _L0_xattn_in = {k: v for k, v in _L0_xattn_all.items() if k in ('Wq', 'bq', 'Wk', 'bk', 'Wv', 'bv', 'Wo', 'bo')}
    del _L0_xattn_all

    def _L0_ffn_setup():
        import jax, jax.numpy as jnp
        import numpy as np
        B, T, D, H, E = (4, 512, 256, 512, 8)
        TOP_K = int(E * 0.25)
        key = jax.random.key(seed)
        ks = jax.random.split(key, 6)
        x = jax.random.normal(ks[0], (B, T, D), dtype=jnp.float32)
        gate = jax.random.normal(ks[1], (D, E), dtype=jnp.float32)
        W1 = jax.random.normal(ks[2], (E, D, H), dtype=jnp.float32) * D ** (-0.5)
        b1 = jnp.zeros((E, H), dtype=jnp.float32)
        W2 = jax.random.normal(ks[3], (E, H, D), dtype=jnp.float32) * H ** (-0.5)
        b2 = jnp.zeros((E, D), dtype=jnp.float32)
        return {'x': x, 'gate': gate, 'W1': W1, 'b1': b1, 'W2': W2, 'b2': b2}
    _L0_ffn_all = _L0_ffn_setup()
    _L0_ffn_in = {k: v for k, v in _L0_ffn_all.items() if k in ('gate', 'W1', 'b1', 'W2', 'b2')}
    del _L0_ffn_all

    def _L1_xattn_setup():
        import jax, jax.numpy as jnp
        import numpy as np
        H, NH, HD = (256, 16, 64)
        INNER = NH * HD
        EPS = 1e-05

        def layernorm(x, g, b):
            mu = jnp.mean(x, axis=-1, keepdims=True)
            var = jnp.var(x, axis=-1, keepdims=True)
            return (x - mu) * jax.lax.rsqrt(var + EPS) * g + b
        key = jax.random.key(seed)
        ks = jax.random.split(key, 10)
        B, N, M = (2, 1024, 256)
        s = 1.0 / np.sqrt(H)
        return {'hidden_states': jax.random.normal(ks[0], (B, N, H), jnp.float32), 'encoder_hidden_states': jax.random.normal(ks[1], (B, M, H), jnp.float32), 'Wq': jax.random.normal(ks[2], (H, INNER), jnp.float32) * s, 'Wk': jax.random.normal(ks[3], (H, INNER), jnp.float32) * s, 'Wv': jax.random.normal(ks[4], (H, INNER), jnp.float32) * s, 'Wo': jax.random.normal(ks[5], (INNER, H), jnp.float32) * (1.0 / np.sqrt(INNER)), 'bo': jnp.zeros((H,), jnp.float32), 'q_gamma': jnp.ones((HD,), jnp.float32), 'q_beta': jnp.zeros((HD,), jnp.float32), 'k_gamma': jnp.ones((HD,), jnp.float32), 'k_beta': jnp.zeros((HD,), jnp.float32)}
    _L1_xattn_all = _L1_xattn_setup()
    _L1_xattn_in = {k: v for k, v in _L1_xattn_all.items() if k in ('Wq', 'Wk', 'Wv', 'Wo', 'bo', 'q_gamma', 'q_beta', 'k_gamma', 'k_beta')}
    del _L1_xattn_all

    def _L1_ffn_setup():
        import jax, jax.numpy as jnp
        import numpy as np
        B, S, D = (4, 512, 256)
        E = 8
        DFF = 1024
        CAP_FACTOR = 1.25
        key = jax.random.key(seed)
        ks = jax.random.split(key, 4)
        std_gate = float(np.sqrt(0.1 / D))
        inputs = jax.random.normal(ks[0], (B, S, D), dtype=jnp.float32)
        gate_w = jax.random.normal(ks[1], (E, D), dtype=jnp.float32) * std_gate
        w1 = jax.random.normal(ks[2], (E, D, DFF), dtype=jnp.float32) * (1.0 / np.sqrt(D))
        b1 = jnp.zeros((E, DFF), dtype=jnp.float32)
        w2 = jax.random.normal(ks[3], (E, DFF, D), dtype=jnp.float32) * (1.0 / np.sqrt(DFF))
        b2 = jnp.zeros((E, D), dtype=jnp.float32)
        return {'inputs': inputs, 'gate_w': gate_w, 'w1': w1, 'b1': b1, 'w2': w2, 'b2': b2}
    _L1_ffn_all = _L1_ffn_setup()
    _L1_ffn_in = {k: v for k, v in _L1_ffn_all.items() if k in ('gate_w', 'w1', 'b1', 'w2', 'b2')}
    del _L1_ffn_all
    return {'x': x, 'ctx_1024': ctx_1024, 'L0_xattn_Wq': _L0_xattn_in['Wq'], 'L0_xattn_bq': _L0_xattn_in['bq'], 'L0_xattn_Wk': _L0_xattn_in['Wk'], 'L0_xattn_bk': _L0_xattn_in['bk'], 'L0_xattn_Wv': _L0_xattn_in['Wv'], 'L0_xattn_bv': _L0_xattn_in['bv'], 'L0_xattn_Wo': _L0_xattn_in['Wo'], 'L0_xattn_bo': _L0_xattn_in['bo'], 'L0_ffn_gate': _L0_ffn_in['gate'], 'L0_ffn_W1': _L0_ffn_in['W1'], 'L0_ffn_b1': _L0_ffn_in['b1'], 'L0_ffn_W2': _L0_ffn_in['W2'], 'L0_ffn_b2': _L0_ffn_in['b2'], 'L1_xattn_Wq': _L1_xattn_in['Wq'], 'L1_xattn_Wk': _L1_xattn_in['Wk'], 'L1_xattn_Wv': _L1_xattn_in['Wv'], 'L1_xattn_Wo': _L1_xattn_in['Wo'], 'L1_xattn_bo': _L1_xattn_in['bo'], 'L1_xattn_q_gamma': _L1_xattn_in['q_gamma'], 'L1_xattn_q_beta': _L1_xattn_in['q_beta'], 'L1_xattn_k_gamma': _L1_xattn_in['k_gamma'], 'L1_xattn_k_beta': _L1_xattn_in['k_beta'], 'L1_ffn_gate_w': _L1_ffn_in['gate_w'], 'L1_ffn_w1': _L1_ffn_in['w1'], 'L1_ffn_b1': _L1_ffn_in['b1'], 'L1_ffn_w2': _L1_ffn_in['w2'], 'L1_ffn_b2': _L1_ffn_in['b2']}

def reference(x, ctx_1024, L0_xattn_Wq, L0_xattn_bq, L0_xattn_Wk, L0_xattn_bk, L0_xattn_Wv, L0_xattn_bv, L0_xattn_Wo, L0_xattn_bo, L0_ffn_gate, L0_ffn_W1, L0_ffn_b1, L0_ffn_W2, L0_ffn_b2, L1_xattn_Wq, L1_xattn_Wk, L1_xattn_Wv, L1_xattn_Wo, L1_xattn_bo, L1_xattn_q_gamma, L1_xattn_q_beta, L1_xattn_k_gamma, L1_xattn_k_beta, L1_ffn_gate_w, L1_ffn_w1, L1_ffn_b1, L1_ffn_w2, L1_ffn_b2):
    import jax
    import jax.numpy as jnp

    def _L0_xattn_ref(queries, keys, values, Wq, bq, Wk, bk, Wv, bv, Wo, bo):
        import jax, jax.numpy as jnp
        import numpy as np
        import math
        D_MODEL = 256
        N_HEADS = 16
        D_HEAD = D_MODEL // N_HEADS
        N, L, _ = queries.shape
        S = keys.shape[1]
        H, D = (N_HEADS, D_HEAD)
        q = (queries @ Wq + bq).reshape(N, L, H, D)
        k = (keys @ Wk + bk).reshape(N, S, H, D)
        v = (values @ Wv + bv).reshape(N, S, H, D)
        sm = jnp.einsum('nlhd,nshd->nlhs', q, k) / math.sqrt(D)
        sm = jax.nn.softmax(sm, axis=1)
        attn = jnp.einsum('nlhs,nshd->nlhd', sm, v).reshape(N, L, H * D)
        return attn @ Wo + bo

    def _L0_ffn_ref(x, gate, W1, b1, W2, b2):
        import jax, jax.numpy as jnp
        import numpy as np
        B, T, D, H, E = (4, 512, 256, 512, 8)
        TOP_K = int(E * 0.25)
        raw_gate = jax.nn.softmax(jnp.einsum('btd,de->bte', x, gate), axis=-1)
        topk_scores, topk_idx = jax.lax.top_k(raw_gate, TOP_K)
        mask = jax.nn.one_hot(topk_idx, E, dtype=raw_gate.dtype).sum(axis=-2)
        gate_topk = mask * raw_gate
        gate_topk = gate_topk / jnp.maximum(gate_topk.sum(axis=-1, keepdims=True), 1e-12)
        h = jax.nn.relu(jnp.einsum('btd,edh->beth', x, W1) + b1[None, :, None, :])
        expert_out = jnp.einsum('beth,ehd->betd', h, W2) + b2[None, :, None, :]
        out = jnp.einsum('bte,betd->btd', gate_topk, expert_out)
        return out

    def _L1_xattn_ref(hidden_states, encoder_hidden_states, Wq, Wk, Wv, Wo, bo, q_gamma, q_beta, k_gamma, k_beta):
        import jax, jax.numpy as jnp
        import numpy as np
        H, NH, HD = (256, 16, 64)
        INNER = NH * HD
        EPS = 1e-05

        def layernorm(x, g, b):
            mu = jnp.mean(x, axis=-1, keepdims=True)
            var = jnp.var(x, axis=-1, keepdims=True)
            return (x - mu) * jax.lax.rsqrt(var + EPS) * g + b
        B, N, D = hidden_states.shape
        M = encoder_hidden_states.shape[1]
        q = (hidden_states @ Wq).reshape(B, N, NH, HD).transpose(0, 2, 1, 3)
        k = (encoder_hidden_states @ Wk).reshape(B, M, NH, HD).transpose(0, 2, 1, 3)
        v = (encoder_hidden_states @ Wv).reshape(B, M, NH, HD).transpose(0, 2, 1, 3)
        q = layernorm(q, q_gamma, q_beta)
        k = layernorm(k, k_gamma, k_beta)
        scale = HD ** (-0.5)
        scores = jnp.einsum('bhnd,bhmd->bhnm', q, k) * scale
        attn = jax.nn.softmax(scores, axis=-1)
        out = jnp.einsum('bhnm,bhmd->bhnd', attn, v)
        out = out.transpose(0, 2, 1, 3).reshape(B, N, INNER)
        return out @ Wo + bo

    def _L1_ffn_ref(inputs, gate_w, w1, b1, w2, b2):
        import jax, jax.numpy as jnp
        import numpy as np
        B, S, D = (4, 512, 256)
        E = 8
        DFF = 1024
        CAP_FACTOR = 1.25
        d_model = inputs.shape[-1]
        tokens = inputs.reshape(-1, d_model)
        T = tokens.shape[0]
        num_experts = gate_w.shape[0]
        capacity = int(np.ceil(CAP_FACTOR * T / num_experts))
        logits = jnp.einsum('td,ed->te', tokens.astype(jnp.float32), gate_w)
        probs = jax.nn.softmax(logits, axis=-1)
        expert_idx = jnp.argmax(probs, axis=-1)
        mask = jax.nn.one_hot(expert_idx, num_experts, dtype=jnp.float32)
        ranks = jnp.cumsum(mask, axis=0) - 1.0
        keep = (ranks < capacity) * mask
        pos = ranks.astype(jnp.int32)
        sec_mask = jax.nn.one_hot(pos, capacity, dtype=jnp.float32) * keep[:, :, None]
        combine_weights = probs[:, :, None] * sec_mask
        dispatch = jnp.einsum('tec,td->ecd', sec_mask, tokens)
        h = jax.nn.relu(jnp.einsum('ecd,edh->ech', dispatch, w1) + b1[:, None, :])
        expert_out = jnp.einsum('ech,ehd->ecd', h, w2) + b2[:, None, :]
        ans = jnp.einsum('tec,ecd->td', combine_weights, expert_out)
        return ans.reshape(inputs.shape)
    x = x + _L0_xattn_ref(_layernorm(x, axis=-1), ctx_1024, ctx_1024, L0_xattn_Wq, L0_xattn_bq, L0_xattn_Wk, L0_xattn_bk, L0_xattn_Wv, L0_xattn_bv, L0_xattn_Wo, L0_xattn_bo)
    x = x + _L0_ffn_ref(_layernorm(x, axis=-1), L0_ffn_gate, L0_ffn_W1, L0_ffn_b1, L0_ffn_W2, L0_ffn_b2)
    x = x + _L1_xattn_ref(_layernorm(x, axis=-1), ctx_1024, L1_xattn_Wq, L1_xattn_Wk, L1_xattn_Wv, L1_xattn_Wo, L1_xattn_bo, L1_xattn_q_gamma, L1_xattn_q_beta, L1_xattn_k_gamma, L1_xattn_k_beta)
    x = x + _L1_ffn_ref(_layernorm(x, axis=-1), L1_ffn_gate_w, L1_ffn_w1, L1_ffn_b1, L1_ffn_w2, L1_ffn_b2)
    return x

_drawn_inputs = setup_inputs


def setup_inputs(seed=0):
    import zlib

    import numpy as np

    out = dict(_drawn_inputs(seed))
    spreads = {'L0_xattn_bq': (0.0, 0.8),
     'L0_xattn_bk': (0.0, 0.578),
     'L0_xattn_bv': (0.0, 0.365),
     'L0_xattn_bo': (0.0, 0.1),
     'L0_ffn_b1': (0.0, 0.1),
     'L0_ffn_b2': (0.0, 0.1),
     'L1_xattn_bo': (0.0, 0.1),
     'L1_xattn_q_gamma': (1.0, 0.2),
     'L1_xattn_q_beta': (0.0, 0.396),
     'L1_xattn_k_gamma': (1.0, 0.2),
     'L1_xattn_k_beta': (0.0, 0.8),
     'L1_ffn_b1': (0.0, 0.8),
     'L1_ffn_b2': (0.0, 0.567)}
    factors = {}
    for name, (base, spread) in spreads.items():
        noise = np.random.default_rng([zlib.crc32(name.encode()), seed]).standard_normal(out[name].shape)
        drawn = base * np.exp(spread * noise) if base else spread * noise
        out[name] = jnp.asarray(drawn.astype(out[name].dtype))
    for name, factor in factors.items():
        out[name] = (out[name] * factor).astype(out[name].dtype)
    return out
```

```python
from contextlib import ExitStack

import concourse.bass as bass
from concourse import mybir

F32 = mybir.dt.float32
BF16 = mybir.dt.bfloat16
I32 = mybir.dt.int32
ALU = mybir.AluOpType
ACT = mybir.ActivationFunctionType
AX = mybir.AxisListType

P = 128
EPS = 1e-5
RSQRT_SEED = 0x5F3759DF
FAR = 8192.0


class Chain:

    def __init__(self, eng, sem):
        self.eng, self.sem, self.base, self.n = eng, sem, 0, 0

    def step(self, ins):
        ins.then_inc(self.sem, 1)
        self.n += 1

    def link(self, ins):
        self.step(ins)
        self.eng.wait_ge(self.sem, self.base + self.n)

    def enter(self, i, per_pass):
        self.before, self.per = self.base + self.n, per_pass
        self.base, self.n = self.before + i * per_pass, 0

    def leave(self, passes):
        assert self.n == self.per, (self.n, self.per)
        self.base, self.n = self.before + passes * self.per, 0


def rsqrt(dve, chain, out, v, tmp):
    chain.link(dve.tensor_scalar(tmp.bitcast(I32), v.bitcast(I32), 1, None, ALU.logical_shift_right))
    chain.link(dve.tensor_scalar(out.bitcast(I32), tmp.bitcast(I32), -1.0, float(RSQRT_SEED), ALU.mult, ALU.add))
    for _ in range(3):
        chain.link(dve.tensor_tensor(tmp, out, out, ALU.mult))
        chain.link(dve.scalar_tensor_tensor(tmp, tmp, -0.5, v, ALU.mult, ALU.mult))
        chain.link(dve.scalar_tensor_tensor(out, tmp, 1.5, out, ALU.add, ALU.mult))


RSQRT_STEPS = 11


def layernorm(dve, chain, x_tiles, xn_tiles, stats, mv, var, rstd, tmp, ready):
    n = len(x_tiles)
    for k in range(n):
        chain.step(dve.bn_stats(stats[:, k, :], x_tiles[k]))
    dve.wait_ge(chain.sem, chain.base + chain.n)
    m0, q0, m1, q1 = (stats[:, :, c] for c in (1, 2, 4, 5))
    count = float(x_tiles[0].shape[-1])
    chain.step(dve.tensor_tensor(mv[:, :, 0], m0, m1, ALU.add))
    chain.step(dve.tensor_tensor(mv[:, :, 1], q0, q1, ALU.add))
    chain.link(dve.tensor_tensor(tmp, m0, m1, ALU.subtract))
    chain.step(dve.tensor_tensor(var, tmp, tmp, ALU.mult))
    chain.step(dve.tensor_scalar(mv[:, :, 0], mv[:, :, 0], 0.5, None, ALU.mult))
    chain.link(dve.tensor_scalar(mv[:, :, 1], mv[:, :, 1], 1.0 / count, EPS, ALU.mult, ALU.add))
    chain.link(dve.scalar_tensor_tensor(var, var, 0.25, mv[:, :, 1], ALU.mult, ALU.add))
    rsqrt(dve, chain, rstd, var, tmp)
    for k in range(n):
        dve.tensor_scalar(xn_tiles[k], x_tiles[k], mv[:, k, 0:1], rstd[:, k:k + 1],
                          ALU.subtract, ALU.mult).then_inc(ready, 1)


def layernorm_steps(n):
    return n + 7 + RSQRT_STEPS


def build_layers(nc, x, ctx, Wq0, bq0, Wk0, bk0, Wv0, bv0, Wo0, bo0, gate0, W10, b10, W20, b20,
                 Wq1, Wk1, Wv1, Wo1, bo1, gq1, betaq1, gk1, betak1, gate1, W11, b11, W21, b21, out):
    NB, L, D = x.shape
    S = ctx.shape[1]
    T = NB * L
    NT = T // P
    TB = L // P
    KC = D // P
    E, _, H0 = W10.shape
    H1 = W11.shape[2]
    HEADS = 16
    HD0 = D // HEADS
    INNER = Wq1.shape[1]
    HD1 = INNER // HEADS
    TILES0 = 2 * T // P + E
    CAP = -(-5 * T // (4 * E))
    CT = CAP // P
    TILES1 = E * CT
    assert CAP % P == 0

    xn_dram = nc.dram_tensor("xn_scratch", (T, D), F32, kind="Internal").ap()
    y0_dram = nc.dram_tensor("y0_scratch", (TILES0 * P, D), F32, kind="Internal").ap()
    xm_dram = nc.dram_tensor("xm_scratch", (T, D), F32, kind="Internal").ap()
    y1_dram = nc.dram_tensor("y1_scratch", (TILES1 * P, D), F32, kind="Internal").ap()

    top = ExitStack()
    with top:
        x_sb = top.enter_context(nc.sbuf_tensor("x_sb", [P, NT, D], F32))
        ident = top.enter_context(nc.sbuf_tensor("ident", [P, P], F32))
        ctxT = top.enter_context(nc.sbuf_tensor("ctxT", [P, KC, NB * S], F32))
        x4 = x_sb[:, :, :].rearrange("p (n k) d -> p n k d", k=TB)

        attention_0(nc, x, ctx, Wq0, bq0, Wk0, bk0, Wv0, bv0, Wo0, bo0, x_sb, x4, ident, ctxT,
                    NB, L, D, S, TB, KC, HEADS, HD0)
        with ExitStack() as routes:
            r0 = route(nc, "r0", routes, x_sb, x4, ident, gate0, xn_dram, 2, E, TILES0, None,
                       NB, TB, KC, D, NT)
            experts_0(nc, xn_dram, y0_dram, ident, r0, W10, b10, W20, b20, E, D, H0, KC, TILES0)
            combine(nc, "c0", x_sb, y0_dram, r0, 2, NT, D, None)
        attention_1(nc, Wq1, Wk1, Wv1, Wo1, bo1, gq1, betaq1, gk1, betak1, x_sb, ident, ctxT,
                    NB, L, D, S, NT, KC, HEADS, HD1, INNER)
        with ExitStack() as routes:
            r1 = route(nc, "r1", routes, x_sb, x4, ident, gate1, xm_dram, 1, E, TILES1, CAP,
                       NB, TB, KC, D, NT)
            experts_1(nc, xm_dram, y1_dram, ident, r1, W11, b11, W21, b21, E, D, H1, KC, CT, TILES1)
            combine(nc, "c1", x_sb, y1_dram, r1, 1, NT, D, out)


def attention_0(nc, x, ctx, Wq, bq, Wk, bk, Wv, bv, Wo, bo, x_sb, x4, ident, ctxT,
                NB, L, D, S, TB, KC, HEADS, HD):
    HM = P // HD
    JT = -(-HM * S // P)
    PADDED = JT * P
    U = KC * JT
    SCALE = float(HD) ** -0.5
    with ExitStack() as c:
        def sb(name, shape, dt=F32):
            return c.enter_context(nc.sbuf_tensor("a0_" + name, shape, dt))

        def sem(name):
            return c.enter_context(nc.semaphore("a0_" + name))

        wq, wk, wv, wo = (sb(n, [P, KC, D]) for n in ("wq", "wk", "wv", "wo"))
        bqT, bkT = sb("bqT", [P, KC]), sb("bkT", [P, KC])
        bv_b, bo_b = sb("bv_b", [P, D]), sb("bo_b", [P, D])
        ctx_sb = sb("ctx", [S, NB, D])
        kT = sb("kT", [P, KC, NB, S])
        v_sb = sb("v", [S, NB, D])
        head_mask = sb("head_mask", [P, HM])
        v_blocks = sb("v_blocks", [P, NB, KC, JT, P])
        k_blocks = sb("k_blocks", [P, KC, PADDED])
        xn = sb("xn", [P, TB, D])
        xT = sb("xT", [P, KC, L])
        qT = sb("qT", [P, KC, L])
        e_sb = sb("e", [P, 2, L])
        v_scaled = sb("v_scaled", [P, 2, P])
        aT = sb("aT", [P, KC, L])
        stats, mv = sb("stats", [P, TB, 6]), sb("mv", [P, TB, 2])
        var, rstd, tmp = sb("var", [P, TB]), sb("rstd", [P, TB]), sb("tmp", [P, TB])
        mx, nmx = sb("mx", [P, U]), sb("nmx", [P, U])
        sums, rsum = sb("sums", [P, U]), sb("rsum", [P, U])

        x_in, ctx_in, w_in, b_in, v_moved = (sem(n) for n in ("x_in", "ctx_in", "w_in", "b_in", "v_moved"))
        ident_ready, mask_ready, pads_ready = sem("ident_ready"), sem("mask_ready"), sem("pads_ready")
        pool_chain, dve_chain = sem("pool_chain"), sem("dve_chain")
        ctxT_done, ctxT_ready = sem("ctxT_done"), sem("ctxT_ready")
        kv_done, k_ready, v_ready = sem("kv_done"), sem("k_ready"), sem("v_ready")
        xn_ready, kb_ready = sem("xn_ready"), sem("kb_ready")
        bo_added, pool_passed = sem("bo_added"), sem("pool_passed")
        work_full, act_freed, dve_freed = sem("work_full"), sem("act_freed"), sem("dve_freed")
        scores_done, max_ready, exp_done = sem("scores_done"), sem("max_ready"), sem("exp_done")
        vs_ready, pv_done, o_moved = sem("vs_ready"), sem("pv_done"), sem("o_moved")

        pieces = []
        for h in range(HM):
            r, end = h * S, (h + 1) * S
            while r < end:
                n = min(end - r, P - r % P)
                pieces.append((h, r - h * S, n, r // P, r % P))
                r += n
        V_MOVES = len(pieces) * KC

        with ExitStack() as c2:
            ps = c2.enter_context(nc.psum_tensor("a0_setup", [P, 8, 512], F32))
            block = c2.enter_context(nc.Block())

            @block.sync
            def _(sp):
                sp.dma_start(ctx_sb[:], ctx.rearrange("n s d -> s n d")).then_inc(ctx_in, 16)
                for w, src in ((wk, Wk), (wv, Wv), (wq, Wq), (wo, Wo)):
                    sp.dma_start(w[:], src.rearrange("(k p) n -> p k n", p=P)).then_inc(w_in, 16)
                sp.dma_start(x_sb[:], x.rearrange("n (k p) d -> p (n k) d", p=P)).then_inc(x_in, 16)
                sp.wait_ge(v_ready, NB)
                sp.wait_ge(pads_ready, 1)
                for h, s0, n, j, p0 in pieces:
                    for m in range(KC):
                        sp.dma_start(v_blocks[p0:p0 + n, :, m, j, h * HD:(h + 1) * HD],
                                     v_sb[s0:s0 + n, :, m * P + h * HD:m * P + (h + 1) * HD]).then_inc(v_moved, 16)

            @block.scalar
            def _(act):
                act.dma_start(bkT[:], bk.rearrange("(m p) -> p m", p=P), allow_slow_non_contiguous=True).then_inc(b_in, 16)
                act.dma_start(bqT[:], bq.rearrange("(m p) -> p m", p=P), allow_slow_non_contiguous=True).then_inc(b_in, 16)
                act.dma_start(bv_b[:], bv.rearrange("(a d) -> a d", a=1).to_broadcast([P, D])).then_inc(b_in, 16)
                act.dma_start(bo_b[:], bo.rearrange("(a d) -> a d", a=1).to_broadcast([P, D])).then_inc(b_in, 16)
                for k in range(KC):
                    act.wait_ge(ctxT_done, k + 1)
                    act.copy(ctxT[:, k, :], ps[:, k, 0:NB * S]).then_inc(ctxT_ready, 1)
                act.wait_ge(b_in, 64)
                for m in range(KC):
                    act.wait_ge(kv_done, m + 1)
                    act.activation(kT[:, m, :, :].rearrange("p n s -> p (n s)"), ps[:, 2 + m, 0:NB * S], ACT.Identity,
                                   bias=bkT[:, m:m + 1]).then_inc(k_ready, 1)

            @block.gpsimd
            def _(pool):
                pool.memset(ident[:], 0.0).then_inc(pool_chain, 1)
                pool.wait_ge(pool_chain, 1)
                pool.affine_select(out=ident[:], in_=ident[:], compare_op=ALU.not_equal, fill=1.0, base=0,
                                   pattern=[[-1, P]], channel_multiplier=1).then_inc(ident_ready, 1)
                pool.memset(head_mask[:], 1.0).then_inc(pool_chain, 1)
                pool.wait_ge(pool_chain, 2)
                pool.affine_select(out=head_mask[:], in_=head_mask[:], compare_op=ALU.is_ge, fill=0.0, base=0,
                                   pattern=[[-HD, HM]], channel_multiplier=1).then_inc(pool_chain, 1)
                pool.wait_ge(pool_chain, 3)
                pool.affine_select(out=head_mask[:], in_=head_mask[:], compare_op=ALU.is_ge, fill=0.0, base=HD - 1,
                                   pattern=[[HD, HM]], channel_multiplier=-1).then_inc(mask_ready, 1)
                pool.memset(v_blocks[:], 0.0).then_inc(pads_ready, 1)

            @block.vector
            def _(dve):
                dve.memset(k_blocks[:], 0.0)
                dve.wait_ge(b_in, 64)
                for n in range(NB):
                    dve.wait_ge(kv_done, KC + n + 1)
                    dve.tensor_tensor(v_sb[:, n, :], ps[0:S, 4 + n, 0:D], bv_b[0:S, :], ALU.add).then_inc(v_ready, 1)

            @block.tensor
            def _(pe):
                pe.wait_ge(ident_ready, 1)
                pe.wait_ge(ctx_in, 16)
                for k in range(KC):
                    for n in range(NB):
                        last = pe.transpose(ps[:, k, n * S:(n + 1) * S], ctx_sb[:, n, k * P:(k + 1) * P],
                                            ident[0:S, 0:S])
                    last.then_inc(ctxT_done, 1)
                pe.wait_ge(ctxT_ready, KC)
                pe.wait_ge(w_in, 64)
                for m in range(KC):
                    for k in range(KC):
                        last = pe.matmul(ps[:, 2 + m, 0:NB * S], wk[:, k, m * P:(m + 1) * P], ctxT[:, k, :],
                                         start=(k == 0), stop=(k == KC - 1))
                    last.then_inc(kv_done, 1)
                for n in range(NB):
                    for k in range(KC):
                        last = pe.matmul(ps[0:S, 4 + n, 0:D], ctxT[:, k, n * S:(n + 1) * S], wv[:, k, :],
                                         start=(k == 0), stop=(k == KC - 1))
                    last.then_inc(kv_done, 1)

        with ExitStack() as c2:
            work = c2.enter_context(nc.psum_tensor("a0_work", [P, 2, 512], F32))
            scores = c2.enter_context(nc.psum_tensor("a0_scores_ps", [P, 2, L], F32))
            o_ps = c2.enter_context(nc.psum_tensor("a0_out_ps", [P, L], F32))
            block = c2.enter_context(nc.Block())
            HALF = L // 2
            TH = TB // 2

            @block.tensor
            def _(pe):
                def unit_scores(n, u):
                    m, j = divmod(u, JT)
                    if u >= 2:
                        pe.wait_ge(exp_done, U * n + u - 1)
                    for h in range(2):
                        last = pe.matmul(scores[:, u % 2, h * HALF:(h + 1) * HALF], k_blocks[:, m, j * P:(j + 1) * P],
                                         qT[:, m, h * HALF:(h + 1) * HALF], start=True, stop=True)
                    last.then_inc(scores_done, 1)

                def unit_values(n, u):
                    m, j = divmod(u, JT)
                    pe.wait_ge(vs_ready, U * n + u + 1)
                    if j == 0 and m > 0:
                        pe.wait_ge(o_moved, KC * n + m)
                    for h in range(2):
                        last = pe.matmul(o_ps[:, h * HALF:(h + 1) * HALF], v_scaled[:, u % 2, :],
                                         e_sb[:, u % 2, h * HALF:(h + 1) * HALF], start=(j == 0), stop=(j == JT - 1))
                    last.then_inc(pv_done, 1)

                with pe.Fori(0, NB) as n:
                    use = 0
                    for h in range(2):
                        pe.wait_ge(xn_ready, TB * n + TH * (h + 1))
                        for k in range(KC):
                            if use >= 2:
                                pe.wait_ge(act_freed, 8 * n + use - 1)
                            for t in range(TH):
                                last = pe.transpose(work[:, use % 2, t * P:(t + 1) * P],
                                                    xn[:, TH * h + t, k * P:(k + 1) * P], ident[:])
                            last.then_inc(work_full, 1)
                            use += 1
                    for h in range(2):
                        for m in range(KC):
                            pe.wait_ge(act_freed, 8 * n + use - 1)
                            for k in range(KC):
                                if m == 0 and k == 0:
                                    pe.wait_ge(act_freed, 8 * n + 2 * h + 2)
                                last = pe.matmul(work[:, use % 2, :], wq[:, k, m * P:(m + 1) * P],
                                                 xT[:, k, h * HALF:(h + 1) * HALF], start=(k == 0), stop=(k == KC - 1))
                            last.then_inc(work_full, 1)
                            use += 1
                    pe.wait_ge(act_freed, 8 * n + 8)
                    pe.wait_ge(kb_ready, KC * n + KC)
                    for u in range(U):
                        unit_scores(n, u)
                        if u:
                            unit_values(n, u - 1)
                    unit_values(n, U - 1)
                    pe.wait_ge(o_moved, KC * n + KC)
                    for w in range(4):
                        if w >= 2:
                            pe.wait_ge(dve_freed, 4 * n + w - 1)
                        for t in range(2):
                            i = 2 * w + t
                            for m in range(KC):
                                last = pe.matmul(work[:, w % 2, t * D:(t + 1) * D], aT[:, m, i * P:(i + 1) * P],
                                                 wo[:, m, :], start=(m == 0), stop=(m == KC - 1))
                        last.then_inc(work_full, 1)
                    pe.wait_ge(dve_freed, 4 * n + 4)

            @block.scalar
            def _(act):
                def unit_exp(n, u):
                    act.wait_ge(max_ready, U * n + u + 1)
                    if u >= 2:
                        act.wait_ge(pv_done, U * n + u - 1)
                    act.activation(e_sb[:, u % 2, :], scores[:, u % 2, :], ACT.Exp, bias=nmx[:, u:u + 1],
                                   scale=SCALE, accum_out=sums[:, u:u + 1]).then_inc(exp_done, 1)

                def move_out(n, m):
                    act.wait_ge(pv_done, U * n + JT * (m + 1))
                    act.copy(aT[:, m, :], o_ps[:, :]).then_inc(o_moved, 1)

                with act.Fori(0, NB) as n:
                    for h in range(2):
                        for k in range(KC):
                            act.wait_ge(work_full, 12 * n + 2 * h + k + 1)
                            act.copy(xT[:, k, h * HALF:(h + 1) * HALF], work[:, k % 2, :]).then_inc(act_freed, 1)
                    for h in range(2):
                        for m in range(KC):
                            act.wait_ge(work_full, 12 * n + 4 + 2 * h + m + 1)
                            act.activation(qT[:, m, h * HALF:(h + 1) * HALF], work[:, m % 2, :], ACT.Identity,
                                           bias=bqT[:, m:m + 1]).then_inc(act_freed, 1)
                    for u in range(U):
                        unit_exp(n, u)
                        if u >= JT and u % JT == 1:
                            move_out(n, u // JT - 1)
                    move_out(n, KC - 1)

            @block.gpsimd
            def _(pool):
                with pool.Fori(0, NB) as n:
                    for k in range(TB):
                        if k == 0:
                            pool.wait_ge(xn_ready, TB * n + TB)
                            alone(pool, pool_passed)
                        pool.tensor_tensor(x4[:, n, k, :], x4[:, n, k, :], bo_b[:], ALU.add).then_inc(bo_added, 1)

            @block.vector
            def _(dve):
                chain = Chain(dve, dve_chain)
                dve.wait_ge(x_in, 16)
                dve.wait_ge(v_moved, 16 * V_MOVES)

                def unit_max(n, u):
                    dve.wait_ge(scores_done, U * n + u + 1)
                    chain.link(dve.tensor_reduce(mx[:, u:u + 1], scores[:, u % 2, :], AX.X, ALU.max))
                    dve.tensor_scalar(nmx[:, u:u + 1], mx[:, u:u + 1], -SCALE, None, ALU.mult).then_inc(max_ready, 1)

                def unit_scale(n, u):
                    m, j = divmod(u, JT)
                    dve.wait_ge(exp_done, U * n + u + 1)
                    chain.link(dve.reciprocal(rsum[:, u:u + 1], sums[:, u:u + 1]))
                    if u >= 2:
                        dve.wait_ge(pv_done, U * n + u - 1)
                    dve.tensor_scalar(v_scaled[:, u % 2, :], v_blocks[:, n, m, j, :], rsum[:, u:u + 1], None,
                                      ALU.mult).then_inc(vs_ready, 1)

                with dve.Fori(0, NB) as n:
                    chain.enter(n, layernorm_steps(TB) + 2 * U)
                    layernorm(dve, chain, [x4[:, n, k, :] for k in range(TB)], [xn[:, k, :] for k in range(TB)],
                              stats, mv, var[:], rstd[:], tmp[:], xn_ready)
                    for m in range(KC):
                        dve.tensor_tensor(k_blocks[:, m, 0:HM * S].rearrange("p (h s) -> p h s", s=S),
                                          kT[:, m, n, :].rearrange("p (a s) -> p a s", a=1).to_broadcast([P, HM, S]),
                                          head_mask[:, :].rearrange("p (h a) -> p h a", a=1).to_broadcast([P, HM, S]),
                                          ALU.mult).then_inc(kb_ready, 1)
                    for u in range(U):
                        unit_max(n, u)
                        if u:
                            unit_scale(n, u - 1)
                    unit_scale(n, U - 1)
                    for w in range(4):
                        dve.wait_ge(work_full, 12 * n + 8 + w + 1)
                        if w == 0:
                            dve.wait_ge(bo_added, TB * n + TB)
                        dve.tensor_tensor(x4[:, n, 2 * w:2 * w + 2, :],
                                          work[:, w % 2, :].rearrange("p (t d) -> p t d", t=2),
                                          x4[:, n, 2 * w:2 * w + 2, :], ALU.add).then_inc(dve_freed, 1)
                    chain.leave(NB)
                    dve.wait_ge(dve_freed, 4 * n + 4)


def alone(eng, passed):
    eng.sem_inc(passed, 1)


class Routes:
    pass


def route(nc, tag, keep, x_sb, x4, ident, gate, xn_dram, K, E, TILES, CAP, NB, TB, KC, D, NT):
    r = Routes()

    def kept(name, shape, dt=F32):
        return keep.enter_context(nc.sbuf_tensor(f"{tag}_{name}", shape, dt))

    r.gates = [kept(f"gate{k}", [P, NT]) for k in range(K)]
    r.slot = [kept(f"slot{k}", [P, NT + 1], I32) for k in range(K)]
    r.token = kept("token", [P, TILES + 1], I32)
    r.expert = kept("expert", [P, TILES], I32)

    with ExitStack() as c:
        def sb(name, shape, dt=F32):
            return c.enter_context(nc.sbuf_tensor(f"{tag}_{name}", shape, dt))

        def sem(name):
            return c.enter_context(nc.semaphore(f"{tag}_{name}"))

        gate_sb = sb("gate_w", [P, KC, E])
        gate_rows = sb("gate_rows", [E, D])
        xn = sb("xn", [P, TB, D])
        xT = sb("xT", [P, KC, TB * P])
        stats, mv = sb("stats", [P, TB, 6]), sb("mv", [P, TB, 2])
        var, rstd, tmp = sb("var", [P, TB]), sb("rstd", [P, TB]), sb("tmp", [P, TB])
        z, p, p2 = sb("z", [P, NT, E]), sb("p", [P, NT, E]), sb("p2", [P, NT, E])
        t1, t2 = sb("t1", [P, NT, E]), sb("t2", [P, NT, E])
        hot = [sb(f"hot{k}", [P, NT, E]) for k in range(K)]
        hot_all = sb("hot_all", [P, NT, E], BF16)
        m1, m2, m3 = sb("m1", [P, NT]), sb("m2", [P, NT]), sb("m3", [P, NT])
        mi, ti, bi = sb("mi", [P, NT], I32), sb("ti", [P, NT], I32), sb("bi", [P, NT], I32)
        tf, bf = sb("tf", [P, NT]), sb("bf", [P, NT])
        slots_f = sb("slots_f", [P, NT, E])
        iota_e = sb("iota_e", [P, E])
        iota_p = sb("iota_p", [P, P])
        iota_t = sb("iota_t", [P, TILES])
        iota_i = sb("iota_i", [P, NT])
        own_p = sb("own_p", [P, 1])
        lower = sb("lower", [P, P], BF16)
        ones = sb("ones", [P, P], BF16)
        count_i, count_t = sb("count_i", [P, E], I32), sb("count_t", [P, E], I32)
        tiles_f, ones_e, upto, first = sb("tiles_f", [P, E]), sb("ones_e", [P, E]), sb("upto", [P, E]), sb("first", [P, E])
        in_row = [sb(f"in_row{k}", [P, NT, P], BF16) for k in range(K)]
        in_tile = [sb(f"in_tile{k}", [P, NT, 2, TILES], BF16) for k in range(K)]
        in_tile_f = sb("in_tile_f", [P, NT, TILES])
        token_f = sb("token_f", [P, TILES])
        tile_e = sb("tile_e", [P, TILES, E])
        tile_s = sb("tile_s", [P, TILES])

        gate_in, xn_out = sem("gate_in"), sem("xn_out")
        consts_ready, pool_chain, dve_chain = sem("consts_ready"), sem("pool_chain"), sem("dve_chain")
        gate_turned, gate_ready = sem("gate_turned"), sem("gate_ready")
        xn_ready, turned, xT_ready, logits_done, z_ready = (sem(s) for s in
                                                            ("xn_ready", "turned", "xT_ready", "logits_done", "z_ready"))
        exp_ready, exp_done, hot_ready, ranks_done = (sem(s) for s in ("exp_ready", "exp_done", "hot_ready", "ranks_done"))
        rows_ready, tokens_done = sem("rows_ready"), sem("tokens_done")
        turn_ps = c.enter_context(nc.psum_tensor(f"{tag}_turn_ps", [P, 2, 512], F32))
        z_ps = c.enter_context(nc.psum_tensor(f"{tag}_z_ps", [P, 2, 512], F32))
        rank_ps = c.enter_context(nc.psum_tensor(f"{tag}_rank_ps", [P, 512], F32))
        count_ps = c.enter_context(nc.psum_tensor(f"{tag}_count_ps", [P, 512], F32))
        token_ps = c.enter_context(nc.psum_tensor(f"{tag}_token_ps", [P, 512], F32))
        block = c.enter_context(nc.Block())
        HALF = TB // 2
        by_rows = tuple(gate.shape) == (E, D)

        @block.sync
        def _(sp):
            if by_rows:
                sp.dma_start(gate_rows[:], gate).then_inc(gate_in, 16)
            else:
                sp.dma_start(gate_sb[:], gate.rearrange("(k p) e -> p k e", p=P)).then_inc(gate_in, 16)
            with sp.Fori(0, NB) as n:
                b = sp.snap(n)
                sp.wait_ge(xn_ready, TB * n + TB)
                sp.dma_start(xn_dram.rearrange("(n k p) d -> n p k d", n=NB, p=P)[b], xn[:]).then_inc(xn_out, 16)
            sp.wait_ge(xn_out, 16 * NB)

        @block.gpsimd
        def _(pool):
            pool.iota(iota_e[:], [[1, E]], base=-E, channel_multiplier=0, allow_small_or_imprecise_dtypes=True)
            pool.iota(iota_p[:], [[1, P]], base=0, channel_multiplier=0, allow_small_or_imprecise_dtypes=True)
            pool.iota(iota_t[:], [[1, TILES]], base=0, channel_multiplier=0, allow_small_or_imprecise_dtypes=True)
            pool.iota(iota_i[:], [[1, NT]], base=0, channel_multiplier=0, allow_small_or_imprecise_dtypes=True)
            pool.iota(own_p[:], [[0, 1]], base=0, channel_multiplier=1, allow_small_or_imprecise_dtypes=True)
            pool.memset(ones_e[:], 1.0)
            pool.memset(r.token[:, TILES:TILES + 1], 0)
            for k in range(K):
                pool.memset(r.slot[k][:, NT:NT + 1], 0)
            pool.memset(ones[:], 1.0)
            pool.memset(lower[:], 1.0).then_inc(pool_chain, 1)
            pool.wait_ge(pool_chain, 1)
            pool.affine_select(out=lower[:], in_=lower[:], compare_op=ALU.is_gt, fill=0.0, base=0,
                               pattern=[[1, P]], channel_multiplier=-1).then_inc(consts_ready, 1)

        @block.tensor
        def _(pe):
            pe.wait_ge(gate_in, 16)
            if by_rows:
                for k in range(KC):
                    last = pe.transpose(count_ps[:, k * E:(k + 1) * E], gate_rows[:, k * P:(k + 1) * P], ident[0:E, 0:E])
                last.then_inc(gate_turned, 1)
                pe.wait_ge(gate_ready, 1)
            with pe.Fori(0, NB) as n:
                use = 0
                for h in range(2):
                    pe.wait_ge(xn_ready, TB * n + HALF * (h + 1))
                    for k in range(KC):
                        if use >= 2:
                            pe.wait_ge(xT_ready, 2 * KC * n + use - 1)
                        for t in range(HALF):
                            last = pe.transpose(turn_ps[:, use % 2, t * P:(t + 1) * P],
                                                xn[:, HALF * h + t, k * P:(k + 1) * P], ident[:])
                        last.then_inc(turned, 1)
                        use += 1
                pe.wait_ge(xT_ready, 2 * KC * n + 2 * KC)
                for t in range(TB):
                    for k in range(KC):
                        last = pe.matmul(z_ps[:, 0, t * E:(t + 1) * E], xT[:, k, t * P:(t + 1) * P], gate_sb[:, k, :],
                                         start=(k == 0), stop=(k == KC - 1))
                last.then_inc(logits_done, 1)
                pe.wait_ge(z_ready, n + 1)
            pe.wait_ge(consts_ready, 1)
            pe.wait_ge(hot_ready, 1)
            h2 = hot_all[:, :, :].rearrange("p i e -> p (i e)")
            for s in range(1, NT):
                pe.matmul(rank_ps[:, s * E:NT * E], ones[:], h2[:, 0:(NT - s) * E], start=(s == 1), stop=False,
                          skip_group_check=True)
            pe.matmul(rank_ps[:, 0:NT * E], lower[:], h2, start=False, stop=True, skip_group_check=True)
            for i in range(NT):
                last = pe.matmul(count_ps[:, 0:E], ones[:], hot_all[:, i, :], start=(i == 0), stop=(i == NT - 1))
            last.then_inc(ranks_done, 1)
            pe.wait_ge(rows_ready, 1)
            for k in range(K):
                for i in range(NT):
                    last = pe.matmul(token_ps[:, 0:2 * TILES], in_row[k][:, i, :],
                                     in_tile[k][:, i, :, :].rearrange("p a t -> p (a t)"),
                                     start=(k == 0 and i == 0), stop=(k == K - 1 and i == NT - 1))
            last.then_inc(tokens_done, 1)

        @block.scalar
        def _(act):
            if by_rows:
                act.wait_ge(gate_turned, 1)
                act.copy(gate_sb[:, :, :].rearrange("p k e -> p (k e)"), count_ps[:, 0:KC * E]).then_inc(gate_ready, 1)
            with act.Fori(0, NB) as n:
                for h in range(2):
                    for k in range(KC):
                        act.wait_ge(turned, 2 * KC * n + 2 * h + k + 1)
                        act.copy(xT[:, k, h * HALF * P:(h + 1) * HALF * P], turn_ps[:, k % 2, :]).then_inc(xT_ready, 1)
            act.wait_ge(exp_ready, 1)
            act.activation(t1[:], t2[:], ACT.Exp).then_inc(exp_done, 1)

        @block.vector
        def _(dve):
            chain = Chain(dve, dve_chain)
            link = chain.link

            def per_token(a):
                return a.rearrange("p (i a) -> p i a", a=1).to_broadcast([P, NT, E])

            def per_expert(a):
                return a.rearrange("p (a e) -> p a e", a=1).to_broadcast([P, NT, E])

            with dve.Fori(0, NB) as n:
                chain.enter(n, layernorm_steps(TB))
                layernorm(dve, chain, [x4[:, n, k, :] for k in range(TB)], [xn[:, k, :] for k in range(TB)],
                          stats, mv, var[:], rstd[:], tmp[:], xn_ready)
                dve.wait_ge(logits_done, n + 1)
                dve.tensor_copy(z[:, :, :].rearrange("p (n k) e -> p n (k e)", k=TB)[:, n, :],
                                z_ps[:, 0, 0:TB * E]).then_inc(z_ready, 1)
                dve.wait_ge(xn_out, 16 * n + 16)
                chain.leave(NB)
            dve.wait_ge(consts_ready, 1)
            dve.wait_ge(z_ready, NB)
            link(dve.tensor_reduce(m1[:], z[:], AX.X, ALU.max))
            dve.tensor_tensor(t2[:], z[:], per_token(m1[:]), ALU.subtract).then_inc(exp_ready, 1)
            dve.wait_ge(exp_done, 1)
            link(dve.tensor_reduce(m2[:], t1[:], AX.X, ALU.add))
            link(dve.reciprocal(m3[:], m2[:]))
            link(dve.tensor_tensor(p[:], t1[:], per_token(m3[:]), ALU.mult))
            left = p
            for k in range(K):
                link(dve.tensor_reduce(r.gates[k][:], left[:], AX.X, ALU.max))
                link(dve.tensor_tensor(t1[:], left[:], per_token(r.gates[k][:]), ALU.is_equal))
                link(dve.tensor_tensor(t2[:], t1[:], per_expert(iota_e[:]), ALU.mult))
                link(dve.tensor_reduce(m1[:], t2[:], AX.X, ALU.min))
                link(dve.tensor_tensor(hot[k][:], per_expert(iota_e[:]), per_token(m1[:]), ALU.is_equal))
                if k + 1 < K:
                    link(dve.scalar_tensor_tensor(p2[:], hot[k][:], -2.0, left[:], ALU.mult, ALU.add))
                    left = p2
            if K == 2:
                link(dve.tensor_tensor(m1[:], r.gates[0][:], r.gates[1][:], ALU.add))
                link(dve.tensor_scalar(m2[:], m1[:], 1e-12, None, ALU.max))
                link(dve.reciprocal(m3[:], m2[:]))
                for k in range(K):
                    link(dve.tensor_tensor(r.gates[k][:], r.gates[k][:], m3[:], ALU.mult))
                dve.tensor_tensor(hot_all[:], hot[0][:], hot[1][:], ALU.add).then_inc(hot_ready, 1)
            else:
                dve.tensor_copy(hot_all[:], hot[0][:]).then_inc(hot_ready, 1)
            dve.wait_ge(ranks_done, 1)
            ranks = rank_ps[:, 0:NT * E].rearrange("p (i e) -> p i e", e=E)
            if CAP is None:
                link(dve.tensor_scalar(count_i[:], count_ps[:, 0:E], float(P - 1), None, ALU.add))
                link(dve.tensor_scalar(count_t[:], count_i[:], P.bit_length() - 1, None, ALU.logical_shift_right))
                link(dve.tensor_copy(tiles_f[:], count_t[:]))
                link(dve.tensor_tensor_scan(upto[:], ones_e[:], tiles_f[:], 0.0, ALU.mult, ALU.add))
                link(dve.tensor_tensor(first[:], upto[:], tiles_f[:], ALU.subtract))
                link(dve.tensor_scalar(first[:], first[:], float(P), None, ALU.mult))
            else:
                link(dve.tensor_scalar(first[:], iota_e[:], float(E), float(CAP), ALU.add, ALU.mult))
                link(dve.tensor_scalar(upto[:], first[:], float(CAP), 1.0 / P, ALU.add, ALU.mult))
            link(dve.tensor_tensor(slots_f[:], ranks, per_expert(first[:]), ALU.add))
            for k in range(K):
                link(dve.tensor_tensor(t1[:], hot[k][:], slots_f[:], ALU.mult))
                link(dve.tensor_reduce(m1[:], t1[:], AX.X, ALU.add))
                if CAP is not None:
                    link(dve.tensor_tensor(t2[:], hot[k][:], ranks, ALU.mult))
                    link(dve.tensor_reduce(m2[:], t2[:], AX.X, ALU.add))
                    link(dve.tensor_scalar(m3[:], m2[:], float(CAP), None, ALU.is_lt))
                    link(dve.tensor_tensor(r.gates[k][:], r.gates[k][:], m3[:], ALU.mult))
                    link(dve.tensor_tensor(m1[:], m1[:], m3[:], ALU.mult))
                    link(dve.tensor_copy(r.slot[k][:, 0:NT], m1[:]))
                    link(dve.tensor_scalar(m3[:], m3[:], -FAR, FAR, ALU.mult, ALU.add))
                    link(dve.tensor_tensor(m1[:], m1[:], m3[:], ALU.add))
                else:
                    link(dve.tensor_copy(r.slot[k][:, 0:NT], m1[:]))
                link(dve.tensor_copy(mi[:], m1[:]))
                link(dve.tensor_scalar(ti[:], mi[:], P.bit_length() - 1, None, ALU.logical_shift_right))
                link(dve.tensor_scalar(bi[:], mi[:], P - 1, None, ALU.bitwise_and))
                link(dve.tensor_copy(tf[:], ti[:]))
                link(dve.tensor_copy(bf[:], bi[:]))
                link(dve.tensor_tensor(in_row[k][:], bf[:, :].rearrange("p (i a) -> p i a", a=1).to_broadcast([P, NT, P]),
                                       iota_p[:, :].rearrange("p (a q) -> p a q", a=1).to_broadcast([P, NT, P]),
                                       ALU.is_equal))
                link(dve.tensor_tensor(in_tile_f[:],
                                       tf[:, :].rearrange("p (i a) -> p i a", a=1).to_broadcast([P, NT, TILES]),
                                       iota_t[:, :].rearrange("p (a q) -> p a q", a=1).to_broadcast([P, NT, TILES]),
                                       ALU.is_equal))
                link(dve.tensor_tensor(in_tile[k][:, :, 0, :], in_tile_f[:],
                                       iota_i[:, :].rearrange("p (i a) -> p i a", a=1).to_broadcast([P, NT, TILES]),
                                       ALU.mult))
                link(dve.tensor_scalar(in_tile[k][:, :, 1, :], in_tile_f[:], own_p[:, 0:1], None, ALU.mult))
            dve.tensor_copy(tf[:], ti[:]).then_inc(rows_ready, 1)
            link(dve.tensor_tensor(tile_e[:], upto[:, :].rearrange("p (a e) -> p a e", a=1).to_broadcast([P, TILES, E]),
                                   iota_t[:, :].rearrange("p (t a) -> p t a", a=1).to_broadcast([P, TILES, E]),
                                   ALU.is_le))
            link(dve.tensor_reduce(tile_s[:], tile_e[:], AX.X, ALU.add))
            link(dve.tensor_scalar(r.expert[:], tile_s[:], float(E - 1), None, ALU.min))
            dve.wait_ge(tokens_done, 1)
            link(dve.tensor_copy(token_f[:], token_ps[:, TILES:2 * TILES]))
            link(dve.scalar_tensor_tensor(r.token[:, 0:TILES], token_ps[:, 0:TILES], float(P), token_f[:],
                                          ALU.mult, ALU.add))
    return r


def experts_0(nc, xn_dram, y_dram, ident, r, W1, b1, W2, b2, E, D, H, KC, TILES):
    HC = H // P
    with ExitStack() as c:
        def sb(name, shape, dt=F32):
            return c.enter_context(nc.sbuf_tensor("e0_" + name, shape, dt))

        def sem(name):
            return c.enter_context(nc.semaphore("e0_" + name))

        w1 = sb("w1", [P, KC, E, H])
        w2 = sb("w2", [P, HC, E, D])
        b1_b, b2_b = sb("b1_b", [P, E, H]), sb("b2_b", [P, E, D])
        index = sb("index", [P, 2], I32)
        xg = sb("xg", [P, 2, D])
        xT = sb("xT", [P, 2, KC * P])
        h_sb = sb("h", [P, 2, H])
        hT = sb("hT", [P, 2, H])
        y_sb = sb("y", [P, 2, D])
        w_in = sem("w_in")
        index_ready = sem("index_ready")
        gathered = [sem(f"gathered{b}") for b in range(2)]
        stored = [sem(f"stored{b}") for b in range(2)]
        x_turned, xT_ready, h_done, h_ready, h_turned, hT_ready, y_done, y_ready = (
            sem(s) for s in ("x_turned", "xT_ready", "h_done", "h_ready", "h_turned", "hT_ready", "y_done", "y_ready"))
        x_ps = c.enter_context(nc.psum_tensor("e0_x_ps", [P, 2, 512], F32))
        h_ps = c.enter_context(nc.psum_tensor("e0_h_ps", [P, 2, 512], F32))
        hT_ps = c.enter_context(nc.psum_tensor("e0_hT_ps", [P, 2, 512], F32))
        y_ps = c.enter_context(nc.psum_tensor("e0_y_ps", [P, 2, 512], F32))
        block = c.enter_context(nc.Block())
        PAIRS = TILES // 2
        W_LOADS = KC + HC + 2
        assert TILES % 2 == 0

        @block.sync
        def _(sp):
            for k in range(KC):
                sp.dma_start(w1[:, k, :, :], W1[:, k * P:(k + 1) * P, :].rearrange("e p h -> p e h")).then_inc(w_in, 16)
            for j in range(HC):
                sp.dma_start(w2[:, j, :, :], W2[:, j * P:(j + 1) * P, :].rearrange("e p d -> p e d")).then_inc(w_in, 16)
            sp.dma_start(b1_b[:, :, :].rearrange("p e h -> p (e h)"),
                         b1.rearrange("(a e) h -> a (e h)", a=1).to_broadcast([P, E * H])).then_inc(w_in, 16)
            sp.dma_start(b2_b[:, :, :].rearrange("p e h -> p (e h)"),
                         b2.rearrange("(a e) h -> a (e h)", a=1).to_broadcast([P, E * D])).then_inc(w_in, 16)
            with sp.Fori(0, PAIRS) as i:
                for b in range(2):
                    t = sp.snap(2 * i + b)
                    sp.wait_ge(y_ready, 2 * i + b + 1)
                    sp.dma_start(y_dram.rearrange("(t p) d -> t p d", p=P)[t], y_sb[:, b, :]).then_inc(stored[b], 16)
            for b in range(2):
                sp.wait_ge(stored[b], 16 * PAIRS)

        @block.gpsimd
        def _(pool):
            pool.tensor_copy(index[:, 0:1], r.token[:, 0:1]).then_inc(index_ready, 1)
            with pool.Fori(0, PAIRS) as i:
                for b in range(2):
                    after = pool.snap(2 * i + b + 1)
                    pool.wait_ge(gathered[1 - b], 16 * i + 16 * b)
                    pool.wait_ge(x_turned, 2 * i)
                    pool.wait_ge(index_ready, 2 * i + b + 1)
                    pool.tensor_copy(index[:, 1 - b:2 - b], r.token[:, bass.ds(after, 1)]).then_inc(index_ready, 1)
                    pool.indirect_dma_start(xg[:, b, :], None, xn_dram,
                                            bass.IndirectOffsetOnAxis(ap=index[:, b:b + 1], axis=0)
                                            ).then_inc(gathered[b], 16)

        @block.tensor
        def _(pe):
            pe.wait_ge(w_in, 16 * W_LOADS)

            def turn_x(i, b):
                pe.wait_ge(gathered[b], 16 * i + 16)
                for k in range(KC):
                    last = pe.transpose(x_ps[:, b, k * P:(k + 1) * P], xg[:, b, k * P:(k + 1) * P], ident[:])
                last.then_inc(x_turned, 1)

            with pe.Fori(0, PAIRS) as i:
                es = [pe.value_load(r.expert[0:1, bass.ds(2 * i + b, 1)], min_val=0, max_val=E - 1) for b in range(2)]
                for b in range(2):
                    turn_x(i, b)
                for b in range(2):
                    pe.wait_ge(xT_ready, 2 * i + b + 1)
                    for k in range(KC):
                        last = pe.matmul(h_ps[:, b, :], xT[:, b, k * P:(k + 1) * P],
                                         w1[:, k, es[b], :], start=(k == 0), stop=(k == KC - 1))
                    last.then_inc(h_done, 1)
                for b in range(2):
                    pe.wait_ge(h_ready, 2 * i + b + 1)
                    for j in range(HC):
                        last = pe.transpose(hT_ps[:, b, j * P:(j + 1) * P], h_sb[:, b, j * P:(j + 1) * P], ident[:])
                    last.then_inc(h_turned, 1)
                for b in range(2):
                    pe.wait_ge(hT_ready, 2 * i + b + 1)
                    pe.wait_ge(y_ready, 2 * i)
                    for j in range(HC):
                        last = pe.matmul(y_ps[:, b, 0:D], hT[:, b, j * P:(j + 1) * P], w2[:, j, es[b], :],
                                         start=(j == 0), stop=(j == HC - 1))
                    last.then_inc(y_done, 1)

        @block.scalar
        def _(act):
            with act.Fori(0, PAIRS) as i:
                for b in range(2):
                    act.wait_ge(x_turned, 2 * i + b + 1)
                    act.copy(xT[:, b, :], x_ps[:, b, 0:KC * P]).then_inc(xT_ready, 1)
                for b in range(2):
                    act.wait_ge(h_turned, 2 * i + b + 1)
                    act.activation(hT[:, b, :], hT_ps[:, b, :], ACT.Relu).then_inc(hT_ready, 1)

        @block.vector
        def _(dve):
            dve.wait_ge(w_in, 16 * W_LOADS)
            with dve.Fori(0, PAIRS) as i:
                es = [dve.value_load(r.expert[0:1, bass.ds(2 * i + b, 1)], min_val=0, max_val=E - 1) for b in range(2)]
                for b in range(2):
                    dve.wait_ge(h_done, 2 * i + b + 1)
                    dve.tensor_tensor(h_sb[:, b, :], h_ps[:, b, :], b1_b[:, es[b], :], ALU.add).then_inc(h_ready, 1)
                for b in range(2):
                    dve.wait_ge(y_done, 2 * i + b + 1)
                    dve.wait_ge(stored[b], 16 * i)
                    dve.tensor_tensor(y_sb[:, b, :], y_ps[:, b, 0:D], b2_b[:, es[b], :], ALU.add).then_inc(y_ready, 1)


def combine(nc, tag, x_sb, y_dram, r, K, NT, D, out):
    with ExitStack() as c:
        def sem(name):
            return c.enter_context(nc.semaphore(f"{tag}_{name}"))

        index = c.enter_context(nc.sbuf_tensor(f"{tag}_index", [P, 2, K], I32))
        yg = c.enter_context(nc.sbuf_tensor(f"{tag}_yg", [P, 2, K, D], F32))
        index_ready, dve_chain = sem("index_ready"), sem("dve_chain")
        gathered = [sem(f"gathered{b}") for b in range(2)]
        added, x_out = sem("added"), sem("x_out")
        block = c.enter_context(nc.Block())
        PAIRS = NT // 2

        @block.gpsimd
        def _(pool):
            for k in range(K):
                pool.tensor_copy(index[:, 0, k:k + 1], r.slot[k][:, 0:1]).then_inc(index_ready, 1)
            with pool.Fori(0, PAIRS) as i:
                for b in range(2):
                    after = pool.snap(2 * i + b + 1)
                    pool.wait_ge(gathered[1 - b], 16 * K * (i + b))
                    pool.wait_ge(added, 2 * i)
                    pool.wait_ge(index_ready, K * (2 * i + b + 1))
                    for k in range(K):
                        pool.tensor_copy(index[:, 1 - b, k:k + 1], r.slot[k][:, bass.ds(after, 1)]).then_inc(index_ready, 1)
                    for k in range(K):
                        pool.indirect_dma_start(yg[:, b, k, :], None, y_dram,
                                                bass.IndirectOffsetOnAxis(ap=index[:, b, k:k + 1], axis=0)
                                                ).then_inc(gathered[b], 16)

        @block.vector
        def _(dve):
            chain = Chain(dve, dve_chain)
            with dve.Fori(0, PAIRS) as i:
                chain.enter(i, 2 * (K - 1))
                for b in range(2):
                    t = 2 * i + b
                    dve.wait_ge(gathered[b], 16 * K * (i + 1))
                    for k in range(K):
                        ins = dve.scalar_tensor_tensor(x_sb[:, t, :], yg[:, b, k, :], r.gates[k][:, bass.ds(t, 1)],
                                                       x_sb[:, t, :], ALU.mult, ALU.add)
                        if k + 1 < K:
                            chain.link(ins)
                        else:
                            ins.then_inc(added, 1)
                chain.leave(PAIRS)

        if out is not None:
            @block.sync
            def _(sp):
                NB, L, _ = out.shape
                for n in range(NB):
                    sp.wait_ge(added, (n + 1) * (NT // NB))
                    sp.dma_start(out[n].rearrange("(k p) d -> p k d", p=P),
                                 x_sb[:, n * (NT // NB):(n + 1) * (NT // NB), :]).then_inc(x_out, 16)
                sp.wait_ge(x_out, 16 * NB)


def attention_1(nc, Wq, Wk, Wv, Wo, bo, gq, betaq, gk, betak, x_sb, ident, ctxT,
                NB, L, D, S, NT, KC, HEADS, HD, INNER):
    PAIR = 2
    G = HEADS // PAIR
    GT = 4
    GROUPS = NT // GT
    PER_N = L // (GT * P)
    SCALE = float(HD) ** -0.5
    WC = PAIR * S
    BANKS = 3
    HB = HEADS // BANKS + 1
    VW = HD + 1
    IC = INNER // P
    split = [(0, 2 * HB), (2 * HB, HEADS)]
    with ExitStack() as c:
        def sb(name, shape, dt=F32):
            return c.enter_context(nc.sbuf_tensor("a1_" + name, shape, dt))

        def sem(name):
            return c.enter_context(nc.semaphore("a1_" + name))

        wq, wo = sb("wq", [P, KC, INNER]), sb("wo", [P, IC, D])
        bo_b = sb("bo_b", [P, D])
        k_pairs = sb("k_pairs", [P, NB, G, WC])
        c_b = sb("c_b", [P, NB, HEADS, S])
        v_sb = sb("v", [S, NB, HEADS, VW])
        halves = sb("halves", [P, PAIR])
        w_in, b_in, kv_in = sem("w_in"), sem("b_in"), sem("kv_in")
        dve_chain = sem("dve_chain")

        with ExitStack() as c2:
            def sb2(name, shape, dt=F32):
                return c2.enter_context(nc.sbuf_tensor("a1s_" + name, shape, dt))

            def sem2(name):
                return c2.enter_context(nc.semaphore("a1s_" + name))

            wk, wv = sb2("wk", [P, KC, INNER]), sb2("wv", [P, KC, INNER])
            gk_b, betak_b = sb2("gk_b", [S, HD]), sb2("betak_b", [S, HD])
            gq2, betaq2 = sb2("gq2", [P, 1]), sb2("betaq2", [P, 1])
            beta_cols = sb2("beta_cols", [P, P])
            k_sb, k_sq = sb2("k", [S, HEADS, HD]), sb2("k_sq", [S, HEADS, HD])
            mean = sb2("mean", [P, KC * HEADS])
            var, rstd, tmp = sb2("var", [S, HEADS]), sb2("rstd", [S, HEADS]), sb2("tmp", [S, HEADS])
            kn_ready, k_done, v_done, k_taken, v_taken = (sem2(s) for s in ("kn_ready", "k_done", "v_done", "k_taken", "v_taken"))
            k_turned, k_placed, c_done, c_taken, beta_ready, pads = (
                sem2(s) for s in ("k_turned", "k_placed", "c_done", "c_taken", "beta_ready", "pads"))
            k_ps = c2.enter_context(nc.psum_tensor("a1s_k_ps", [P, 2, 512], F32))
            v_ps = c2.enter_context(nc.psum_tensor("a1s_v_ps", [P, 2, 512], F32))
            kT_ps = c2.enter_context(nc.psum_tensor("a1s_kT_ps", [P, 2, 512], F32))
            c_ps = c2.enter_context(nc.psum_tensor("a1s_c_ps", [P, 2, 512], F32))
            block = c2.enter_context(nc.Block())
            kT4 = kT_ps[:, :, :].rearrange("p b (g s) -> p b g s", g=4)

            @block.sync
            def _(sp):
                sp.dma_start(wk[:], Wk.rearrange("(k p) n -> p k n", p=P)).then_inc(kv_in, 16)
                sp.dma_start(wv[:], Wv.rearrange("(k p) n -> p k n", p=P)).then_inc(kv_in, 16)
                sp.dma_start(wq[:], Wq.rearrange("(k p) n -> p k n", p=P)).then_inc(w_in, 16)
                sp.dma_start(wo[:], Wo.rearrange("(k p) n -> p k n", p=P)).then_inc(w_in, 16)
                for dst, src in ((gk_b, gk), (betak_b, betak)):
                    sp.dma_start(dst[:], src.rearrange("(a d) -> a d", a=1).to_broadcast([S, HD])).then_inc(b_in, 16)
                for dst, src in ((gq2, gq), (betaq2, betaq)):
                    for h in range(PAIR):
                        sp.dma_start(dst[h * HD:(h + 1) * HD, :], src.rearrange("(d a) -> d a", a=1), allow_slow_non_contiguous=True).then_inc(b_in, 16)
                sp.dma_start(bo_b[:], bo.rearrange("(a d) -> a d", a=1).to_broadcast([P, D])).then_inc(b_in, 16)

            @block.gpsimd
            def _(pool):
                pool.memset(k_pairs[:], 0.0).then_inc(pads, 1)
                pool.memset(v_sb[:, :, :, HD:VW], 1.0)

            @block.tensor
            def _(pe):
                pe.wait_ge(kv_in, 32)
                for n in range(NB):
                    for h in range(2):
                        if n:
                            pe.wait_ge(k_taken, 2 * n - 1 + h)
                        for k in range(KC):
                            last = pe.matmul(k_ps[0:S, h, :], ctxT[:, k, n * S:(n + 1) * S],
                                             wk[:, k, h * 512:(h + 1) * 512], start=(k == 0), stop=(k == KC - 1))
                        last.then_inc(k_done, 1)
                    for h in range(2):
                        if n:
                            pe.wait_ge(v_taken, 2 * n - 1 + h)
                        for k in range(KC):
                            last = pe.matmul(v_ps[0:S, h, :], ctxT[:, k, n * S:(n + 1) * S],
                                             wv[:, k, h * 512:(h + 1) * 512], start=(k == 0), stop=(k == KC - 1))
                        last.then_inc(v_done, 1)
                    pe.wait_ge(kn_ready, n + 1)
                    if n:
                        pe.wait_ge(k_placed, 4 * n)
                    kf = k_sb[:, :, :].rearrange("s h d -> s (h d)")
                    for g in range(G):
                        last = pe.transpose(kT4[:, g // 4, g % 4, 0:S], kf[:, g * P:(g + 1) * P], ident[0:S, 0:S])
                    last.then_inc(k_turned, 1)
                    pe.wait_ge(k_placed, 4 * n + 4)
                    pe.wait_ge(beta_ready, 1)
                    for g in range(G):
                        b = g // 3
                        if n or b >= 2:
                            pe.wait_ge(c_taken, 3 * n + b - 1)
                        last = pe.matmul(c_ps[:, b % 2, (g % 3) * WC:(g % 3 + 1) * WC], beta_cols[:], k_pairs[:, n, g, :],
                                         start=True, stop=True)
                        if g % 3 == 2 or g == G - 1:
                            last.then_inc(c_done, 1)
                    if n + 1 < NB:
                        pe.wait_ge(c_taken, 3 * n + 3)

            @block.scalar
            def _(act):
                for n in range(NB):
                    for h in range(2):
                        act.wait_ge(v_done, 2 * n + h + 1)
                        act.copy(v_sb[:, n, 8 * h:8 * h + 8, 0:HD],
                                 v_ps[0:S, h, :].rearrange("s (h d) -> s h d", d=HD)).then_inc(v_taken, 1)
                    for b in range(3):
                        g0, g1 = 3 * b, min(3 * b + 3, G)
                        act.wait_ge(c_done, 3 * n + b + 1)
                        act.copy(c_b[:, n, PAIR * g0:PAIR * g1, :].rearrange("p h s -> p (h s)"),
                                 c_ps[:, b % 2, 0:(g1 - g0) * WC]).then_inc(c_taken, 1)

            @block.vector
            def _(dve):
                chain = Chain(dve, dve_chain)
                link = chain.link
                for h in range(PAIR):
                    for q in range(PAIR):
                        dve.memset(halves[q * HD:(q + 1) * HD, h:h + 1], float(h == q))
                dve.wait_ge(b_in, 16 * 7)
                dve.tensor_copy(beta_cols[:], betaq2[:, 0:1].to_broadcast([P, P])).then_inc(beta_ready, 1)
                dve.wait_ge(w_in, 32)
                wq_h = wq[:, :, :].rearrange("p k (h d) -> p (k h) d", d=HD)
                link(dve.tensor_reduce(mean[:], wq_h, AX.X, ALU.add))
                link(dve.tensor_scalar(mean[:], mean[:], 1.0 / HD, None, ALU.mult))
                link(dve.tensor_tensor(wq_h, wq_h, mean[:, :].rearrange("p (h a) -> p h a", a=1)
                                       .to_broadcast([P, KC * HEADS, HD]), ALU.subtract))

                def per_head(a):
                    return a.rearrange("s (h a) -> s h a", a=1).to_broadcast([S, HEADS, HD])

                def per_column(a):
                    return a.rearrange("s (a d) -> s a d", a=1).to_broadcast([S, HEADS, HD])

                for n in range(NB):
                    for h in range(2):
                        dve.wait_ge(k_done, 2 * n + h + 1)
                        if n:
                            dve.wait_ge(k_turned, n)
                        chain.step(dve.tensor_copy(k_sb[:, 8 * h:8 * h + 8, :],
                                                   k_ps[0:S, h, :].rearrange("s (h d) -> s h d", d=HD)))
                    dve.wait_ge(dve_chain, chain.base + chain.n)
                    chain.link(dve.tensor_reduce(mean[0:S, 0:HEADS], k_sb[:], AX.X, ALU.add))
                    dve.tensor_scalar(mean[0:S, 0:HEADS], mean[0:S, 0:HEADS], 1.0 / HD, None, ALU.mult).then_inc(k_taken, 2)
                    dve.wait_ge(k_taken, 2 * n + 2)
                    link(dve.tensor_tensor(k_sb[:], k_sb[:], per_head(mean[0:S, 0:HEADS]), ALU.subtract))
                    link(dve.tensor_tensor(k_sq[:], k_sb[:], k_sb[:], ALU.mult))
                    link(dve.tensor_reduce(var[:], k_sq[:], AX.X, ALU.add))
                    link(dve.tensor_scalar(var[:], var[:], 1.0 / HD, EPS, ALU.mult, ALU.add))
                    rsqrt(dve, chain, rstd[:], var[:], tmp[:])
                    link(dve.tensor_tensor(k_sb[:], k_sb[:], per_head(rstd[:]), ALU.mult))
                    link(dve.tensor_tensor(k_sb[:], k_sb[:], per_column(gk_b[:]), ALU.mult))
                    dve.tensor_tensor(k_sb[:], k_sb[:], per_column(betak_b[:]), ALU.add).then_inc(kn_ready, 1)
                    dve.wait_ge(k_turned, n + 1)
                    dve.wait_ge(pads, 1)
                    for h in range(PAIR):
                        for b in range(2):
                            dve.tensor_copy(k_pairs[h * HD:(h + 1) * HD, n, 4 * b:4 * b + 4, h * S:(h + 1) * S],
                                            kT4[h * HD:(h + 1) * HD, b, :, 0:S]).then_inc(k_placed, 1)
                    dve.wait_ge(c_done, 3 * n + 3)
                    dve.wait_ge(k_placed, 4 * n + 4)
                    link(dve.tensor_scalar(k_pairs[:, n, :, :], k_pairs[:, n, :, :], gq2[:, 0:1], None, ALU.mult))

        with ExitStack() as c2:
            def sb3(name, shape, dt=F32):
                return c2.enter_context(nc.sbuf_tensor("a1m_" + name, shape, dt))

            def sem3(name):
                return c2.enter_context(nc.semaphore("a1m_" + name))

            xn = sb3("xn", [P, GT, D])
            xT = sb3("xT", [P, KC, GT * P])
            qT = sb3("qT", [P, G, GT * P])
            q_sq = sb3("q_sq", [P, 2, GT * P])
            stats, mv = sb3("stats", [P, GT, 6]), sb3("mv", [P, GT, 2])
            var, rstd, tmp = sb3("var", [P, GT]), sb3("rstd", [P, GT]), sb3("tmp", [P, GT])
            q_var, q_rstd, q_tmp = (sb3(s, [P, GT * HEADS]) for s in ("q_var", "q_rstd", "q_tmp"))
            s_sb = sb3("s", [P, 2, HEADS, S])
            e_sb = sb3("e", [P, 2, HEADS, S])
            mx = sb3("mx", [P, 2, HEADS])
            eT = sb3("eT", [S, HEADS, P])
            rsum = sb3("rsum", [P, HEADS])
            o_sb = sb3("o", [P, INNER])
            oT = sb3("oT", [P, IC, P])
            y_sb = sb3("y", [P, 2, D])
            work = c2.enter_context(nc.psum_tensor("a1_work", [P, 2, 512], F32))
            s_ps = c2.enter_context(nc.psum_tensor("a1_s_ps", [P, BANKS, 512], F32))
            o_ps = c2.enter_context(nc.psum_tensor("a1_o_ps", [P, BANKS, 512], F32))
            xn_ready, work_full, work_freed, sq_ready, rstd_ready = (
                sem3(s) for s in ("xn_ready", "work_full", "work_freed", "sq_ready", "rstd_ready"))
            s_done, s_taken, c_added, m_ready, m_taken, e_ready = (
                sem3(s) for s in ("s_done", "s_taken", "c_added", "m_ready", "m_taken", "e_ready"))
            o_done, o_taken, x_added, bo_added, var_ready, sums_read = (
                sem3(s) for s in ("o_done", "o_taken", "x_added", "bo_added", "var_ready", "sums_read"))
            var_taken, pool_passed = sem3("var_taken"), sem3("pool_passed")
            var_ps = o_ps[:, BANKS - 1, 512 - GT * HEADS:512]
            block = c2.enter_context(nc.Block())
            ET = HEADS // 4
            OT = IC // 4
            TILE_USES = ET + OT + 1
            Q0 = KC
            T0 = KC + G
            USES = T0 + GT * TILE_USES

            @block.tensor
            def _(pe):
                with pe.Fori(0, NB) as n, pe.Fori(0, PER_N) as part:
                    g = n * PER_N + part
                    state = {"use": 0, "last": [0, 0], "seen": [False, False]}

                    def take():
                        use = state["use"]
                        b = use % 2
                        if state["seen"][b]:
                            pe.wait_ge(work_freed, USES * g + state["last"][b] + 1)
                        else:
                            pe.wait_ge(work_freed, USES * g)
                        state["last"][b], state["seen"][b] = use, True
                        state["use"] += 1
                        return work[:, b, :]

                    def sum_squares(q):
                        if q == 0:
                            pe.wait_ge(var_taken, g)
                        pe.wait_ge(sq_ready, G * g + q + 1)
                        for t in range(GT):
                            last = pe.matmul(var_ps[:, (t * G + q) * PAIR:(t * G + q + 1) * PAIR],
                                             q_sq[:, q % 2, t * P:(t + 1) * P], halves[:], start=True, stop=True)
                        last.then_inc(var_ready, 1)

                    pe.wait_ge(xn_ready, GT * g + GT)
                    for k in range(KC):
                        bank = take()
                        for t in range(GT):
                            last = pe.transpose(bank[:, t * P:(t + 1) * P], xn[:, t, k * P:(k + 1) * P], ident[:])
                        last.then_inc(work_full, 1)
                    pe.wait_ge(work_freed, USES * g + Q0)
                    for q in range(G):
                        bank = take()
                        for k in range(KC):
                            last = pe.matmul(bank, wq[:, k, q * P:(q + 1) * P], xT[:, k, :], start=(k == 0), stop=(k == KC - 1))
                        last.then_inc(work_full, 1)
                        if q:
                            sum_squares(q - 1)
                    sum_squares(G - 1)

                    def tile_scores(t):
                        pe.wait_ge(s_taken, GT * g + t)
                        for q in range(G):
                            last = pe.matmul(s_ps[:, q // 3, (q % 3) * WC:(q % 3 + 1) * WC], qT[:, q, t * P:(t + 1) * P],
                                             k_pairs[:, n, q, :], start=True, stop=True)
                        last.then_inc(s_done, 1)

                    def tile_rest(t):
                        pe.wait_ge(e_ready, GT * g + t + 1)
                        first = T0 + t * TILE_USES
                        for b in range(ET):
                            bank = take()
                            for h in range(4):
                                last = pe.transpose(bank[0:S, h * P:(h + 1) * P], e_sb[:, t % 2, 4 * b + h, :], ident[:])
                            last.then_inc(work_full, 1)
                        pe.wait_ge(o_taken, GT * g + t)
                        for h in range(HEADS):
                            if h % 4 == 0:
                                pe.wait_ge(work_freed, USES * g + first + h // 4 + 1)
                            last = pe.matmul(o_ps[:, h // HB, (h % HB) * VW:(h % HB + 1) * VW], eT[:, h, :],
                                             v_sb[:, n, h, :], start=True, stop=True)
                        last.then_inc(o_done, 1)
                        pe.wait_ge(o_taken, GT * g + t + 1)
                        for b in range(OT):
                            bank = take()
                            for j in range(4):
                                last = pe.transpose(bank[:, j * P:(j + 1) * P], o_sb[:, (4 * b + j) * P:(4 * b + j + 1) * P], ident[:])
                            last.then_inc(work_full, 1)
                        bank = take()
                        for j in range(IC):
                            if j % 4 == 0:
                                pe.wait_ge(work_freed, USES * g + first + ET + j // 4 + 1)
                            last = pe.matmul(bank[:, 0:D], oT[:, j, :], wo[:, j, :], start=(j == 0), stop=(j == IC - 1))
                        last.then_inc(work_full, 1)

                    pe.wait_ge(work_freed, USES * g + T0)
                    tile_scores(0)
                    for t in range(GT):
                        if t + 1 < GT:
                            tile_scores(t + 1)
                        tile_rest(t)
                    assert state["use"] == USES

            @block.scalar
            def _(act):
                with act.Fori(0, NB) as n, act.Fori(0, PER_N) as part:
                    g = n * PER_N + part
                    state = {"use": 0}

                    def full():
                        act.wait_ge(work_full, USES * g + state["use"] + 1)
                        bank = work[:, state["use"] % 2, :]
                        state["use"] += 1
                        return bank

                    for k in range(KC):
                        act.copy(xT[:, k, :], full()).then_inc(work_freed, 1)
                    for q in range(G):
                        bank = full()
                        if q >= 2:
                            act.wait_ge(var_ready, G * g + q - 1)
                        act.activation(q_sq[:, q % 2, :], bank, ACT.Square).then_inc(sq_ready, 1)
                        act.copy(qT[:, q, :], bank).then_inc(work_freed, 1)

                    def tile_exp(t):
                        act.wait_ge(m_taken, GT * g + t + 1)
                        act.activation(e_sb[:, t % 2, :, :], s_sb[:, t % 2, :, :], ACT.Exp, scale=SCALE).then_inc(e_ready, 1)

                    for t in range(GT):
                        tile_exp(t)
                        for b in range(ET):
                            act.copy(eT[:, 4 * b:4 * b + 4, :].rearrange("s h p -> s (h p)"), full()[0:S, :]).then_inc(work_freed, 1)
                        for b in range(OT):
                            act.copy(oT[:, 4 * b:4 * b + 4, :].rearrange("s h p -> s (h p)"), full()).then_inc(work_freed, 1)
                        bank = full()
                        if t >= 2:
                            act.wait_ge(x_added, GT * g + t - 1)
                        else:
                            act.wait_ge(x_added, GT * g)
                        act.copy(y_sb[:, t % 2, :], bank[:, 0:D]).then_inc(work_freed, 1)

            @block.gpsimd
            def _(pool):
                with pool.Fori(0, NB) as n, pool.Fori(0, PER_N) as part:
                    g = n * PER_N + part
                    gg = pool.snap(g)
                    batch = pool.snap(n)
                    xg = x_sb[:, :, :].rearrange("p (g t) d -> p g t d", t=GT)

                    def tile_add(t):
                        pool.wait_ge(work_freed, USES * g + T0 + (t + 1) * TILE_USES)
                        alone(pool, pool_passed)
                        pool.tensor_tensor(xg[:, gg, t, :], xg[:, gg, t, :], y_sb[:, t % 2, :], ALU.add).then_inc(x_added, 1)

                    for t in range(GT):
                        if t == 0:
                            pool.wait_ge(xn_ready, GT * g + GT)
                            alone(pool, pool_passed)
                        pool.tensor_tensor(xg[:, gg, t, :], xg[:, gg, t, :], bo_b[:], ALU.add).then_inc(bo_added, 1)
                    pool.wait_ge(bo_added, GT * g + GT)
                    for t in range(GT):
                        pool.wait_ge(s_taken, GT * g + t + 1)
                        alone(pool, pool_passed)
                        pool.tensor_tensor(s_sb[:, t % 2, :, :], s_sb[:, t % 2, :, :], c_b[:, batch, :, :], ALU.add).then_inc(c_added, 1)
                        pool.wait_ge(m_ready, GT * g + t + 1)
                        pool.tensor_tensor(s_sb[:, t % 2, :, :], s_sb[:, t % 2, :, :],
                                           mx[:, t % 2, :].rearrange("p (h a) -> p h a", a=1).to_broadcast([P, HEADS, S]),
                                           ALU.subtract).then_inc(m_taken, 1)
                        if t:
                            tile_add(t - 1)
                    tile_add(GT - 1)

            @block.vector
            def _(dve):
                chain = Chain(dve, dve_chain)
                chain.n = SETUP_STEPS(NB)
                xg = x_sb[:, :, :].rearrange("p (g t) d -> p g t d", t=GT)
                with dve.Fori(0, NB) as n, dve.Fori(0, PER_N) as part:
                    g = n * PER_N + part
                    chain.enter(g, layernorm_steps(GT) + RSQRT_STEPS + GT * 3)
                    layernorm(dve, chain, [xg[:, g, t, :] for t in range(GT)], [xn[:, t, :] for t in range(GT)],
                              stats, mv, var[:], rstd[:], tmp[:], xn_ready)
                    dve.wait_ge(var_ready, G * g + G)
                    dve.tensor_scalar(q_var[:], var_ps, 1.0 / HD, EPS, ALU.mult, ALU.add).then_inc(var_taken, 1)
                    dve.wait_ge(var_taken, g + 1)
                    rsqrt(dve, chain, q_rstd[:], q_var[:], q_tmp[:])

                    def tile_scale(t):
                        dve.wait_ge(s_done, GT * g + t + 1)
                        if t >= 2:
                            dve.wait_ge(e_ready, GT * g + t - 1)
                        for i, (h0, h1) in enumerate(split):
                            b0, b1 = h0 // HB, -(-h1 // HB)
                            nh = min(HB, h1 - h0)
                            r4 = q_rstd[:, t * HEADS + h0:t * HEADS + h1].rearrange("p (b h a) -> p b h a", h=nh, a=1)
                            ins = dve.tensor_tensor(
                                s_sb[:, t % 2, h0:h1, :].rearrange("p (b h) s -> p b h s", h=nh),
                                s_ps[:, b0:b1, 0:nh * S].rearrange("p b (h s) -> p b h s", s=S),
                                r4.to_broadcast([P, b1 - b0, nh, S]), ALU.mult)
                            if i == 0:
                                chain.step(ins)
                            else:
                                ins.then_inc(s_taken, 1)

                    def tile_max(t):
                        dve.wait_ge(c_added, GT * g + t + 1)
                        dve.tensor_reduce(mx[:, t % 2, :], s_sb[:, t % 2, :, :], AX.X, ALU.max).then_inc(m_ready, 1)

                    def tile_out(t):
                        dve.wait_ge(o_done, GT * g + t + 1)
                        o5 = [o_ps[:, h0 // HB:-(-h1 // HB), 0:min(HB, h1 - h0) * VW].rearrange("p b (h v) -> p b h v", v=VW)
                              for h0, h1 in split]
                        for i, (h0, h1) in enumerate(split):
                            nh = min(HB, h1 - h0)
                            last = dve.reciprocal(rsum[:, h0:h1].rearrange("p (b h) -> p b h", h=nh), o5[i][:, :, :, HD])
                            if i == 0:
                                chain.step(last)
                        last.then_inc(sums_read, 1)
                        dve.wait_ge(sums_read, GT * g + t + 1)
                        for i, (h0, h1) in enumerate(split):
                            nh = min(HB, h1 - h0)
                            r4 = rsum[:, h0:h1].rearrange("p (b h a) -> p b h a", h=nh, a=1)
                            last = dve.tensor_tensor(
                                o_sb[:, h0 * HD:h1 * HD].rearrange("p (b h d) -> p b h d", h=nh, d=HD),
                                o5[i][:, :, :, 0:HD], r4.to_broadcast([P, (h1 - h0) // nh, nh, HD]), ALU.mult)
                            if i == 0:
                                chain.step(last)
                            else:
                                last.then_inc(o_taken, 1)

                    tile_scale(0)
                    for t in range(GT):
                        tile_max(t)
                        if t + 1 < GT:
                            tile_scale(t + 1)
                        tile_out(t)
                    chain.leave(GROUPS)
                    dve.wait_ge(e_ready, GT * g + GT)


def SETUP_STEPS(NB):
    return 3 + NB * (2 + 1 + 4 + RSQRT_STEPS + 2 + 1)


def experts_1(nc, xn_dram, y_dram, ident, r, W1, b1, W2, b2, E, D, H, KC, CT, TILES):
    HC = H // P
    CAP = CT * P
    HALVES = [(0, CAP // 2), (CAP // 2, CAP)]
    with ExitStack() as c:
        def sb(name, shape, dt=F32):
            return c.enter_context(nc.sbuf_tensor("e1_" + name, shape, dt))

        def sem(name):
            return c.enter_context(nc.semaphore("e1_" + name))

        w1, w2 = sb("w1", [P, 2, KC, H]), sb("w2", [P, 2, HC, D])
        b1T, b1_now = sb("b1T", [P, E, HC]), sb("b1_now", [P, 2, HC])
        b1_rows = sb("b1_rows", [E * HC, P])
        b2_b = sb("b2_b", [P, E, D])
        index = sb("index", [P, 2], I32)
        xg = sb("xg", [P, 2, CT, D])
        xT = sb("xT", [P, KC, CAP])
        hT = sb("hT", [P, HC, CAP])
        y_sb = sb("y", [P, 2, CT, D])
        b_in, b1_turned, b1_ready, index_ready = sem("b_in"), sem("b1_turned"), sem("b1_ready"), sem("index_ready")
        b1_copied = sem("b1_copied")
        w_in = [sem(f"w_in{b}") for b in range(2)]
        gathered = [sem(f"gathered{b}") for b in range(2)]
        stored = [sem(f"stored{b}") for b in range(2)]
        x_turned, xT_ready, h_done, h_ready, y_done, y_ready = (
            sem(s) for s in ("x_turned", "xT_ready", "h_done", "h_ready", "y_done", "y_ready"))
        x_ps = c.enter_context(nc.psum_tensor("e1_x_ps", [P, 2, 512], F32))
        h_ps = c.enter_context(nc.psum_tensor("e1_h_ps", [P, 4, 512], F32))
        y_ps = c.enter_context(nc.psum_tensor("e1_y_ps", [P, 2, 512], F32))
        block = c.enter_context(nc.Block())
        PASSES = E // 2
        HU = 2 * HC

        @block.sync
        def _(sp):
            sp.dma_start(b1_rows[:], b1.rearrange("e (j p) -> (e j) p", p=P)).then_inc(b_in, 16)
            sp.dma_start(b2_b[:, :, :].rearrange("p e h -> p (e h)"),
                         b2.rearrange("(a e) h -> a (e h)", a=1).to_broadcast([P, E * D])).then_inc(b_in, 16)
            with sp.Fori(0, PASSES) as i:
                for b in range(2):
                    e = sp.snap(2 * i + b)
                    sp.wait_ge(y_done, CT * 2 * i)
                    sp.dma_start(w1[:, b, :, :], W1.rearrange("e (k p) h -> e p k h", p=P)[e]).then_inc(w_in[b], 16)
                    sp.dma_start(w2[:, b, :, :], W2.rearrange("e (j p) d -> e p j d", p=P)[e]).then_inc(w_in[b], 16)

        @block.gpsimd
        def _(pool):
            pool.tensor_copy(index[:, 0:1], r.token[:, 0:1]).then_inc(index_ready, 1)
            pool.wait_ge(index_ready, 1)
            with pool.Fori(0, PASSES) as i:
                for b in range(2):
                    for t in range(CT):
                        u = CT * b + t
                        after = pool.snap(2 * CT * i + u + 1)
                        if u:
                            pb, pt = divmod(u - 1, CT)
                            pool.wait_ge(gathered[pb], 16 * (CT * i + pt + 1))
                        else:
                            pool.wait_ge(gathered[1], 16 * CT * i)
                        pool.wait_ge(index_ready, 2 * CT * i + u + 1)
                        if t == 0:
                            pool.wait_ge(x_turned, 2 * CT * i)
                        pool.tensor_copy(index[:, (u + 1) % 2:(u + 1) % 2 + 1], r.token[:, bass.ds(after, 1)]
                                         ).then_inc(index_ready, 1)
                        pool.indirect_dma_start(xg[:, b, t, :], None, xn_dram,
                                                bass.IndirectOffsetOnAxis(ap=index[:, u % 2:u % 2 + 1], axis=0)
                                                ).then_inc(gathered[b], 16)

        @block.tensor
        def _(pe):
            pe.wait_ge(b_in, 32)
            pe.transpose(x_ps[:, 0, 0:E * HC], b1_rows[:], ident[0:E * HC, 0:E * HC]).then_inc(b1_turned, 1)
            pe.wait_ge(b1_ready, 1)
            with pe.Fori(0, PASSES) as i:
                for b in range(2):
                    e = 2 * i + b
                    for t in range(CT):
                        if t >= 2:
                            pe.wait_ge(xT_ready, CT * e + t - 1)
                        else:
                            pe.wait_ge(xT_ready, CT * e)
                        pe.wait_ge(gathered[b], 16 * (CT * i + CT))
                        for k in range(KC):
                            last = pe.transpose(x_ps[:, t % 2, k * P:(k + 1) * P], xg[:, b, t, k * P:(k + 1) * P], ident[:])
                        last.then_inc(x_turned, 1)
                    pe.wait_ge(xT_ready, CT * e + CT)
                    pe.wait_ge(w_in[b], 32 * i + 32)
                    for u in range(HU):
                        j, s = divmod(u, 2)
                        if u >= 4:
                            pe.wait_ge(h_ready, HU * e + u - 3)
                        c0, c1 = HALVES[s]
                        for k in range(KC):
                            last = pe.matmul(h_ps[:, u % 4, 0:c1 - c0], w1[:, b, k, j * P:(j + 1) * P], xT[:, k, c0:c1],
                                             start=(k == 0), stop=(k == KC - 1))
                        last.then_inc(h_done, 1)
                    pe.wait_ge(h_ready, HU * e + HU)
                    for t in range(CT):
                        if t >= 2:
                            pe.wait_ge(y_ready, CT * e + t - 1)
                        else:
                            pe.wait_ge(y_ready, CT * e)
                        for j in range(HC):
                            last = pe.matmul(y_ps[:, t % 2, 0:D], hT[:, j, t * P:(t + 1) * P], w2[:, b, j, :],
                                             start=(j == 0), stop=(j == HC - 1))
                        last.then_inc(y_done, 1)

        @block.scalar
        def _(act):
            act.wait_ge(b1_turned, 1)
            act.copy(b1T[:, :, :].rearrange("p e j -> p (e j)"), x_ps[:, 0, 0:E * HC]).then_inc(b1_ready, 1)
            act.wait_ge(b1_ready, 1)
            with act.Fori(0, PASSES) as i:
                for b in range(2):
                    e = 2 * i + b
                    act.copy(b1_now[:, b, :], b1T[:, e, :]).then_inc(b1_copied, 1)
                    for t in range(CT):
                        act.wait_ge(x_turned, CT * e + t + 1)
                        act.copy(xT[:, :, t * P:(t + 1) * P],
                                 x_ps[:, t % 2, 0:KC * P].rearrange("p (k q) -> p k q", k=KC)).then_inc(xT_ready, 1)
                    act.wait_ge(b1_copied, e + 1)
                    for u in range(HU):
                        j, s = divmod(u, 2)
                        c0, c1 = HALVES[s]
                        act.wait_ge(h_done, HU * e + u + 1)
                        act.activation(hT[:, j, c0:c1], h_ps[:, u % 4, 0:c1 - c0], ACT.Relu,
                                       bias=b1_now[:, b, j:j + 1]).then_inc(h_ready, 1)
                    ee = act.snap(e)
                    act.wait_ge(y_ready, CT * e + CT)
                    act.dma_start(y_dram.rearrange("(e t p) d -> e p t d", p=P, t=CT)[ee], y_sb[:, b, :, :]
                                  ).then_inc(stored[b], 16)
            for b in range(2):
                act.wait_ge(stored[b], 16 * PASSES)

        @block.vector
        def _(dve):
            with dve.Fori(0, PASSES) as i:
                for b in range(2):
                    e = 2 * i + b
                    for t in range(CT):
                        dve.wait_ge(y_done, CT * e + t + 1)
                        if t == 0:
                            dve.wait_ge(stored[b], 16 * i)
                        dve.tensor_tensor(y_sb[:, b, t, :], y_ps[:, t % 2, 0:D], b2_b[:, e, :], ALU.add).then_inc(y_ready, 1)


_INS = ['x', 'ctx_1024', 'L0_xattn_Wq', 'L0_xattn_bq', 'L0_xattn_Wk', 'L0_xattn_bk', 'L0_xattn_Wv', 'L0_xattn_bv',
        'L0_xattn_Wo', 'L0_xattn_bo', 'L0_ffn_gate', 'L0_ffn_W1', 'L0_ffn_b1', 'L0_ffn_W2', 'L0_ffn_b2',
        'L1_xattn_Wq', 'L1_xattn_Wk', 'L1_xattn_Wv', 'L1_xattn_Wo', 'L1_xattn_bo', 'L1_xattn_q_gamma',
        'L1_xattn_q_beta', 'L1_xattn_k_gamma', 'L1_xattn_k_beta', 'L1_ffn_gate_w', 'L1_ffn_w1', 'L1_ffn_b1',
        'L1_ffn_w2', 'L1_ffn_b2']
_OUTS = [((4, 1024, 256), 'float32')]


def kernel(**inputs):
    import numpy as _np
    import concourse.bacc as _bacc
    from concourse import mybir as _mybir
    from concourse.bass_utils import run_bass_kernel_spmd as _run

    nc = _bacc.Bacc("TRN2", target_bir_lowering=False, num_devices=1)
    arrays, args = {}, []
    for name in _INS:
        a = _np.ascontiguousarray(inputs[name])
        arrays[f"in_{name}_dram"] = a
        args.append(nc.dram_tensor(f"in_{name}_dram", a.shape, _mybir.dt.from_np(a.dtype), kind="ExternalInput").ap())
    for i, (shape, dtype) in enumerate(_OUTS):
        dt = _mybir.dt.from_np(_np.dtype(dtype))
        args.append(nc.dram_tensor(f"out_{i}_dram", shape, dt, kind="ExternalOutput").ap())
    build_layers(nc, *args)
    r = _run(nc, [arrays], core_ids=[0])
    got = tuple(r.results[0][f"out_{i}_dram"] for i in range(len(_OUTS)))
    return got[0]
```

```python
from contextlib import ExitStack

import concourse.bass as bass
from concourse import mybir

F32 = mybir.dt.float32
BF16 = mybir.dt.bfloat16
I32 = mybir.dt.int32
ALU = mybir.AluOpType
ACT = mybir.ActivationFunctionType
AX = mybir.AxisListType

P = 128
EPS = 1e-5
RSQRT_SEED = 0x5F3759DF
FAR = 8192.0


class Chain:

    def __init__(self, eng, sem):
        self.eng, self.sem, self.base, self.n = eng, sem, 0, 0

    def step(self, ins):
        ins.then_inc(self.sem, 1)
        self.n += 1

    def link(self, ins):
        self.step(ins)
        self.eng.wait_ge(self.sem, self.base + self.n)

    def enter(self, i, per_pass):
        self.before, self.per = self.base + self.n, per_pass
        self.base, self.n = self.before + i * per_pass, 0

    def leave(self, passes):
        assert self.n == self.per, (self.n, self.per)
        self.base, self.n = self.before + passes * self.per, 0


def rsqrt(dve, chain, out, v, tmp):
    chain.link(dve.tensor_scalar(tmp.bitcast(I32), v.bitcast(I32), 1, None, ALU.logical_shift_right))
    chain.link(dve.tensor_scalar(out.bitcast(I32), tmp.bitcast(I32), -1.0, float(RSQRT_SEED), ALU.mult, ALU.add))
    for _ in range(3):
        chain.link(dve.tensor_tensor(tmp, out, out, ALU.mult))
        chain.link(dve.scalar_tensor_tensor(tmp, tmp, -0.5, v, ALU.mult, ALU.mult))
        chain.link(dve.scalar_tensor_tensor(out, tmp, 1.5, out, ALU.add, ALU.mult))


RSQRT_STEPS = 11


def moments(dve, chain, stats, mv, var, rstd, tmp, count):
    m0, q0, m1, q1 = (stats[:, :, c] for c in (1, 2, 4, 5))
    chain.step(dve.tensor_tensor(mv[:, :, 0], m0, m1, ALU.add))
    chain.step(dve.tensor_tensor(mv[:, :, 1], q0, q1, ALU.add))
    chain.link(dve.tensor_tensor(tmp, m0, m1, ALU.subtract))
    chain.step(dve.tensor_tensor(var, tmp, tmp, ALU.mult))
    chain.step(dve.tensor_scalar(mv[:, :, 0], mv[:, :, 0], 0.5, None, ALU.mult))
    chain.link(dve.tensor_scalar(mv[:, :, 1], mv[:, :, 1], 1.0 / count, EPS, ALU.mult, ALU.add))
    chain.link(dve.scalar_tensor_tensor(var, var, 0.25, mv[:, :, 1], ALU.mult, ALU.add))
    rsqrt(dve, chain, rstd, var, tmp)


MOMENTS_STEPS = 7 + RSQRT_STEPS


def build_layers(nc, x, ctx, Wq0, bq0, Wk0, bk0, Wv0, bv0, Wo0, bo0, gate0, W10, b10, W20, b20,
                 Wq1, Wk1, Wv1, Wo1, bo1, gq1, betaq1, gk1, betak1, gate1, W11, b11, W21, b21, out):
    NB, L, D = x.shape
    S = ctx.shape[1]
    T = NB * L
    NT = T // P
    TB = L // P
    KC = D // P
    E, _, H0 = W10.shape
    H1 = W11.shape[2]
    HEADS = 16
    HD0 = D // HEADS
    INNER = Wq1.shape[1]
    HD1 = INNER // HEADS
    TILES0 = 2 * T // P + E
    CAP = -(-5 * T // (4 * E))
    CT = CAP // P
    TILES1 = E * CT
    assert CAP % P == 0

    xn_dram = nc.dram_tensor("xn_scratch", (T, D), F32, kind="Internal").ap()
    y0_dram = nc.dram_tensor("y0_scratch", (TILES0 * P, D), F32, kind="Internal").ap()
    xm_dram = nc.dram_tensor("xm_scratch", (T, 2 * D), F32, kind="Internal").ap()

    top = ExitStack()
    with top:
        x_sb = top.enter_context(nc.sbuf_tensor("x_sb", [P, NT, D], F32))
        ident = top.enter_context(nc.sbuf_tensor("ident", [P, P], F32))
        ctxT = top.enter_context(nc.sbuf_tensor("ctxT", [P, KC, NB * S], F32))
        z_all = top.enter_context(nc.sbuf_tensor("z_all", [P, NT, E], F32))
        x4 = x_sb[:, :, :].rearrange("p (n k) d -> p n k d", k=TB)

        attention_0(nc, x, ctx, Wq0, bq0, Wk0, bk0, Wv0, bv0, Wo0, bo0, gate0, x_sb, x4, ident, ctxT,
                    xn_dram, z_all, NB, L, D, S, TB, KC, HEADS, HD0, E)
        with ExitStack() as routes:
            a1 = attention_1_weights(nc, routes, D, KC, INNER)
            r0 = routes_of(nc, "r0", routes, 2, TILES0, None, NT)
            with ExitStack() as expert_weights:
                w0 = experts_0_weights(nc, expert_weights, E, D, H0, KC)
                route(nc, "r0", r0, z_all, 2, E, TILES0, None, NT,
                      lambda sp: load_experts_0(sp, w0, W10, b10, W20, b20, E, D, H0, KC))
                experts_0(nc, xn_dram, y0_dram, ident, r0, w0, E, D, H0, KC, TILES0, a1, Wq1, Wk1, Wv1, Wo1, HD1)
            attention_1(nc, a1, bo1, gq1, betaq1, gk1, betak1, gate1, x_sb, ident, ctxT, y0_dram,
                        r0, z_all, xm_dram, out, NB, L, D, S, NT, KC, HEADS, HD1, INNER, E)
        with ExitStack() as routes:
            r1 = routes_of(nc, "r1", routes, 1, TILES1, CAP, NT)
            w1 = experts_1_weights(nc, routes, E, D, H1, KC)
            route(nc, "r1", r1, z_all, 1, E, TILES1, CAP, NT,
                  lambda sp: load_experts_1(sp, w1, W11, b11, W21, b21, E, D, H1, KC))
            experts_1(nc, xm_dram, out, ident, r1, w1, W11, W21, E, D, H1, KC, CT)


def attention_0(nc, x, ctx, Wq, bq, Wk, bk, Wv, bv, Wo, bo, gate, x_sb, x4, ident, ctxT,
                xn_dram, z_all, NB, L, D, S, TB, KC, HEADS, HD, E):
    HM = P // HD
    JT = -(-HM * S // P)
    PADDED = JT * P
    U = KC * JT
    SCALE = float(HD) ** -0.5
    with ExitStack() as c:
        def sb(name, shape, dt=F32):
            return c.enter_context(nc.sbuf_tensor("a0_" + name, shape, dt))

        def sem(name):
            return c.enter_context(nc.semaphore("a0_" + name))

        wq, wk, wv, wo = (sb(n, [P, KC, D]) for n in ("wq", "wk", "wv", "wo"))
        bqT, bkT = sb("bqT", [P, KC]), sb("bkT", [P, KC])
        bv_b, bo_b = sb("bv_b", [P, D]), sb("bo_b", [P, D])
        ctx_sb = sb("ctx", [S, NB, D])
        kT = sb("kT", [P, KC, NB, S])
        v_sb = sb("v", [S, NB, D])
        head_mask = sb("head_mask", [P, HM])
        v_blocks = sb("v_blocks", [P, NB, KC, JT, P])
        k_blocks = sb("k_blocks", [P, KC, PADDED])

        x_in, ctx_in, w_in, b_in, v_moved = (sem(n) for n in ("x_in", "ctx_in", "w_in", "b_in", "v_moved"))
        ident_ready, mask_ready, pads_ready = sem("ident_ready"), sem("mask_ready"), sem("pads_ready")
        pool_chain = sem("pool_chain")
        ctxT_done, ctxT_ready = sem("ctxT_done"), sem("ctxT_ready")
        kv_done, k_ready, v_ready = sem("kv_done"), sem("k_ready"), sem("v_ready")

        pieces = []
        for h in range(HM):
            r, end = h * S, (h + 1) * S
            while r < end:
                n = min(end - r, P - r % P)
                pieces.append((h, r - h * S, n, r // P, r % P))
                r += n
        V_MOVES = len(pieces) * KC

        with ExitStack() as c2:
            ps = c2.enter_context(nc.psum_tensor("a0_setup", [P, 8, 512], F32))
            block = c2.enter_context(nc.Block())

            @block.sync
            def _(sp):
                sp.dma_start(ctx_sb[:], ctx.rearrange("n s d -> s n d")).then_inc(ctx_in, 16)
                for w, src in ((wk, Wk), (wv, Wv), (wq, Wq), (wo, Wo)):
                    sp.dma_start(w[:], src.rearrange("(k p) n -> p k n", p=P)).then_inc(w_in, 16)
                sp.dma_start(x_sb[:], x.rearrange("n (k p) d -> p (n k) d", p=P)).then_inc(x_in, 16)
                sp.wait_ge(v_ready, NB)
                sp.wait_ge(pads_ready, 1)
                for h, s0, n, j, p0 in pieces:
                    for m in range(KC):
                        sp.dma_start(v_blocks[p0:p0 + n, :, m, j, h * HD:(h + 1) * HD],
                                     v_sb[s0:s0 + n, :, m * P + h * HD:m * P + (h + 1) * HD]).then_inc(v_moved, 16)

            @block.scalar
            def _(act):
                act.dma_start(bkT[:], bk.rearrange("(m p) -> p m", p=P), allow_slow_non_contiguous=True).then_inc(b_in, 16)
                act.dma_start(bqT[:], bq.rearrange("(m p) -> p m", p=P), allow_slow_non_contiguous=True).then_inc(b_in, 16)
                act.dma_start(bv_b[:], bv.rearrange("(a d) -> a d", a=1).to_broadcast([P, D])).then_inc(b_in, 16)
                act.dma_start(bo_b[:], bo.rearrange("(a d) -> a d", a=1).to_broadcast([P, D])).then_inc(b_in, 16)
                for k in range(KC):
                    act.wait_ge(ctxT_done, k + 1)
                    act.copy(ctxT[:, k, :], ps[:, k, 0:NB * S]).then_inc(ctxT_ready, 1)
                act.wait_ge(b_in, 64)
                for m in range(KC):
                    act.wait_ge(kv_done, m + 1)
                    act.activation(kT[:, m, :, :].rearrange("p n s -> p (n s)"), ps[:, 2 + m, 0:NB * S], ACT.Identity,
                                   bias=bkT[:, m:m + 1]).then_inc(k_ready, 1)

            @block.gpsimd
            def _(pool):
                pool.memset(ident[:], 0.0).then_inc(pool_chain, 1)
                pool.wait_ge(pool_chain, 1)
                pool.affine_select(out=ident[:], in_=ident[:], compare_op=ALU.not_equal, fill=1.0, base=0,
                                   pattern=[[-1, P]], channel_multiplier=1).then_inc(ident_ready, 1)
                pool.memset(head_mask[:], 1.0).then_inc(pool_chain, 1)
                pool.wait_ge(pool_chain, 2)
                pool.affine_select(out=head_mask[:], in_=head_mask[:], compare_op=ALU.is_ge, fill=0.0, base=0,
                                   pattern=[[-HD, HM]], channel_multiplier=1).then_inc(pool_chain, 1)
                pool.wait_ge(pool_chain, 3)
                pool.affine_select(out=head_mask[:], in_=head_mask[:], compare_op=ALU.is_ge, fill=0.0, base=HD - 1,
                                   pattern=[[HD, HM]], channel_multiplier=-1).then_inc(mask_ready, 1)
                pool.memset(v_blocks[:], 0.0).then_inc(pads_ready, 1)

            @block.vector
            def _(dve):
                dve.memset(k_blocks[:], 0.0)
                dve.wait_ge(b_in, 64)
                for n in range(NB):
                    dve.wait_ge(kv_done, KC + n + 1)
                    dve.tensor_tensor(v_sb[:, n, :], ps[0:S, 4 + n, 0:D], bv_b[0:S, :], ALU.add).then_inc(v_ready, 1)

            @block.tensor
            def _(pe):
                pe.wait_ge(ident_ready, 1)
                pe.wait_ge(ctx_in, 16)
                for k in range(KC):
                    for n in range(NB):
                        last = pe.transpose(ps[:, k, n * S:(n + 1) * S], ctx_sb[:, n, k * P:(k + 1) * P],
                                            ident[0:S, 0:S])
                    last.then_inc(ctxT_done, 1)
                pe.wait_ge(ctxT_ready, KC)
                pe.wait_ge(w_in, 64)
                for m in range(KC):
                    for k in range(KC):
                        last = pe.matmul(ps[:, 2 + m, 0:NB * S], wk[:, k, m * P:(m + 1) * P], ctxT[:, k, :],
                                         start=(k == 0), stop=(k == KC - 1))
                    last.then_inc(kv_done, 1)
                for n in range(NB):
                    for k in range(KC):
                        last = pe.matmul(ps[0:S, 4 + n, 0:D], ctxT[:, k, n * S:(n + 1) * S], wv[:, k, :],
                                         start=(k == 0), stop=(k == KC - 1))
                    last.then_inc(kv_done, 1)

        with ExitStack() as c2:
            def sb2(name, shape, dt=F32):
                return c2.enter_context(nc.sbuf_tensor("a0m_" + name, shape, dt))

            def sem2(name):
                return c2.enter_context(nc.semaphore("a0m_" + name))

            gate_sb = sb2("gate", [P, KC, E])
            xn, xn2 = sb2("xn", [P, TB, D]), sb2("xn2", [P, TB, D])
            xT, x2T = sb2("xT", [P, KC, L]), sb2("x2T", [P, KC, L])
            qT = sb2("qT", [P, KC, L])
            e_sb = sb2("e", [P, 2, L])
            v_scaled = sb2("v_scaled", [P, 2, P])
            aT = sb2("aT", [P, KC, L])
            stats, mv = sb2("stats", [P, TB, 6]), sb2("mv", [P, TB, 2])
            var, rstd, tmp = sb2("var", [P, TB]), sb2("rstd", [P, TB]), sb2("tmp", [P, TB])
            mx, nmx = sb2("mx", [P, U]), sb2("nmx", [P, U])
            sums, rsum = sb2("sums", [P, U]), sb2("rsum", [P, U])
            dve_chain, gate_in, xn_out = sem2("dve_chain"), sem2("gate_in"), sem2("xn_out")
            xn_ready, xn2_ready, kb_ready = sem2("xn_ready"), sem2("xn2_ready"), sem2("kb_ready")
            bo_added, x_added = sem2("bo_added"), sem2("x_added")
            pool_passed, dve_passed = sem2("pool_passed"), sem2("dve_passed")
            scores_done, max_ready, exp_done = sem2("scores_done"), sem2("max_ready"), sem2("exp_done")
            vs_ready, pv_done, o_moved = sem2("vs_ready"), sem2("pv_done"), sem2("o_moved")
            work = c2.enter_context(nc.psum_tensor("a0_work", [P, 2, 512], F32))
            scores = c2.enter_context(nc.psum_tensor("a0_scores_ps", [P, 2, L], F32))
            o_ps = c2.enter_context(nc.psum_tensor("a0_out_ps", [P, L], F32))
            HALF = L // 2
            TH = TB // 2
            ORDER = [("q1", 0, 0), ("q1", 1, 0), ("out", 0, -1), ("out", 1, -1), ("out", 2, -1), ("out", 3, -1),
                     ("xT", 0, 1), ("xT", 1, 1), ("xT", 2, 1), ("xT", 3, 1), ("q0", 0, 1), ("q0", 1, 1),
                     ("x2", 0, -1), ("x2", 1, -1), ("x2", 2, -1), ("x2", 3, -1), ("z", 0, -1), ("z", 1, -1)]
            per = {kind: u + 1 for kind, u, _ in sorted(ORDER)}
            place = {(kind, u): i for i, (kind, u, _) in enumerate(ORDER)}
            assert len(ORDER) % 2 == 0
            full = {kind: sem2("full_" + kind) for kind in per}
            freed = {kind: sem2("freed_" + kind) for kind in per}
            block = c2.enter_context(nc.Block())

            def has(n):
                return not isinstance(n, int) or 0 <= n < NB

            def wait(eng, sem, value):
                if not isinstance(value, int) or value > 0:
                    eng.wait_ge(sem, value)

            def bank(kind, u):
                return work[:, place[kind, u] % 2, :]

            def take(n, kind, u):
                row, i = n, place[kind, u] - 2
                for _ in range(len(ORDER)):
                    if i < 0:
                        i, row = i + len(ORDER), row - 1
                    kind2, u2, dist2 = ORDER[i]
                    if has(row + dist2):
                        before = per["z"] if kind2 == "z" else 0
                        wait(nc.tensor, freed[kind2], per[kind2] * (row + dist2) + u2 + 1 + before)
                        break
                    i -= 2
                return bank(kind, u)

            def program(eng, row, chain=None, steps=0):
                row(-1)
                row(0)
                with eng.Fori(1, NB - 1) as n:
                    if chain:
                        chain.enter(n - 1, steps)
                    row(n)
                if chain:
                    chain.leave(NB - 2)
                row(NB - 1)
                row(NB)

            @block.sync
            def _(sp):
                sp.dma_start(gate_sb[:], gate.rearrange("(k p) e -> p k e", p=P)).then_inc(gate_in, 16)
                with sp.Fori(0, NB) as n:
                    b = sp.snap(n)
                    sp.wait_ge(xn2_ready, TB * n + TB)
                    sp.dma_start(xn_dram.rearrange("(n k p) d -> n p k d", n=NB, p=P)[b], xn2[:]).then_inc(xn_out, 16)
                sp.wait_ge(xn_out, 16 * NB)

            @block.tensor
            def _(pe):
                def unit_scores(n, u):
                    m, j = divmod(u, JT)
                    if j == 0:
                        pe.wait_ge(kb_ready, KC * n + m + 1)
                        pe.wait_ge(freed["q0" if m == 0 else "q1"], 2 * n + 2)
                    wait(pe, exp_done, U * n + u - 1)
                    for h in range(2):
                        last = pe.matmul(scores[:, u % 2, h * HALF:(h + 1) * HALF], k_blocks[:, m, j * P:(j + 1) * P],
                                         qT[:, m, h * HALF:(h + 1) * HALF], start=True, stop=True)
                    last.then_inc(scores_done, 1)

                def unit_values(n, u):
                    m, j = divmod(u, JT)
                    pe.wait_ge(vs_ready, U * n + u + 1)
                    if j == 0:
                        wait(pe, o_moved, KC * n + m)
                    for h in range(2):
                        last = pe.matmul(o_ps[:, h * HALF:(h + 1) * HALF], v_scaled[:, u % 2, :],
                                         e_sb[:, u % 2, h * HALF:(h + 1) * HALF], start=(j == 0), stop=(j == JT - 1))
                    last.then_inc(pv_done, 1)

                def turn(n, kind, u, rows, ready, i):
                    h, k = divmod(u, KC)
                    pe.wait_ge(ready, TB * i + TH * (h + 1))
                    ps = take(n, kind, u)
                    for t in range(TH):
                        last = pe.transpose(ps[:, t * P:(t + 1) * P], rows[:, TH * h + t, k * P:(k + 1) * P], ident[:])
                    last.then_inc(full[kind], 1)

                def project_q(n, m, h, i):
                    kind = "q0" if m == 0 else "q1"
                    pe.wait_ge(freed["xT"], 4 * i + 2 * h + 2)
                    ps = take(n, kind, h)
                    for k in range(KC):
                        last = pe.matmul(ps, wq[:, k, m * P:(m + 1) * P], xT[:, k, h * HALF:(h + 1) * HALF],
                                         start=(k == 0), stop=(k == KC - 1))
                    last.then_inc(full[kind], 1)

                def output(n, w, i):
                    pe.wait_ge(o_moved, KC * i + KC)
                    ps = take(n, "out", w)
                    for t in range(2):
                        c0 = (2 * w + t) * P
                        for m in range(KC):
                            last = pe.matmul(ps[:, t * D:(t + 1) * D], aT[:, m, c0:c0 + P], wo[:, m, :],
                                             start=(m == 0), stop=(m == KC - 1))
                    last.then_inc(full["out"], 1)

                def logits(n, h, i):
                    pe.wait_ge(freed["x2"], 4 * i + 2 * h + 2)
                    ps = take(n, "z", h)
                    for t in range(TH):
                        for k in range(KC):
                            last = pe.matmul(ps[:, t * E:(t + 1) * E], x2T[:, k, (TH * h + t) * P:(TH * h + t + 1) * P],
                                             gate_sb[:, k, :], start=(k == 0), stop=(k == KC - 1))
                    last.then_inc(full["z"], 1)

                def row(n):
                    for u in range(U):
                        if has(n):
                            unit_scores(n, u)
                            if u:
                                unit_values(n, u - 1)
                            if u == 0:
                                project_q(n, 1, 0, n)
                                project_q(n, 1, 1, n)
                        if 1 <= u <= 4 and has(n - 1):
                            output(n, u - 1, n - 1)
                        if 5 <= u <= 6 and has(n + 1):
                            for k in range(KC):
                                turn(n, "xT", 2 * (u - 5) + k, xn, xn_ready, n + 1)
                        if 7 <= u <= 8 and has(n + 1):
                            project_q(n, 0, u - 7, n + 1)
                        if u == 9 and has(n - 1):
                            for k in range(KC):
                                turn(n, "x2", k, xn2, xn2_ready, n - 1)
                    if has(n):
                        unit_values(n, U - 1)
                    if has(n - 1):
                        for k in range(KC):
                            turn(n, "x2", 2 + k, xn2, xn2_ready, n - 1)
                        for h in range(2):
                            logits(n, h, n - 1)

                pe.wait_ge(gate_in, 16)
                program(pe, row)

            @block.scalar
            def _(act):
                def unit_exp(n, u):
                    act.wait_ge(max_ready, U * n + u + 1)
                    wait(act, pv_done, U * n + u - 1)
                    act.activation(e_sb[:, u % 2, :], scores[:, u % 2, :], ACT.Exp, bias=nmx[:, u:u + 1],
                                   scale=SCALE, accum_out=sums[:, u:u + 1]).then_inc(exp_done, 1)

                def move_out(n, m):
                    act.wait_ge(pv_done, U * n + JT * (m + 1))
                    wait(act, full["out"], 4 * n)
                    act.copy(aT[:, m, :], o_ps[:, :]).then_inc(o_moved, 1)

                def take_turned(kind, u, dst, i):
                    h, k = divmod(u, KC)
                    act.wait_ge(full[kind], 4 * i + u + 1)
                    if kind == "x2" and u == 0:
                        wait(act, full["z"], 2 * i)
                    act.copy(dst[:, k, h * HALF:(h + 1) * HALF], bank(kind, u)).then_inc(freed[kind], 1)

                def take_q(m, h, i):
                    kind = "q0" if m == 0 else "q1"
                    act.wait_ge(full[kind], 2 * i + h + 1)
                    act.activation(qT[:, m, h * HALF:(h + 1) * HALF], bank(kind, h), ACT.Identity,
                                   bias=bqT[:, m:m + 1]).then_inc(freed[kind], 1)

                def row(n):
                    for u in range(U):
                        if has(n):
                            unit_exp(n, u)
                            if u == 0:
                                take_q(1, 0, n)
                                take_q(1, 1, n)
                            if u == JT:
                                move_out(n, 0)
                        if 5 <= u <= 6 and has(n + 1):
                            if u == 5 and has(n):
                                act.wait_ge(full["q1"], 2 * n + 2)
                            for k in range(KC):
                                take_turned("xT", 2 * (u - 5) + k, xT, n + 1)
                        if 7 <= u <= 8 and has(n + 1):
                            if has(n):
                                act.wait_ge(scores_done, U * n + JT)
                            take_q(0, u - 7, n + 1)
                        if u == 9 and has(n - 1):
                            for k in range(KC):
                                take_turned("x2", k, x2T, n - 1)
                    if has(n):
                        move_out(n, KC - 1)
                    if has(n - 1):
                        for k in range(KC):
                            take_turned("x2", 2 + k, x2T, n - 1)

                program(act, row)

            @block.gpsimd
            def _(pool):
                with pool.Fori(0, NB) as n:
                    for k in range(TB):
                        if k == 0:
                            pool.wait_ge(xn_ready, TB * n + TB)
                            alone(pool, pool_passed)
                        pool.tensor_tensor(x4[:, n, k, :], x4[:, n, k, :], bo_b[:], ALU.add).then_inc(bo_added, 1)

            @block.vector
            def _(dve):
                chain = Chain(dve, dve_chain)

                def unit_max(n, u):
                    dve.wait_ge(scores_done, U * n + u + 1)
                    chain.link(dve.tensor_reduce(mx[:, u:u + 1], scores[:, u % 2, :], AX.X, ALU.max))
                    dve.tensor_scalar(nmx[:, u:u + 1], mx[:, u:u + 1], -SCALE, None, ALU.mult).then_inc(max_ready, 1)

                def unit_scale(n, u):
                    m, j = divmod(u, JT)
                    dve.wait_ge(exp_done, U * n + u + 1)
                    chain.link(dve.reciprocal(rsum[:, u:u + 1], sums[:, u:u + 1]))
                    wait(dve, pv_done, U * n + u - 1)
                    dve.tensor_scalar(v_scaled[:, u % 2, :], v_blocks[:, n, m, j, :], rsum[:, u:u + 1], None,
                                      ALU.mult).then_inc(vs_ready, 1)

                def place_keys(n, m):
                    dve.tensor_tensor(k_blocks[:, m, 0:HM * S].rearrange("p (h s) -> p h s", s=S),
                                      kT[:, m, n, :].rearrange("p (a s) -> p a s", a=1).to_broadcast([P, HM, S]),
                                      head_mask[:, :].rearrange("p (h a) -> p h a", a=1).to_broadcast([P, HM, S]),
                                      ALU.mult).then_inc(kb_ready, 1)

                def tiles(i, h):
                    return [x4[:, i, TH * h + t, :] for t in range(TH)]

                def statistics(i, h):
                    for t, x_tile in enumerate(tiles(i, h)):
                        chain.step(dve.bn_stats(stats[:, TH * h + t, :], x_tile))

                def write(i, h, rows, ready):
                    for t, x_tile in enumerate(tiles(i, h)):
                        k = TH * h + t
                        dve.tensor_scalar(rows[:, k, :], x_tile, mv[:, k, 0:1], rstd[:, k:k + 1],
                                          ALU.subtract, ALU.mult).then_inc(ready, 1)

                def add_output(w, i):
                    dve.wait_ge(full["out"], 4 * i + w + 1)
                    if w == 0:
                        dve.wait_ge(bo_added, TB * i + TB)
                    dve.tensor_tensor(x4[:, i, 2 * w:2 * w + 2, :], bank("out", w).rearrange("p (t d) -> p t d", t=2),
                                      x4[:, i, 2 * w:2 * w + 2, :], ALU.add).then_inc(freed["out"], 1)

                def take_logits(h, i):
                    dve.wait_ge(full["z"], 2 * i + h + 1)
                    dve.tensor_copy(z_all[:, :, :].rearrange("p (n h k) e -> p n h (k e)", h=2, k=TH)[:, i, h, :],
                                    bank("z", h)[:, 0:TH * E]).then_inc(freed["z"], 1)

                def row(n):
                    for u in range(U):
                        if has(n):
                            if u:
                                unit_scale(n, u - 1)
                            unit_max(n, u)
                            if u == 0:
                                place_keys(n, 1)
                        if 1 <= u <= 2 and has(n + 1):
                            statistics(n + 1, u - 1)
                        if 2 <= u <= 5 and has(n - 1):
                            add_output(u - 2, n - 1)
                        if u == 3 and has(n + 1):
                            dve.wait_ge(chain.sem, chain.base + chain.n)
                            moments(dve, chain, stats, mv, var[:], rstd[:], tmp[:], D)
                        if 4 <= u <= 5 and has(n + 1):
                            wait(dve, full["xT"], 4 * (n + 1))
                            write(n + 1, u - 4, xn, xn_ready)
                        if 5 <= u <= 6 and has(n - 1):
                            if u == 5:
                                dve.wait_ge(freed["out"], 4 * (n - 1) + 4)
                                if has(n + 1):
                                    dve.wait_ge(xn_ready, TB * (n + 1) + TB)
                                alone(dve, dve_passed)
                            statistics(n - 1, u - 5)
                        if u == 6 and has(n + 1):
                            place_keys(n + 1, 0)
                        if u == 7 and has(n - 1):
                            dve.wait_ge(chain.sem, chain.base + chain.n)
                            moments(dve, chain, stats, mv, var[:], rstd[:], tmp[:], D)
                        if 8 <= u <= 9 and has(n - 1):
                            wait(dve, full["x2"], 4 * (n - 1))
                            wait(dve, xn_out, 16 * (n - 1))
                            write(n - 1, u - 8, xn2, xn2_ready)
                    if has(n):
                        unit_scale(n, U - 1)
                    if has(n - 1):
                        for h in range(2):
                            take_logits(h, n - 1)

                dve.sem_inc(freed["z"], per["z"])
                dve.wait_ge(x_in, 16)
                dve.wait_ge(v_moved, 16 * V_MOVES)
                program(dve, row, chain, 2 * (TB + MOMENTS_STEPS) + 2 * U)


def alone(eng, passed):
    eng.sem_inc(passed, 1)


class Routes:
    pass


def routes_of(nc, tag, keep, K, TILES, CAP, NT):
    r = Routes()

    def kept(name, shape, dt=F32):
        return keep.enter_context(nc.sbuf_tensor(f"{tag}_{name}", shape, dt))

    r.gates = [kept(f"gate{k}", [P, NT]) for k in range(K)]
    r.slot = [kept(f"slot{k}", [P, NT + 1], I32) for k in range(K)]
    r.token = kept("token", [P, TILES + 1], I32)
    r.expert = kept("expert", [P, TILES], I32)
    if CAP is not None:
        r.target = kept("target", [P, TILES], I32)
        r.slot_gate = kept("slot_gate", [P, TILES])
    return r


def route(nc, tag, r, z, K, E, TILES, CAP, NT, load):
    GROUPS = 2 if CAP is None else 6
    with ExitStack() as c:
        def sb(name, shape, dt=F32):
            return c.enter_context(nc.sbuf_tensor(f"{tag}_{name}", shape, dt))

        def sem(name):
            return c.enter_context(nc.semaphore(f"{tag}_{name}"))

        p, p2 = sb("p", [P, NT, E]), sb("p2", [P, NT, E])
        t1, t2 = sb("t1", [P, NT, E]), sb("t2", [P, NT, E])
        hot = [sb(f"hot{k}", [P, NT, E]) for k in range(K)]
        hot_all = sb("hot_all", [P, NT, E], BF16)
        m1, m2, m3 = sb("m1", [P, NT]), sb("m2", [P, NT]), sb("m3", [P, NT])
        mi, ti, bi = sb("mi", [P, NT], I32), sb("ti", [P, NT], I32), sb("bi", [P, NT], I32)
        tf, bf = sb("tf", [P, NT]), sb("bf", [P, NT])
        slots_f = sb("slots_f", [P, NT, E])
        iota_e = sb("iota_e", [P, E])
        iota_p = sb("iota_p", [P, P])
        iota_t = sb("iota_t", [P, TILES])
        iota_i = sb("iota_i", [P, NT])
        own_p = sb("own_p", [P, 1])
        gate_part = sb("gate_part", [P, NT], BF16)
        lower = sb("lower", [P, P], BF16)
        ones = sb("ones", [P, P], BF16)
        count_i, count_t = sb("count_i", [P, E], I32), sb("count_t", [P, E], I32)
        tiles_f, ones_e, upto, first = sb("tiles_f", [P, E]), sb("ones_e", [P, E]), sb("upto", [P, E]), sb("first", [P, E])
        in_row = [sb(f"in_row{k}", [P, NT, P], BF16) for k in range(K)]
        in_tile = [sb(f"in_tile{k}", [P, NT, GROUPS, TILES], BF16) for k in range(K)]
        in_tile_f = sb("in_tile_f", [P, NT, TILES], BF16)
        token_f = sb("token_f", [P, TILES])
        tile_e = sb("tile_e", [P, TILES, E], BF16)
        tile_s = sb("tile_s", [P, TILES])

        consts_ready, pool_chain, dve_chain = sem("consts_ready"), sem("pool_chain"), sem("dve_chain")
        exp_ready, exp_done, hot_ready, ranks_done = (sem(s) for s in ("exp_ready", "exp_done", "hot_ready", "ranks_done"))
        rows_ready, tokens_done = sem("rows_ready"), sem("tokens_done")
        rank_ps = c.enter_context(nc.psum_tensor(f"{tag}_rank_ps", [P, 512], F32))
        count_ps = c.enter_context(nc.psum_tensor(f"{tag}_count_ps", [P, 512], F32))
        token_ps = c.enter_context(nc.psum_tensor(f"{tag}_token_ps", [P, 512], F32))
        block = c.enter_context(nc.Block())

        @block.sync
        def _(sp):
            load(sp)

        @block.gpsimd
        def _(pool):
            pool.iota(iota_e[:], [[1, E]], base=-E, channel_multiplier=0, allow_small_or_imprecise_dtypes=True)
            pool.iota(iota_p[:], [[1, P]], base=0, channel_multiplier=0, allow_small_or_imprecise_dtypes=True)
            pool.iota(iota_t[:], [[1, TILES]], base=0, channel_multiplier=0, allow_small_or_imprecise_dtypes=True)
            pool.iota(iota_i[:], [[1, NT]], base=0, channel_multiplier=0, allow_small_or_imprecise_dtypes=True)
            pool.iota(own_p[:], [[0, 1]], base=0, channel_multiplier=1, allow_small_or_imprecise_dtypes=True)
            pool.memset(ones_e[:], 1.0)
            pool.memset(r.token[:, TILES:TILES + 1], 0)
            for k in range(K):
                pool.memset(r.slot[k][:, NT:NT + 1], 0)
            pool.memset(ones[:], 1.0)
            pool.memset(lower[:], 1.0).then_inc(pool_chain, 1)
            pool.wait_ge(pool_chain, 1)
            pool.affine_select(out=lower[:], in_=lower[:], compare_op=ALU.is_gt, fill=0.0, base=0,
                               pattern=[[1, P]], channel_multiplier=-1).then_inc(consts_ready, 1)

        @block.tensor
        def _(pe):
            pe.wait_ge(consts_ready, 1)
            pe.wait_ge(hot_ready, 1)
            h2 = hot_all[:, :, :].rearrange("p i e -> p (i e)")
            for s in range(1, NT):
                pe.matmul(rank_ps[:, s * E:NT * E], ones[:], h2[:, 0:(NT - s) * E], start=(s == 1), stop=False,
                          skip_group_check=True)
            pe.matmul(rank_ps[:, 0:NT * E], lower[:], h2, start=False, stop=True, skip_group_check=True)
            for i in range(NT):
                last = pe.matmul(count_ps[:, 0:E], ones[:], hot_all[:, i, :], start=(i == 0), stop=(i == NT - 1))
            last.then_inc(ranks_done, 1)
            pe.wait_ge(rows_ready, 1)
            for k in range(K):
                for i in range(NT):
                    last = pe.matmul(token_ps[:, 0:GROUPS * TILES], in_row[k][:, i, :],
                                     in_tile[k][:, i, :, :].rearrange("p a t -> p (a t)"),
                                     start=(k == 0 and i == 0), stop=(k == K - 1 and i == NT - 1))
            last.then_inc(tokens_done, 1)

        @block.scalar
        def _(act):
            act.wait_ge(exp_ready, 1)
            act.activation(t1[:], t2[:], ACT.Exp).then_inc(exp_done, 1)

        @block.vector
        def _(dve):
            chain = Chain(dve, dve_chain)
            link = chain.link

            def per_token(a):
                return a.rearrange("p (i a) -> p i a", a=1).to_broadcast([P, NT, E])

            def per_expert(a):
                return a.rearrange("p (a e) -> p a e", a=1).to_broadcast([P, NT, E])

            dve.wait_ge(consts_ready, 1)
            link(dve.tensor_reduce(m1[:], z[:], AX.X, ALU.max))
            dve.tensor_tensor(t2[:], z[:], per_token(m1[:]), ALU.subtract).then_inc(exp_ready, 1)
            dve.wait_ge(exp_done, 1)
            link(dve.tensor_reduce(m2[:], t1[:], AX.X, ALU.add))
            link(dve.reciprocal(m3[:], m2[:]))
            link(dve.tensor_tensor(p[:], t1[:], per_token(m3[:]), ALU.mult))
            left = p
            for k in range(K):
                link(dve.tensor_reduce(r.gates[k][:], left[:], AX.X, ALU.max))
                link(dve.tensor_tensor(t1[:], left[:], per_token(r.gates[k][:]), ALU.is_equal))
                link(dve.tensor_tensor(t2[:], t1[:], per_expert(iota_e[:]), ALU.mult))
                link(dve.tensor_reduce(m1[:], t2[:], AX.X, ALU.min))
                link(dve.tensor_tensor(hot[k][:], per_expert(iota_e[:]), per_token(m1[:]), ALU.is_equal))
                if k + 1 < K:
                    link(dve.scalar_tensor_tensor(p2[:], hot[k][:], -2.0, left[:], ALU.mult, ALU.add))
                    left = p2
            if K == 2:
                link(dve.tensor_tensor(m1[:], r.gates[0][:], r.gates[1][:], ALU.add))
                link(dve.tensor_scalar(m2[:], m1[:], 1e-12, None, ALU.max))
                link(dve.reciprocal(m3[:], m2[:]))
                for k in range(K):
                    link(dve.tensor_tensor(r.gates[k][:], r.gates[k][:], m3[:], ALU.mult))
                dve.tensor_tensor(hot_all[:], hot[0][:], hot[1][:], ALU.add).then_inc(hot_ready, 1)
            else:
                dve.tensor_copy(hot_all[:], hot[0][:]).then_inc(hot_ready, 1)
            dve.wait_ge(ranks_done, 1)
            ranks = rank_ps[:, 0:NT * E].rearrange("p (i e) -> p i e", e=E)
            if CAP is None:
                link(dve.tensor_scalar(count_i[:], count_ps[:, 0:E], float(P - 1), None, ALU.add))
                link(dve.tensor_scalar(count_t[:], count_i[:], P.bit_length() - 1, None, ALU.logical_shift_right))
                link(dve.tensor_copy(tiles_f[:], count_t[:]))
                link(dve.tensor_tensor_scan(upto[:], ones_e[:], tiles_f[:], 0.0, ALU.mult, ALU.add))
                link(dve.tensor_tensor(first[:], upto[:], tiles_f[:], ALU.subtract))
                link(dve.tensor_scalar(first[:], first[:], float(P), None, ALU.mult))
            else:
                link(dve.tensor_scalar(first[:], iota_e[:], float(E), float(CAP), ALU.add, ALU.mult))
                link(dve.tensor_scalar(upto[:], first[:], float(CAP), 1.0 / P, ALU.add, ALU.mult))
            link(dve.tensor_tensor(slots_f[:], ranks, per_expert(first[:]), ALU.add))
            for k in range(K):
                link(dve.tensor_tensor(t1[:], hot[k][:], slots_f[:], ALU.mult))
                link(dve.tensor_reduce(m1[:], t1[:], AX.X, ALU.add))
                if CAP is not None:
                    link(dve.tensor_tensor(t2[:], hot[k][:], ranks, ALU.mult))
                    link(dve.tensor_reduce(m2[:], t2[:], AX.X, ALU.add))
                    link(dve.tensor_scalar(m3[:], m2[:], float(CAP), None, ALU.is_lt))
                    link(dve.tensor_tensor(r.gates[k][:], r.gates[k][:], m3[:], ALU.mult))
                    link(dve.tensor_tensor(m1[:], m1[:], m3[:], ALU.mult))
                    link(dve.tensor_copy(r.slot[k][:, 0:NT], m1[:]))
                    link(dve.tensor_scalar(m3[:], m3[:], -FAR, FAR, ALU.mult, ALU.add))
                    link(dve.tensor_tensor(m1[:], m1[:], m3[:], ALU.add))
                else:
                    link(dve.tensor_copy(r.slot[k][:, 0:NT], m1[:]))
                link(dve.tensor_copy(mi[:], m1[:]))
                link(dve.tensor_scalar(ti[:], mi[:], P.bit_length() - 1, None, ALU.logical_shift_right))
                link(dve.tensor_scalar(bi[:], mi[:], P - 1, None, ALU.bitwise_and))
                link(dve.tensor_copy(tf[:], ti[:]))
                link(dve.tensor_copy(bf[:], bi[:]))
                link(dve.tensor_tensor(in_row[k][:], bf[:, :].rearrange("p (i a) -> p i a", a=1).to_broadcast([P, NT, P]),
                                       iota_p[:, :].rearrange("p (a q) -> p a q", a=1).to_broadcast([P, NT, P]),
                                       ALU.is_equal))
                link(dve.tensor_tensor(in_tile_f[:],
                                       tf[:, :].rearrange("p (i a) -> p i a", a=1).to_broadcast([P, NT, TILES]),
                                       iota_t[:, :].rearrange("p (a q) -> p a q", a=1).to_broadcast([P, NT, TILES]),
                                       ALU.is_equal))
                link(dve.tensor_tensor(in_tile[k][:, :, 0, :], in_tile_f[:],
                                       iota_i[:, :].rearrange("p (i a) -> p i a", a=1).to_broadcast([P, NT, TILES]),
                                       ALU.mult))
                link(dve.tensor_scalar(in_tile[k][:, :, 1, :], in_tile_f[:], own_p[:, 0:1], None, ALU.mult))
                if CAP is not None:
                    chain.step(dve.tensor_copy(in_tile[k][:, :, 2, :], in_tile_f[:]))
                    link(dve.tensor_copy(m1[:], r.gates[k][:]))
                    for part in range(3):
                        link(dve.tensor_copy(gate_part[:], m1[:]))
                        chain.step(dve.tensor_tensor(m1[:], m1[:], gate_part[:], ALU.subtract))
                        link(dve.tensor_tensor(in_tile[k][:, :, 3 + part, :], in_tile_f[:],
                                               gate_part[:, :].rearrange("p (i a) -> p i a", a=1)
                                               .to_broadcast([P, NT, TILES]), ALU.mult))
            dve.tensor_copy(tf[:], ti[:]).then_inc(rows_ready, 1)
            link(dve.tensor_tensor(tile_e[:], upto[:, :].rearrange("p (a e) -> p a e", a=1).to_broadcast([P, TILES, E]),
                                   iota_t[:, :].rearrange("p (t a) -> p t a", a=1).to_broadcast([P, TILES, E]),
                                   ALU.is_le))
            link(dve.tensor_reduce(tile_s[:], tile_e[:], AX.X, ALU.add))
            link(dve.tensor_scalar(r.expert[:], tile_s[:], float(E - 1), None, ALU.min))
            dve.wait_ge(tokens_done, 1)
            link(dve.tensor_copy(token_f[:], token_ps[:, TILES:2 * TILES]))
            link(dve.scalar_tensor_tensor(r.token[:, 0:TILES], token_ps[:, 0:TILES], float(P), token_f[:],
                                          ALU.mult, ALU.add))
            if CAP is not None:
                link(dve.tensor_scalar(token_f[:], token_ps[:, 2 * TILES:3 * TILES], -FAR, FAR, ALU.mult, ALU.add))
                chain.step(dve.tensor_tensor(r.target[:], r.token[:, 0:TILES], token_f[:], ALU.add))
                link(dve.tensor_copy(r.slot_gate[:], token_ps[:, 3 * TILES:4 * TILES]))
                for part in (4, 5):
                    link(dve.tensor_tensor(r.slot_gate[:], r.slot_gate[:],
                                           token_ps[:, part * TILES:(part + 1) * TILES], ALU.add))


class Weights:
    pass


def experts_0_weights(nc, keep, E, D, H, KC):
    w = Weights()
    HC = H // P

    def kept(name, shape):
        return keep.enter_context(nc.sbuf_tensor("e0_" + name, shape, F32))

    w.w1, w.w2 = kept("w1", [P, KC, E, H]), kept("w2", [P, HC, E, D])
    w.b1_b, w.b2_b = kept("b1_b", [P, E, H]), kept("b2_b", [P, E, D])
    w.w_in = keep.enter_context(nc.semaphore("e0_w_in"))
    w.loads = KC + HC + 2
    return w


def load_experts_0(sp, w, W1, b1, W2, b2, E, D, H, KC):
    for k in range(KC):
        sp.dma_start(w.w1[:, k, :, :], W1[:, k * P:(k + 1) * P, :].rearrange("e p h -> p e h")).then_inc(w.w_in, 16)
    sp.dma_start(w.b1_b[:, :, :].rearrange("p e h -> p (e h)"),
                 b1.rearrange("(a e) h -> a (e h)", a=1).to_broadcast([P, E * H])).then_inc(w.w_in, 16)
    for j in range(H // P):
        sp.dma_start(w.w2[:, j, :, :], W2[:, j * P:(j + 1) * P, :].rearrange("e p d -> p e d")).then_inc(w.w_in, 16)
    sp.dma_start(w.b2_b[:, :, :].rearrange("p e h -> p (e h)"),
                 b2.rearrange("(a e) h -> a (e h)", a=1).to_broadcast([P, E * D])).then_inc(w.w_in, 16)


def attention_1_weights(nc, keep, D, KC, INNER):
    w = Weights()

    def kept(name, shape):
        return keep.enter_context(nc.sbuf_tensor("a1_" + name, shape, F32))

    w.wq, w.wk, w.wv = (kept(n, [P, KC, INNER]) for n in ("wq", "wk", "wv"))
    w.wo = kept("wo", [P, INNER // P, D])
    w.w_in = keep.enter_context(nc.semaphore("a1_w_in"))
    return w


def experts_0(nc, xn_dram, y_dram, ident, r, w, E, D, H, KC, TILES, a1, Wq1, Wk1, Wv1, Wo1, HD1):
    HC = H // P
    w1, w2, b1_b, b2_b = w.w1, w.w2, w.b1_b, w.b2_b
    with ExitStack() as c:
        def sb(name, shape, dt=F32):
            return c.enter_context(nc.sbuf_tensor("e0_" + name, shape, dt))

        def sem(name):
            return c.enter_context(nc.semaphore("e0_" + name))

        index = sb("index", [P, 2], I32)
        xg = sb("xg", [P, 2, D])
        xT = sb("xT", [P, 2, KC * P])
        h_sb = sb("h", [P, 2, H])
        hT = sb("hT", [P, 2, H])
        y_sb = sb("y", [P, 2, D])
        means = sb("means", [P, a1.wq.shape[1] * a1.wq.shape[2] // HD1])
        index_ready, dve_chain = sem("index_ready"), sem("dve_chain")
        gathered = [sem(f"gathered{b}") for b in range(2)]
        stored = [sem(f"stored{b}") for b in range(2)]
        x_turned, xT_ready, h_done, h_ready, h_turned, hT_ready, y_done, y_ready = (
            sem(s) for s in ("x_turned", "xT_ready", "h_done", "h_ready", "h_turned", "hT_ready", "y_done", "y_ready"))
        x_ps = c.enter_context(nc.psum_tensor("e0_x_ps", [P, 2, 512], F32))
        h_ps = c.enter_context(nc.psum_tensor("e0_h_ps", [P, 2, 512], F32))
        hT_ps = c.enter_context(nc.psum_tensor("e0_hT_ps", [P, 2, 512], F32))
        y_ps = c.enter_context(nc.psum_tensor("e0_y_ps", [P, 2, 512], F32))
        block = c.enter_context(nc.Block())
        PAIRS = TILES // 2
        assert TILES % 2 == 0

        def pairs(eng, pair):
            pair(0)
            with eng.Fori(1, PAIRS - 1) as i:
                pair(i)
            pair(PAIRS - 1)

        def later(i):
            return not isinstance(i, int) or i > 0

        def has_next(i):
            return not isinstance(i, int) or i + 1 < PAIRS

        @block.sync
        def _(sp):
            for dst, src in ((a1.wk, Wk1), (a1.wv, Wv1), (a1.wq, Wq1), (a1.wo, Wo1)):
                sp.dma_start(dst[:], src.rearrange("(k p) n -> p k n", p=P)).then_inc(a1.w_in, 16)

            def pair(i):
                for b in range(2):
                    t = sp.snap(2 * i + b) if not isinstance(i, int) else 2 * i + b
                    sp.wait_ge(y_ready, 2 * i + b + 1)
                    sp.dma_start(y_dram.rearrange("(t p) d -> t p d", p=P)[t], y_sb[:, b, :]).then_inc(stored[b], 16)

            pairs(sp, pair)
            for b in range(2):
                sp.wait_ge(stored[b], 16 * PAIRS)

        @block.gpsimd
        def _(pool):
            pool.tensor_copy(index[:, 0:1], r.token[:, 0:1]).then_inc(index_ready, 1)

            def pair(i):
                for b in range(2):
                    after = pool.snap(2 * i + b + 1) if not isinstance(i, int) else 2 * i + b + 1
                    if later(i) or b:
                        pool.wait_ge(gathered[1 - b], 16 * i + 16 * b)
                    if later(i):
                        pool.wait_ge(x_turned, 2 * i + b - 1)
                    pool.wait_ge(index_ready, 2 * i + b + 1)
                    pool.tensor_copy(index[:, 1 - b:2 - b], r.token[:, bass.ds(after, 1)]).then_inc(index_ready, 1)
                    pool.indirect_dma_start(xg[:, b, :], None, xn_dram,
                                            bass.IndirectOffsetOnAxis(ap=index[:, b:b + 1], axis=0)
                                            ).then_inc(gathered[b], 16)

            pairs(pool, pair)

        @block.tensor
        def _(pe):
            def turn_x(i, b):
                pe.wait_ge(gathered[b], 16 * i + 16)
                if later(i):
                    pe.wait_ge(xT_ready, 2 * i + b - 1)
                for k in range(KC):
                    last = pe.transpose(x_ps[:, b, k * P:(k + 1) * P], xg[:, b, k * P:(k + 1) * P], ident[:])
                last.then_inc(x_turned, 1)

            def turn_h(i, b):
                pe.wait_ge(h_ready, 2 * i + b + 1)
                for j in range(HC):
                    last = pe.transpose(hT_ps[:, b, j * P:(j + 1) * P], h_sb[:, b, j * P:(j + 1) * P], ident[:])
                last.then_inc(h_turned, 1)

            def pair(i):
                es = [pe.value_load(r.expert[0:1, bass.ds(2 * i + b, 1)], min_val=0, max_val=E - 1) for b in range(2)]
                for b in range(2):
                    pe.wait_ge(xT_ready, 2 * i + b + 1)
                    for k in range(KC):
                        last = pe.matmul(h_ps[:, b, :], xT[:, b, k * P:(k + 1) * P],
                                         w1[:, k, es[b], :], start=(k == 0), stop=(k == KC - 1))
                    last.then_inc(h_done, 1)
                turn_h(i, 0)
                if has_next(i):
                    for b in range(2):
                        turn_x(i + 1, b)
                turn_h(i, 1)
                for b in range(2):
                    pe.wait_ge(hT_ready, 2 * i + b + 1)
                    if later(i):
                        pe.wait_ge(y_ready, 2 * i + b - 1)
                    for j in range(HC):
                        last = pe.matmul(y_ps[:, b, 0:D], hT[:, b, j * P:(j + 1) * P], w2[:, j, es[b], :],
                                         start=(j == 0), stop=(j == HC - 1))
                    last.then_inc(y_done, 1)

            for b in range(2):
                turn_x(0, b)
            pe.wait_ge(w.w_in, 16 * w.loads)
            pairs(pe, pair)

        @block.scalar
        def _(act):
            def take_x(i, b):
                act.wait_ge(x_turned, 2 * i + b + 1)
                if later(i):
                    act.wait_ge(h_done, 2 * i + b - 1)
                act.copy(xT[:, b, :], x_ps[:, b, 0:KC * P]).then_inc(xT_ready, 1)

            def take_h(i, b):
                act.wait_ge(h_turned, 2 * i + b + 1)
                if later(i):
                    act.wait_ge(y_done, 2 * i + b - 1)
                act.activation(hT[:, b, :], hT_ps[:, b, :], ACT.Relu).then_inc(hT_ready, 1)

            def pair(i):
                take_h(i, 0)
                if has_next(i):
                    for b in range(2):
                        take_x(i + 1, b)
                take_h(i, 1)

            for b in range(2):
                take_x(0, b)
            pairs(act, pair)

        @block.vector
        def _(dve):
            chain = Chain(dve, dve_chain)

            def pair(i):
                es = [dve.value_load(r.expert[0:1, bass.ds(2 * i + b, 1)], min_val=0, max_val=E - 1) for b in range(2)]
                for b in range(2):
                    dve.wait_ge(h_done, 2 * i + b + 1)
                    if later(i):
                        dve.wait_ge(h_turned, 2 * i + b - 1)
                    dve.tensor_tensor(h_sb[:, b, :], h_ps[:, b, :], b1_b[:, es[b], :], ALU.add).then_inc(h_ready, 1)
                for b in range(2):
                    dve.wait_ge(y_done, 2 * i + b + 1)
                    if later(i):
                        dve.wait_ge(stored[b], 16 * i)
                    dve.tensor_tensor(y_sb[:, b, :], y_ps[:, b, 0:D], b2_b[:, es[b], :], ALU.add).then_inc(y_ready, 1)

            dve.wait_ge(w.w_in, 16 * w.loads)
            pairs(dve, pair)
            dve.wait_ge(a1.w_in, 64)
            for weights in (a1.wk, a1.wq):
                heads = weights[:, :, :].rearrange("p k (h d) -> p (k h) d", d=HD1)
                chain.link(dve.tensor_reduce(means[:], heads, AX.X, ALU.add))
                chain.link(dve.tensor_scalar(means[:], means[:], 1.0 / HD1, None, ALU.mult))
                chain.link(dve.tensor_tensor(heads, heads, means[:, :].rearrange("p (h a) -> p h a", a=1)
                                             .to_broadcast([P, heads.shape[1], HD1]), ALU.subtract))


def attention_1(nc, a1, bo, gq, betaq, gk, betak, gate, x_sb, ident, ctxT, y0_dram, r0, z_all,
                xm_dram, out, NB, L, D, S, NT, KC, HEADS, HD, INNER, E):
    PAIR = 2
    G = HEADS // PAIR
    TB = NT // NB
    SCALE = float(HD) ** -0.5
    WC = PAIR * S
    ROWS = HEADS * S
    JT = -(-ROWS // P)
    VW = HD + 1
    OH = 512 // VW
    OB = -(-HEADS // OH)
    SB = -(-G // 3)
    IC = INNER // P
    K0 = len(r0.gates)
    first_head = [j * P // S for j in range(JT)]
    last_head = [min(((j + 1) * P - 1) // S, HEADS - 1) for j in range(JT)]
    v_at, total = [], 0
    for j in range(JT):
        v_at.append(total)
        total += (last_head[j] - first_head[j] + 1) * VW
    pieces = []
    for h in range(HEADS):
        r, end = h * S, (h + 1) * S
        while r < end:
            n = min(end - r, P - r % P)
            pieces.append((h, r - h * S, n, r // P, r % P))
            r += n
    with ExitStack() as c:
        def sb(name, shape, dt=F32):
            return c.enter_context(nc.sbuf_tensor("a1_" + name, shape, dt))

        def sem(name):
            return c.enter_context(nc.semaphore("a1_" + name))

        wq, wk, wv, wo = a1.wq, a1.wk, a1.wv, a1.wo
        bo_b = sb("bo_b", [P, D])
        gate_sb = sb("gate_w", [P, KC, E])
        k_pairs = sb("k_pairs", [P, NB, G, WC])
        v_rows = sb("v_rows", [P, NB, total])
        gq2, betaq2 = sb("gq2", [P, 1]), sb("betaq2", [P, 1])
        b_in = sem("b_in")
        setup_chain, dve_chain = sem("setup_chain"), sem("dve_chain")

        with ExitStack() as c2:
            def sb2(name, shape, dt=F32):
                return c2.enter_context(nc.sbuf_tensor("a1s_" + name, shape, dt))

            def sem2(name):
                return c2.enter_context(nc.semaphore("a1s_" + name))

            gate_rows = sb2("gate_rows", [E, D])
            v_sb = sb2("v", [S, NB, HEADS, VW])
            gk_b, betak_b = sb2("gk_b", [S, HD]), sb2("betak_b", [S, HD])
            k_sb, k_sq = sb2("k", [S, 2, HEADS, HD]), sb2("k_sq", [S, 2, HEADS, HD])
            var, rstd, tmp = sb2("var", [S, HEADS]), sb2("rstd", [S, HEADS]), sb2("tmp", [S, HEADS])
            kn_ready, k_done, v_done, k_taken, v_taken, v_moved = (
                sem2(s) for s in ("kn_ready", "k_done", "v_done", "k_taken", "v_taken", "v_moved"))
            k_turned, k_placed, pads, gate_turned = (sem2(s) for s in ("k_turned", "k_placed", "pads", "gate_turned"))
            k_squared, k_scaled, k_by_gamma = (sem2(s) for s in ("k_squared", "k_scaled", "k_by_gamma"))
            k_ps = c2.enter_context(nc.psum_tensor("a1s_k_ps", [P, 2, 512], F32))
            v_ps = c2.enter_context(nc.psum_tensor("a1s_v_ps", [P, 2, 512], F32))
            kT_ps = c2.enter_context(nc.psum_tensor("a1s_kT_ps", [P, 2, 512], F32))
            gate_ps = c2.enter_context(nc.psum_tensor("a1s_gate_ps", [P, 512], F32))
            block = c2.enter_context(nc.Block())
            kT4 = kT_ps[:, :, :].rearrange("p b (g s) -> p b g s", g=4)

            @block.sync
            def _(sp):
                for dst, src in ((gk_b, gk), (betak_b, betak)):
                    sp.dma_start(dst[:], src.rearrange("(a d) -> a d", a=1).to_broadcast([S, HD])).then_inc(b_in, 16)
                for dst, src in ((gq2, gq), (betaq2, betaq)):
                    for h in range(PAIR):
                        sp.dma_start(dst[h * HD:(h + 1) * HD, :], src.rearrange("(d a) -> d a", a=1),
                                     allow_slow_non_contiguous=True).then_inc(b_in, 16)
                sp.dma_start(bo_b[:], bo.rearrange("(a d) -> a d", a=1).to_broadcast([P, D])).then_inc(b_in, 16)
                sp.dma_start(gate_rows[:], gate).then_inc(b_in, 16)
                sp.wait_ge(v_taken, 2 * NB)
                sp.wait_ge(pads, 3)
                for h, s0, n, j, p0 in pieces:
                    at = v_at[j] + (h - first_head[j]) * VW
                    sp.dma_start(v_rows[p0:p0 + n, :, at:at + VW], v_sb[s0:s0 + n, :, h, :]).then_inc(v_moved, 16)
                sp.wait_ge(v_moved, 16 * len(pieces))

            @block.gpsimd
            def _(pool):
                pool.memset(k_pairs[:], 0.0).then_inc(pads, 1)
                pool.memset(v_rows[:], 0.0).then_inc(pads, 1)
                pool.wait_ge(pads, 2)
                pool.memset(v_sb[:, :, :, HD:VW], 1.0).then_inc(pads, 1)

                def per_column(a):
                    return a.rearrange("s (a d) -> s a d", a=1).to_broadcast([S, HEADS, HD])

                pool.wait_ge(b_in, 16 * 8)
                for n in range(NB):
                    keys = k_sb[:, n % 2, :, :]
                    pool.wait_ge(k_scaled, n + 1)
                    pool.tensor_tensor(keys, keys, per_column(gk_b[:]), ALU.mult).then_inc(k_by_gamma, 1)
                    pool.wait_ge(k_by_gamma, n + 1)
                    pool.tensor_tensor(keys, keys, per_column(betak_b[:]), ALU.add).then_inc(kn_ready, 1)

            def turn_keys(pe, n):
                pe.wait_ge(kn_ready, n + 1)
                if n:
                    pe.wait_ge(k_placed, 4 * n)
                kf = k_sb[:, n % 2, :, :].rearrange("s h d -> s (h d)")
                for g in range(G):
                    last = pe.transpose(kT4[:, g // 4, g % 4, 0:S], kf[:, g * P:(g + 1) * P], ident[0:S, 0:S])
                last.then_inc(k_turned, 1)

            @block.tensor
            def _(pe):
                for n in range(NB):
                    for h in range(2):
                        if n:
                            pe.wait_ge(k_taken, 2 * n)
                        for k in range(KC):
                            last = pe.matmul(k_ps[0:S, h, :], ctxT[:, k, n * S:(n + 1) * S],
                                             wk[:, k, h * 512:(h + 1) * 512], start=(k == 0), stop=(k == KC - 1))
                        last.then_inc(k_done, 1)
                    for h in range(2):
                        if n:
                            pe.wait_ge(v_taken, 2 * n - 1 + h)
                        for k in range(KC):
                            last = pe.matmul(v_ps[0:S, h, :], ctxT[:, k, n * S:(n + 1) * S],
                                             wv[:, k, h * 512:(h + 1) * 512], start=(k == 0), stop=(k == KC - 1))
                        last.then_inc(v_done, 1)
                    if n:
                        turn_keys(pe, n - 1)
                pe.wait_ge(b_in, 16 * 8)
                for k in range(KC):
                    last = pe.transpose(gate_ps[:, k * E:(k + 1) * E], gate_rows[:, k * P:(k + 1) * P], ident[0:E, 0:E])
                last.then_inc(gate_turned, 1)
                turn_keys(pe, NB - 1)

            @block.scalar
            def _(act):
                act.wait_ge(pads, 3)
                for n in range(NB):
                    for h in range(2):
                        act.wait_ge(k_done, 2 * n + h + 1)
                        if n >= 2:
                            act.wait_ge(k_turned, n - 1)
                        ps = k_ps[0:S, h, :].rearrange("s (h d) -> s h d", d=HD)
                        act.activation(k_sq[:, n % 2, 8 * h:8 * h + 8, :], ps, ACT.Square).then_inc(k_squared, 1)
                        act.copy(k_sb[:, n % 2, 8 * h:8 * h + 8, :], ps).then_inc(k_taken, 1)
                    for h in range(2):
                        act.wait_ge(v_done, 2 * n + h + 1)
                        act.copy(v_sb[:, n, 8 * h:8 * h + 8, 0:HD],
                                 v_ps[0:S, h, :].rearrange("s (h d) -> s h d", d=HD)).then_inc(v_taken, 1)
                act.wait_ge(gate_turned, 1)
                act.copy(gate_sb[:, :, :].rearrange("p k e -> p (k e)"), gate_ps[:, 0:KC * E])

            @block.vector
            def _(dve):
                chain = Chain(dve, setup_chain)
                link = chain.link

                def per_head(a):
                    return a.rearrange("s (h a) -> s h a", a=1).to_broadcast([S, HEADS, HD])

                def place_keys(n):
                    dve.wait_ge(k_turned, n + 1)
                    dve.wait_ge(pads, 1)
                    for h in range(PAIR):
                        for b in range(2):
                            dve.tensor_copy(k_pairs[h * HD:(h + 1) * HD, n, 4 * b:4 * b + 4, h * S:(h + 1) * S],
                                            kT4[h * HD:(h + 1) * HD, b, :, 0:S]).then_inc(k_placed, 1)

                for n in range(NB):
                    keys = k_sb[:, n % 2, :, :]
                    dve.wait_ge(k_squared, 2 * n + 2)
                    link(dve.tensor_reduce(var[:], k_sq[:, n % 2, :, :], AX.X, ALU.add))
                    link(dve.tensor_scalar(var[:], var[:], 1.0 / HD, EPS, ALU.mult, ALU.add))
                    rsqrt(dve, chain, rstd[:], var[:], tmp[:])
                    dve.wait_ge(k_taken, 2 * n + 2)
                    dve.tensor_tensor(keys, keys, per_head(rstd[:]), ALU.mult).then_inc(k_scaled, 1)
                    if n:
                        place_keys(n - 1)
                place_keys(NB - 1)

        with ExitStack() as c2:
            def sb3(name, shape, dt=F32):
                return c2.enter_context(nc.sbuf_tensor("a1m_" + name, shape, dt))

            def sem3(name):
                return c2.enter_context(nc.semaphore("a1m_" + name))

            YR = 4
            index = sb3("index", [P, YR, K0], I32)
            yg = sb3("yg", [P, YR, K0, D])
            stats, mv, tmp2, var2 = sb3("stats", [P, 2, 6]), sb3("mv", [P, 2, 2]), sb3("tmp2", [P, 2]), sb3("var2", [P, 2])
            VN = 2 + HEADS
            var, rstd, tmp = sb3("var", [P, VN]), sb3("rstd", [P, VN]), sb3("tmp", [P, VN])
            xn, xn2 = sb3("xn", [P, 2, D]), sb3("xn2", [P, 2, D])
            xT, x2T = sb3("xT", [P, KC * P]), sb3("x2T", [P, 2, KC * P])
            q_sb, q_sq = sb3("q", [P, 2, INNER]), sb3("q_sq", [P, 2, INNER])
            qn = sb3("qn", [P, 2, INNER])
            qT = sb3("qT", [P, G, P])
            s_sb, e_sb = sb3("s", [P, ROWS]), sb3("e", [P, 2, JT * P])
            mx, rsum = sb3("mx", [P, HEADS]), sb3("rsum", [P, HEADS])
            eT = sb3("eT", [P, JT, P])
            o_sb = sb3("o", [P, 2, INNER])
            oT = sb3("oT", [P, IC, P])
            y_sb = sb3("y", [P, 2, D])
            work = c2.enter_context(nc.psum_tensor("a1_work", [P, 2, 512], F32))
            s_ps = c2.enter_context(nc.psum_tensor("a1_s_ps", [P, SB, 512], F32))
            o_ps = c2.enter_context(nc.psum_tensor("a1_o_ps", [P, OB, 512], F32))
            z_ps = o_ps[:, OB - 1, 512 - E:512]
            index_ready, combined, var_ready, xn_ready, qn_ready, xn2_ready = (
                sem3(s) for s in ("index_ready", "combined", "var_ready", "xn_ready", "qn_ready", "xn2_ready"))
            s_done, max_ready, s_taken, e_ready, o_done, sums_ready, o_taken = (
                sem3(s) for s in ("s_done", "max_ready", "s_taken", "e_ready", "o_done", "sums_ready", "o_taken"))
            z_done, z_taken, bo_added, x_added, x_out, sq_ready, e_pads = (
                sem3(s) for s in ("z_done", "z_taken", "bo_added", "x_added", "x_out", "sq_ready", "e_pads"))
            passed_dve, passed_pool = sem3("passed_dve"), sem3("passed_pool")
            gathered = [sem3(f"gathered{b}") for b in range(YR)]
            xn2_out = [sem3(f"xn2_out{b}") for b in range(2)]
            ORDER = [("xT", 0, 3), ("qT", 0, 1), ("qT", 1, 1), ("q", 0, 3), ("eT", 0, 0), ("eT", 1, 0),
                     ("q", 1, 3), ("eT", 2, 0), ("oT", 0, -1), ("oT", 1, -1), ("x2", 0, -4), ("y", 0, -1)]
            per = {kind: u + 1 for kind, u, _ in sorted(ORDER)}
            place = {(kind, u): i for i, (kind, u, _) in enumerate(ORDER)}
            assert len(ORDER) % 2 == 0 and per["eT"] == -(-JT // 4) and per["oT"] == IC // 4
            full = {kind: sem3("full_" + kind) for kind in per}
            freed = {kind: sem3("freed_" + kind) for kind in per}
            block = c2.enter_context(nc.Block())
            AHEAD, BEHIND = 5, 5

            def has(n, k):
                return not isinstance(n, int) or 0 <= TB * n + k < NT

            def wait(eng, sem, n, k, times=1, add=1):
                value = times * (TB * n + k) + add
                if not isinstance(n, int) or value > 0:
                    eng.wait_ge(sem, value)

            def bank_of(kind, u):
                return place[kind, u] % 2

            def take(n, k, kind, u):
                slot, i = k, place[kind, u] - 2
                while slot > k - 12:
                    if i < 0:
                        i, slot = i + len(ORDER), slot - 1
                    kind2, u2, dist2 = ORDER[i]
                    if has(n, slot + dist2):
                        wait(nc.tensor, freed[kind2], n, slot + dist2, per[kind2], u2 + 1)
                        break
                    i -= 2
                return work[:, bank_of(kind, u), :]

            def program(eng, slot, chain=None, per_row=0):
                for k in range(TB - AHEAD, TB):
                    slot(-1, k)
                for k in range(TB):
                    slot(0, k)
                with eng.Fori(1, NB - 1) as n:
                    if chain:
                        chain.enter(n - 1, per_row)
                    for k in range(TB):
                        slot(n, k)
                if chain:
                    chain.leave(NB - 2)
                for k in range(TB):
                    slot(NB - 1, k)
                for k in range(BEHIND):
                    slot(NB, k)

            @block.gpsimd
            def _(pool):
                def copy_index(n, k):
                    for j in range(K0):
                        pool.tensor_copy(index[:, k % YR, j:j + 1], r0.slot[j][:, bass.ds(TB * n + k, 1)]
                                         ).then_inc(index_ready, 1)

                def slot(n, k):
                    if has(n, k + AHEAD):
                        t = k + AHEAD
                        if isinstance(n, int) and TB * n + t == 0:
                            copy_index(0, 0)
                        wait(pool, combined, n, t - YR)
                        wait(pool, index_ready, n, t, K0, K0)
                        alone(pool, passed_pool)
                        for j in range(K0):
                            pool.indirect_dma_start(yg[:, t % YR, j, :], None, y0_dram,
                                                    bass.IndirectOffsetOnAxis(ap=index[:, t % YR, j:j + 1], axis=0)
                                                    ).then_inc(gathered[t % YR], 16)
                        if has(n, t + 1):
                            wait(pool, combined, n, t + 1 - YR)
                            alone(pool, passed_pool)
                            copy_index(n, t + 1)
                    if has(n, k - 1):
                        t = k - 1
                        wait(pool, freed["y"], n, t)
                        pool.tensor_tensor(y_sb[:, t % 2, :], y_sb[:, t % 2, :], bo_b[:], ALU.add).then_inc(bo_added, 1)
                        wait(pool, bo_added, n, t)
                        alone(pool, passed_pool)
                        pool.tensor_tensor(x_sb[:, TB * n + t, :], x_sb[:, TB * n + t, :], y_sb[:, t % 2, :], ALU.add
                                           ).then_inc(x_added, 1)

                program(pool, slot)

            @block.sync
            def _(sp):
                xm_rows = xm_dram.rearrange("(t p) (a d) -> t a p d", p=P, a=2)
                out_rows = out.rearrange("n (k p) d -> (n k) p d", p=P)

                def slot(n, k):
                    if has(n, k - 3):
                        t = sp.snap(TB * n + k - 3) if not isinstance(n, int) else TB * n + k - 3
                        wait(sp, xn2_ready, n, k - 3)
                        sp.dma_start(xm_rows[t, 0], xn2[:, (k - 3) % 2, :]).then_inc(xn2_out[(k - 3) % 2], 16)
                        sp.dma_start(xm_rows[t, 1], x_sb[:, t, :]).then_inc(x_out, 16)
                        sp.dma_start(out_rows[t], x_sb[:, t, :]).then_inc(x_out, 16)

                program(sp, slot)
                sp.wait_ge(x_out, 32 * NT)
                for b in range(2):
                    sp.wait_ge(xn2_out[b], 16 * (NT // 2))

            @block.tensor
            def _(pe):
                def turn(n, k, kind, u, rows, count):
                    bank = take(n, k, kind, u)
                    for j in range(count):
                        last = pe.transpose(bank[:, j * P:(j + 1) * P],
                                            rows[:, (4 * u + j) * P:(4 * u + j + 1) * P], ident[:])
                    last.then_inc(full[kind], 1)

                def turn_x(n, k, t):
                    wait(pe, xn_ready, n, t)
                    turn(n, k, "xT", 0, xn[:, t % 2, :], KC)

                def turn_q(n, k, t, u):
                    wait(pe, qn_ready, n, t)
                    turn(n, k, "qT", u, qn[:, t % 2, :], 4)

                def project_q(n, k, t, u):
                    wait(pe, freed["xT"], n, t)
                    bank = take(n, k, "q", u)
                    for j in range(KC):
                        last = pe.matmul(bank, xT[:, j * P:(j + 1) * P], wq[:, j, u * 512:(u + 1) * 512],
                                         start=(j == 0), stop=(j == KC - 1))
                    last.then_inc(full["q"], 1)

                def scores(n, k, t):
                    wait(pe, freed["qT"], n, t, 2, 2)
                    wait(pe, s_taken, n, t - 1)
                    for g in range(G):
                        last = pe.matmul(s_ps[:, g // 3, (g % 3) * WC:(g % 3 + 1) * WC], qT[:, g, :],
                                         k_pairs[:, n + t // TB, g, :], start=True, stop=True)
                    last.then_inc(s_done, 1)

                def turn_e(n, k, t, u):
                    wait(pe, e_ready, n, t)
                    turn(n, k, "eT", u, e_sb[:, t % 2, :], min(4, JT - 4 * u))

                def values(n, k, t):
                    wait(pe, freed["eT"], n, t, per["eT"], per["eT"])
                    wait(pe, o_taken, n, t - 1)
                    wait(pe, z_taken, n, t - 5)
                    opened = set()
                    for j in range(JT):
                        h = first_head[j]
                        while h <= last_head[j]:
                            b = h // OH
                            h1 = min(last_head[j], b * OH + OH - 1)
                            at = v_at[j] + (h - first_head[j]) * VW
                            last = pe.matmul(o_ps[:, b, (h - b * OH) * VW:(h1 - b * OH + 1) * VW], eT[:, j, :],
                                             v_rows[:, n, at:at + (h1 - h + 1) * VW], start=b not in opened,
                                             stop=True, skip_group_check=True)
                            opened.add(b)
                            h = h1 + 1
                    last.then_inc(o_done, 1)

                def turn_o(n, k, t, u):
                    wait(pe, o_taken, n, t)
                    turn(n, k, "oT", u, o_sb[:, t % 2, :], 4)

                def output(n, k, t):
                    wait(pe, freed["oT"], n, t, per["oT"], per["oT"])
                    bank = take(n, k, "y", 0)
                    for j in range(IC):
                        last = pe.matmul(bank[:, 0:D], oT[:, j, :], wo[:, j, :], start=(j == 0), stop=(j == IC - 1))
                    last.then_inc(full["y"], 1)

                def turn_x2(n, k, t):
                    wait(pe, xn2_ready, n, t)
                    turn(n, k, "x2", 0, xn2[:, t % 2, :], KC)

                def logits(n, k, t):
                    wait(pe, freed["x2"], n, t)
                    if has(n, k - 1):
                        wait(pe, o_taken, n, k - 1)
                    wait(pe, z_taken, n, t - 1)
                    for j in range(KC):
                        last = pe.matmul(z_ps, x2T[:, t % 2, j * P:(j + 1) * P], gate_sb[:, j, :],
                                         start=(j == 0), stop=(j == KC - 1))
                    last.then_inc(z_done, 1)

                def slot(n, k):
                    if has(n, k + 3):
                        turn_x(n, k, k + 3)
                    if has(n, k + 1):
                        turn_q(n, k, k + 1, 0)
                        turn_q(n, k, k + 1, 1)
                    if has(n, k + 3):
                        project_q(n, k, k + 3, 0)
                    if has(n, k):
                        turn_e(n, k, k, 0)
                        turn_e(n, k, k, 1)
                    if has(n, k + 3):
                        project_q(n, k, k + 3, 1)
                    if has(n, k + 1):
                        scores(n, k, k + 1)
                    if has(n, k):
                        turn_e(n, k, k, 2)
                    if has(n, k - 1):
                        turn_o(n, k, k - 1, 0)
                    if has(n, k - 5):
                        logits(n, k, k - 5)
                    if has(n, k - 1):
                        turn_o(n, k, k - 1, 1)
                    if has(n, k - 4):
                        turn_x2(n, k, k - 4)
                    if has(n, k):
                        values(n, k, k)
                    if has(n, k - 1):
                        output(n, k, k - 1)

                program(pe, slot)

            @block.scalar
            def _(act):
                def take_x(n, t):
                    wait(act, full["xT"], n, t)
                    act.copy(xT[:], work[:, bank_of("xT", 0), 0:KC * P]).then_inc(freed["xT"], 1)

                def take_qT(n, t, u):
                    wait(act, full["qT"], n, t, 2, u + 1)
                    act.activation(qT[:, 4 * u:4 * u + 4, :].rearrange("p g q -> p (g q)"),
                                   work[:, bank_of("qT", u), :], ACT.Identity, bias=betaq2[:, 0:1],
                                   scale=gq2[:, 0:1]).then_inc(freed["qT"], 1)

                def take_q(n, t, u):
                    wait(act, full["q"], n, t, 2, u + 1)
                    wait(act, qn_ready, n, t - 2)
                    act.copy(q_sb[:, t % 2, u * 512:(u + 1) * 512], work[:, bank_of("q", u), :]).then_inc(freed["q"], 1)

                def squares(n, t):
                    wait(act, freed["q"], n, t, 2, 2)
                    act.activation(q_sq[:, t % 2, :], q_sb[:, t % 2, :], ACT.Square).then_inc(sq_ready, 1)

                def take_rows(n, t, kind, u, dst, count):
                    wait(act, full[kind], n, t, per[kind], u + 1)
                    act.copy(dst[:, 4 * u:4 * u + count, :].rearrange("p j q -> p (j q)"),
                             work[:, bank_of(kind, u), 0:count * P]).then_inc(freed[kind], 1)

                def take_y(n, t):
                    wait(act, full["y"], n, t)
                    wait(act, x_added, n, t - 2)
                    act.copy(y_sb[:, t % 2, :], work[:, bank_of("y", 0), 0:D]).then_inc(freed["y"], 1)

                def take_x2(n, t):
                    wait(act, full["x2"], n, t)
                    act.copy(x2T[:, t % 2, :], work[:, bank_of("x2", 0), 0:KC * P]).then_inc(freed["x2"], 1)

                def exponentials(n, t):
                    wait(act, s_taken, n, t)
                    if isinstance(n, int) and TB * n + t == 0:
                        act.wait_ge(e_pads, 1)
                    act.activation(e_sb[:, t % 2, 0:ROWS], s_sb[:], ACT.Exp, scale=SCALE).then_inc(e_ready, 1)

                def slot(n, k):
                    if has(n, k + 3):
                        take_x(n, k + 3)
                    if has(n, k + 1):
                        take_qT(n, k + 1, 0)
                        take_qT(n, k + 1, 1)
                    if has(n, k + 3):
                        take_q(n, k + 3, 0)
                    if has(n, k):
                        take_rows(n, k, "eT", 0, eT, min(4, JT - 0))
                        take_rows(n, k, "eT", 1, eT, min(4, JT - 4))
                    if has(n, k + 3):
                        take_q(n, k + 3, 1)
                        squares(n, k + 3)
                    if has(n, k):
                        take_rows(n, k, "eT", 2, eT, min(4, JT - 8))
                    if has(n, k - 1):
                        take_rows(n, k - 1, "oT", 0, oT, 4)
                        take_rows(n, k - 1, "oT", 1, oT, 4)
                    if has(n, k - 4):
                        take_x2(n, k - 4)
                    if has(n, k + 1):
                        exponentials(n, k + 1)
                    if has(n, k - 1):
                        take_y(n, k - 1)

                program(act, slot)

            @block.vector
            def _(dve):
                chain = Chain(dve, dve_chain)
                dve.memset(e_sb[:, :, ROWS:JT * P], 0.0).then_inc(e_pads, 1)
                dve.memset(stats[:], 0.0)
                chain.link(dve.memset(var[:], 1.0))
                s_parts = [(0, 6 * (SB - 1), 6), (6 * (SB - 1), HEADS, HEADS - 6 * (SB - 1))]
                o_parts = [(0, OH * (OB - 1), OH), (OH * (OB - 1), HEADS, HEADS - OH * (OB - 1))]

                def scores(part):
                    h0, h1, nh = part
                    b0 = h0 // 6
                    return s_ps[:, b0:b0 + (h1 - h0) // nh, 0:nh * S].rearrange("p b (h s) -> p b h s", s=S)

                def outputs(part):
                    h0, h1, nh = part
                    b0 = h0 // OH
                    return o_ps[:, b0:b0 + (h1 - h0) // nh, 0:nh * VW].rearrange("p b (h v) -> p b h v", v=VW)

                def slot(n, k):
                    enters, leaves, queries = has(n, k + 4), has(n, k - 3), has(n, k + 2)
                    if enters:
                        t = k + 4
                        for j in range(K0):
                            if j == 0:
                                dve.wait_ge(gathered[t % YR], 16 * K0 * ((TB // YR) * n + t // YR + 1))
                            ins = dve.scalar_tensor_tensor(x_sb[:, TB * n + t, :], yg[:, t % YR, j, :],
                                                           r0.gates[j][:, bass.ds(TB * n + t, 1)], x_sb[:, TB * n + t, :],
                                                           ALU.mult, ALU.add)
                            if j + 1 < K0:
                                chain.link(ins)
                            else:
                                ins.then_inc(combined, 1)
                                wait(dve, combined, n, t)
                                alone(dve, passed_dve)
                        chain.step(dve.bn_stats(stats[:, 0, :], x_sb[:, TB * n + t, :]))
                    if leaves:
                        wait(dve, x_added, n, k - 3)
                        alone(dve, passed_dve)
                        chain.step(dve.bn_stats(stats[:, 1, :], x_sb[:, TB * n + k - 3, :]))
                    if enters or leaves:
                        dve.wait_ge(chain.sem, chain.base + chain.n)
                        m0, v0, m1, v1 = (stats[:, :, c] for c in (1, 2, 4, 5))
                        chain.step(dve.tensor_tensor(mv[:, :, 0], m0, m1, ALU.add))
                        chain.step(dve.tensor_tensor(mv[:, :, 1], v0, v1, ALU.add))
                        chain.link(dve.tensor_tensor(tmp2[:], m0, m1, ALU.subtract))
                        chain.step(dve.tensor_tensor(var2[:], tmp2[:], tmp2[:], ALU.mult))
                        chain.step(dve.tensor_scalar(mv[:, :, 0], mv[:, :, 0], 0.5, None, ALU.mult))
                        chain.link(dve.tensor_scalar(mv[:, :, 1], mv[:, :, 1], 1.0 / D, EPS, ALU.mult, ALU.add))
                        chain.step(dve.scalar_tensor_tensor(var[:, 0:2], var2[:], 0.25, mv[:, :, 1], ALU.mult, ALU.add))
                    if queries:
                        wait(dve, sq_ready, n, k + 2)
                        chain.link(dve.tensor_reduce(var[:, 2:VN], q_sq[:, k % 2, :].rearrange("p (h d) -> p h d", d=HD),
                                                     AX.X, ALU.add))
                        chain.step(dve.tensor_scalar(var[:, 2:VN], var[:, 2:VN], 1.0 / HD, EPS, ALU.mult, ALU.add))
                    if enters or leaves or queries:
                        dve.wait_ge(chain.sem, chain.base + chain.n)
                        rsqrt(dve, chain, rstd[:], var[:], tmp[:])
                    if enters:
                        t = k + 4
                        wait(dve, full["xT"], n, t - 2)
                        dve.tensor_scalar(xn[:, t % 2, :], x_sb[:, TB * n + t, :], mv[:, 0, 0:1], rstd[:, 0:1],
                                          ALU.subtract, ALU.mult).then_inc(xn_ready, 1)
                    if queries:
                        t = k + 2
                        wait(dve, freed["q"], n, t, 2, 2)
                        wait(dve, full["qT"], n, t - 2, 2, 2)
                        dve.tensor_tensor(qn[:, t % 2, :].rearrange("p (h d) -> p h d", d=HD),
                                          q_sb[:, t % 2, :].rearrange("p (h d) -> p h d", d=HD),
                                          rstd[:, 2:VN].rearrange("p (h a) -> p h a", a=1).to_broadcast([P, HEADS, HD]),
                                          ALU.mult).then_inc(qn_ready, 1)
                    if leaves:
                        t = k - 3
                        rounds = (TB // 2) * n + (t - 2) // 2 + 1
                        if not isinstance(n, int) or rounds > 0:
                            dve.wait_ge(xn2_out[t % 2], 16 * rounds)
                        wait(dve, full["x2"], n, t - 2)
                        dve.tensor_scalar(xn2[:, t % 2, :], x_sb[:, TB * n + t, :], mv[:, 1, 0:1], rstd[:, 1:2],
                                          ALU.subtract, ALU.mult).then_inc(xn2_ready, 1)
                    if has(n, k - 5):
                        t = k - 5
                        wait(dve, z_done, n, t)
                        dve.tensor_scalar(z_all[:, TB * n + t, :], z_ps, 1.0, None, ALU.mult).then_inc(z_taken, 1)
                    if has(n, k + 1):
                        t = k + 1
                        wait(dve, s_done, n, t)
                        chain.step(dve.tensor_reduce(mx[:, 0:s_parts[0][1]].rearrange("p (b h) -> p b h", h=6),
                                                     scores(s_parts[0]), AX.X, ALU.max))
                        dve.tensor_reduce(mx[:, s_parts[1][0]:HEADS].rearrange("p (b h) -> p b h", b=1),
                                          scores(s_parts[1]), AX.X, ALU.max).then_inc(max_ready, 1)
                        wait(dve, max_ready, n, t)
                        wait(dve, e_ready, n, t - 1)
                        for part in s_parts:
                            h0, h1, nh = part
                            nb = (h1 - h0) // nh
                            ins = dve.tensor_tensor(
                                s_sb[:, h0 * S:h1 * S].rearrange("p (b h s) -> p b h s", h=nh, s=S), scores(part),
                                mx[:, h0:h1].rearrange("p (b h a) -> p b h a", h=nh, a=1).to_broadcast([P, nb, nh, S]),
                                ALU.subtract)
                            if h0 == 0:
                                chain.step(ins)
                            else:
                                ins.then_inc(s_taken, 1)
                    if has(n, k):
                        wait(dve, o_done, n, k)
                        for part in o_parts:
                            h0, h1, nh = part
                            ins = dve.reciprocal(rsum[:, h0:h1].rearrange("p (b h) -> p b h", h=nh),
                                                 outputs(part)[:, :, :, HD])
                            if h0 == 0:
                                chain.step(ins)
                            else:
                                ins.then_inc(sums_ready, 1)
                        wait(dve, sums_ready, n, k)
                        wait(dve, full["oT"], n, k - 2, per["oT"], per["oT"])
                        for part in o_parts:
                            h0, h1, nh = part
                            nb = (h1 - h0) // nh
                            ins = dve.tensor_tensor(
                                o_sb[:, k % 2, h0 * HD:h1 * HD].rearrange("p (b h d) -> p b h d", h=nh, d=HD),
                                outputs(part)[:, :, :, 0:HD],
                                rsum[:, h0:h1].rearrange("p (b h a) -> p b h a", h=nh, a=1).to_broadcast([P, nb, nh, HD]),
                                ALU.mult)
                            if h0 == 0:
                                chain.step(ins)
                            else:
                                ins.then_inc(o_taken, 1)

                SLOT = (K0 - 1) + 2 + 7 + 2 + RSQRT_STEPS + 1 + 1 + 1 + 1
                program(dve, slot, chain, TB * SLOT)


def experts_1_weights(nc, keep, E, D, H, KC):
    w = Weights()
    HC = H // P

    def kept(name, shape):
        return keep.enter_context(nc.sbuf_tensor("e1_" + name, shape, F32))

    w.w1, w.w2 = kept("w1", [P, 2, KC, H]), kept("w2", [P, 2, HC, D])
    w.b1_rows, w.b2_b = kept("b1_rows", [E * HC, P]), kept("b2_b", [P, E, D])
    w.b_in = keep.enter_context(nc.semaphore("e1_b_in"))
    w.w_in = [keep.enter_context(nc.semaphore(f"e1_w_in{b}")) for b in range(2)]
    return w


def load_expert_1(sp, w, W1, W2, e, b):
    sp.dma_start(w.w1[:, b, :, :], W1.rearrange("e (k p) h -> e p k h", p=P)[e]).then_inc(w.w_in[b], 16)
    sp.dma_start(w.w2[:, b, :, :], W2.rearrange("e (j p) d -> e p j d", p=P)[e]).then_inc(w.w_in[b], 16)


def load_experts_1(sp, w, W1, b1, W2, b2, E, D, H, KC):
    sp.dma_start(w.b1_rows[:], b1.rearrange("e (j p) -> (e j) p", p=P)).then_inc(w.b_in, 16)
    for b in range(2):
        load_expert_1(sp, w, W1, W2, b, b)
    sp.dma_start(w.b2_b[:, :, :].rearrange("p e h -> p (e h)"),
                 b2.rearrange("(a e) h -> a (e h)", a=1).to_broadcast([P, E * D])).then_inc(w.b_in, 16)


def experts_1(nc, xm_dram, out, ident, r, w, W1, W2, E, D, H, KC, CT):
    HC = H // P
    CAP = CT * P
    HALVES = [(0, CAP // 2), (CAP // 2, CAP)]
    PASSES = E // 2
    HU = 2 * HC
    with ExitStack() as c:
        def sb(name, shape, dt=F32):
            return c.enter_context(nc.sbuf_tensor("e1_" + name, shape, dt))

        def sem(name):
            return c.enter_context(nc.semaphore("e1_" + name))

        w1, w2, b1_rows, b2_b = w.w1, w.w2, w.b1_rows, w.b2_b
        b1T, b1_now = sb("b1T", [P, E, HC]), sb("b1_now", [P, 2, HC])
        source, target = sb("source", [P, 2, CT], I32), sb("target", [P, 2, CT], I32)
        xg = sb("xg", [P, 2, CT, 2 * D])
        x_kept = sb("x_kept", [P, 2, CT, D])
        xT = sb("xT", [P, KC, CAP])
        hT = sb("hT", [P, HC, CAP])
        biased = sb("biased", [P, 2, D])
        y_sb = sb("y", [P, 2, CT, D])
        b1_turned, b1_ready = sem("b1_turned"), sem("b1_ready")
        source_ready, target_ready, passed_pool = sem("source_ready"), sem("target_ready"), sem("passed_pool")
        b1_copied, kept = sem("b1_copied"), sem("kept")
        w_in = w.w_in
        gathered = [sem(f"gathered{b}") for b in range(2)]
        scattered = [sem(f"scattered{b}") for b in range(2)]
        x_turned, xT_ready, h_done, h_ready, y_done, y_taken, y_ready = (
            sem(s) for s in ("x_turned", "xT_ready", "h_done", "h_ready", "y_done", "y_taken", "y_ready"))
        x_ps = c.enter_context(nc.psum_tensor("e1_x_ps", [P, 2, 512], F32))
        h_ps = c.enter_context(nc.psum_tensor("e1_h_ps", [P, 4, 512], F32))
        y_ps = c.enter_context(nc.psum_tensor("e1_y_ps", [P, 2, 512], F32))
        block = c.enter_context(nc.Block())

        def experts(eng, one):
            for b in range(2):
                one(0, b)
            with eng.Fori(1, PASSES) as i:
                for b in range(2):
                    one(i, b)

        def later(i):
            return not isinstance(i, int) or i > 0

        @block.sync
        def _(sp):
            with sp.Fori(1, PASSES) as i:
                for b in range(2):
                    e = sp.snap(2 * i + b)
                    sp.wait_ge(y_done, CT * (2 * i + b - 1))
                    load_expert_1(sp, w, W1, W2, e, b)

        @block.gpsimd
        def _(pool):
            out_rows = out.rearrange("n l d -> (n l) d")

            def gather(i, b):
                e = 2 * i + b
                if later(i):
                    pool.wait_ge(gathered[b], 16 * CT * i)
                    pool.wait_ge(x_turned, CT * (2 * i + b - 1))
                    pool.wait_ge(kept, CT * (2 * i + b - 1))
                    alone(pool, passed_pool)
                pool.tensor_copy(source[:, b, :], r.token[:, bass.ds(CT * e, CT)]).then_inc(source_ready, 1)
                pool.wait_ge(source_ready, e + 1)
                alone(pool, passed_pool)
                for t in range(CT):
                    pool.indirect_dma_start(xg[:, b, t, :], None, xm_dram,
                                            bass.IndirectOffsetOnAxis(ap=source[:, b, t:t + 1], axis=0)
                                            ).then_inc(gathered[b], 16)

            def scatter(i, b, first):
                e = 2 * i + b
                if not first:
                    pool.wait_ge(scattered[b], 16 * CT * i)
                    alone(pool, passed_pool)
                pool.tensor_copy(target[:, b, :], r.target[:, bass.ds(CT * e, CT)]).then_inc(target_ready, 1)
                pool.wait_ge(target_ready, e + 1)
                for t in range(CT):
                    pool.wait_ge(y_ready, CT * e + t + 1)
                    alone(pool, passed_pool)
                    pool.indirect_dma_start(out_rows, bass.IndirectOffsetOnAxis(ap=target[:, b, t:t + 1], axis=0),
                                            y_sb[:, b, t, :], None, bounds_check=out_rows.shape[0] - 1,
                                            oob_is_err=False).then_inc(scattered[b], 16)

            for b in range(2):
                gather(0, b)
            for b in range(2):
                gather(1, b)
                scatter(0, b, True)
            with pool.Fori(2, PASSES) as i:
                for b in range(2):
                    gather(i, b)
                    scatter(i - 1, b, False)
            for b in range(2):
                scatter(PASSES - 1, b, False)
            for b in range(2):
                pool.wait_ge(scattered[b], 16 * CT * PASSES)

        @block.tensor
        def _(pe):
            pe.wait_ge(w.b_in, 32)
            pe.transpose(x_ps[:, 0, 0:E * HC], b1_rows[:], ident[0:E * HC, 0:E * HC]).then_inc(b1_turned, 1)
            pe.wait_ge(b1_ready, 1)

            def one(i, b):
                e = 2 * i + b
                for t in range(CT):
                    if later(i) or b or t >= 2:
                        pe.wait_ge(xT_ready, CT * e + max(t - 1, 0))
                    pe.wait_ge(gathered[b], 16 * (CT * i + CT))
                    for k in range(KC):
                        last = pe.transpose(x_ps[:, t % 2, k * P:(k + 1) * P], xg[:, b, t, k * P:(k + 1) * P], ident[:])
                    last.then_inc(x_turned, 1)
                pe.wait_ge(xT_ready, CT * e + CT)
                pe.wait_ge(w_in[b], 32 * i + 32)
                for u in range(HU):
                    j, s = divmod(u, 2)
                    if u >= 4:
                        pe.wait_ge(h_ready, HU * e + u - 3)
                    c0, c1 = HALVES[s]
                    for k in range(KC):
                        last = pe.matmul(h_ps[:, u % 4, 0:c1 - c0], w1[:, b, k, j * P:(j + 1) * P], xT[:, k, c0:c1],
                                         start=(k == 0), stop=(k == KC - 1))
                    last.then_inc(h_done, 1)
                pe.wait_ge(h_ready, HU * e + HU)
                for t in range(CT):
                    if later(i) or b or t >= 2:
                        pe.wait_ge(y_taken, CT * e + max(t - 1, 0))
                    for j in range(HC):
                        last = pe.matmul(y_ps[:, t % 2, 0:D], hT[:, j, t * P:(t + 1) * P], w2[:, b, j, :],
                                         start=(j == 0), stop=(j == HC - 1))
                    last.then_inc(y_done, 1)

            experts(pe, one)

        @block.scalar
        def _(act):
            act.wait_ge(b1_turned, 1)
            act.copy(b1T[:, :, :].rearrange("p e j -> p (e j)"), x_ps[:, 0, 0:E * HC]).then_inc(b1_ready, 1)
            act.wait_ge(b1_ready, 1)

            def one(i, b):
                e = 2 * i + b
                act.copy(b1_now[:, b, :], b1T[:, e, :]).then_inc(b1_copied, 1)
                for t in range(CT):
                    act.wait_ge(x_turned, CT * e + t + 1)
                    act.copy(xT[:, :, t * P:(t + 1) * P],
                             x_ps[:, t % 2, 0:KC * P].rearrange("p (k q) -> p k q", k=KC)).then_inc(xT_ready, 1)
                act.wait_ge(b1_copied, e + 1)
                for u in range(HU):
                    j, s = divmod(u, 2)
                    c0, c1 = HALVES[s]
                    act.wait_ge(h_done, HU * e + u + 1)
                    act.activation(hT[:, j, c0:c1], h_ps[:, u % 4, 0:c1 - c0], ACT.Relu,
                                   bias=b1_now[:, b, j:j + 1]).then_inc(h_ready, 1)

            experts(act, one)

        @block.vector
        def _(dve):
            dve.wait_ge(w.b_in, 32)

            def one(i, b):
                e = 2 * i + b
                dve.wait_ge(gathered[b], 16 * (CT * i + CT))
                if later(i):
                    dve.wait_ge(y_ready, CT * (2 * i + b - 1))
                dve.tensor_copy(x_kept[:, b, :, :], xg[:, b, :, D:2 * D]).then_inc(kept, CT)
                for t in range(CT):
                    dve.wait_ge(y_done, CT * e + t + 1)
                    dve.tensor_tensor(biased[:, (CT * b + t) % 2, :], y_ps[:, t % 2, 0:D], b2_b[:, e, :], ALU.add
                                      ).then_inc(y_taken, 1)
                    dve.wait_ge(y_taken, CT * e + t + 1)
                    if t == 0:
                        dve.wait_ge(kept, CT * (2 * i + b + 1))
                        if later(i):
                            dve.wait_ge(scattered[b], 16 * CT * i)
                    dve.scalar_tensor_tensor(y_sb[:, b, t, :], biased[:, (CT * b + t) % 2, :],
                                             r.slot_gate[:, bass.ds(CT * e + t, 1)], x_kept[:, b, t, :],
                                             ALU.mult, ALU.add).then_inc(y_ready, 1)

            experts(dve, one)


_INS = ['x', 'ctx_1024', 'L0_xattn_Wq', 'L0_xattn_bq', 'L0_xattn_Wk', 'L0_xattn_bk', 'L0_xattn_Wv', 'L0_xattn_bv',
        'L0_xattn_Wo', 'L0_xattn_bo', 'L0_ffn_gate', 'L0_ffn_W1', 'L0_ffn_b1', 'L0_ffn_W2', 'L0_ffn_b2',
        'L1_xattn_Wq', 'L1_xattn_Wk', 'L1_xattn_Wv', 'L1_xattn_Wo', 'L1_xattn_bo', 'L1_xattn_q_gamma',
        'L1_xattn_q_beta', 'L1_xattn_k_gamma', 'L1_xattn_k_beta', 'L1_ffn_gate_w', 'L1_ffn_w1', 'L1_ffn_b1',
        'L1_ffn_w2', 'L1_ffn_b2']
_OUTS = [((4, 1024, 256), 'float32')]


def kernel(**inputs):
    import numpy as _np
    import concourse.bacc as _bacc
    from concourse import mybir as _mybir
    from concourse.bass_utils import run_bass_kernel_spmd as _run

    nc = _bacc.Bacc("TRN2", target_bir_lowering=False, num_devices=1)
    arrays, args = {}, []
    for name in _INS:
        a = _np.ascontiguousarray(inputs[name])
        arrays[f"in_{name}_dram"] = a
        args.append(nc.dram_tensor(f"in_{name}_dram", a.shape, _mybir.dt.from_np(a.dtype), kind="ExternalInput").ap())
    for i, (shape, dtype) in enumerate(_OUTS):
        dt = _mybir.dt.from_np(_np.dtype(dtype))
        args.append(nc.dram_tensor(f"out_{i}_dram", shape, dt, kind="ExternalOutput").ap())
    build_layers(nc, *args)
    r = _run(nc, [arrays], core_ids=[0])
    got = tuple(r.results[0][f"out_{i}_dram"] for i in range(len(_OUTS)))
    return got[0]
```

```python
from contextlib import ExitStack

import concourse.bass as bass
from concourse import mybir

F32 = mybir.dt.float32
BF16 = mybir.dt.bfloat16
F32R = mybir.dt.float32r
I32 = mybir.dt.int32
ALU = mybir.AluOpType
ACT = mybir.ActivationFunctionType
AX = mybir.AxisListType

P = 128
EPS = 1e-5
RSQRT_SEED = 0x5F3759DF
FAR = 8192.0


class Chain:

    def __init__(self, eng, sem, base=0):
        self.eng, self.sem, self.base, self.n = eng, sem, base, 0

    def step(self, ins):
        ins.then_inc(self.sem, 1)
        self.n += 1

    def link(self, ins):
        self.step(ins)
        self.eng.wait_ge(self.sem, self.base + self.n)

    def enter(self, i, per_pass):
        self.before, self.per = self.base + self.n, per_pass
        self.base, self.n = self.before + i * per_pass, 0

    def leave(self, passes):
        assert self.n == self.per, (self.n, self.per)
        self.base, self.n = self.before + passes * self.per, 0


def rsqrt(dve, chain, out, v, tmp):
    chain.link(dve.tensor_scalar(tmp.bitcast(I32), v.bitcast(I32), 1, None, ALU.logical_shift_right))
    chain.link(dve.tensor_scalar(out.bitcast(I32), tmp.bitcast(I32), -1.0, float(RSQRT_SEED), ALU.mult, ALU.add))
    for _ in range(3):
        chain.link(dve.tensor_tensor(tmp, out, out, ALU.mult))
        chain.link(dve.scalar_tensor_tensor(tmp, tmp, -0.5, v, ALU.mult, ALU.mult))
        chain.link(dve.scalar_tensor_tensor(out, tmp, 1.5, out, ALU.add, ALU.mult))


RSQRT_STEPS = 11


def moments(dve, chain, stats, mv, var, rstd, tmp, count):
    m0, q0, m1, q1 = (stats[:, :, c] for c in (1, 2, 4, 5))
    chain.step(dve.tensor_tensor(mv[:, :, 0], m0, m1, ALU.add))
    chain.step(dve.tensor_tensor(mv[:, :, 1], q0, q1, ALU.add))
    chain.link(dve.tensor_tensor(tmp, m0, m1, ALU.subtract))
    chain.step(dve.tensor_tensor(var, tmp, tmp, ALU.mult))
    chain.step(dve.tensor_scalar(mv[:, :, 0], mv[:, :, 0], 0.5, None, ALU.mult))
    chain.link(dve.tensor_scalar(mv[:, :, 1], mv[:, :, 1], 1.0 / count, EPS, ALU.mult, ALU.add))
    chain.link(dve.scalar_tensor_tensor(var, var, 0.25, mv[:, :, 1], ALU.mult, ALU.add))
    rsqrt(dve, chain, rstd, var, tmp)


MOMENTS_STEPS = 7 + RSQRT_STEPS


def build_layers(nc, x, ctx, Wq0, bq0, Wk0, bk0, Wv0, bv0, Wo0, bo0, gate0, W10, b10, W20, b20,
                 Wq1, Wk1, Wv1, Wo1, bo1, gq1, betaq1, gk1, betak1, gate1, W11, b11, W21, b21, out):
    NB, L, D = x.shape
    S = ctx.shape[1]
    T = NB * L
    NT = T // P
    TB = L // P
    KC = D // P
    E, _, H0 = W10.shape
    H1 = W11.shape[2]
    HEADS = 16
    HD0 = D // HEADS
    INNER = Wq1.shape[1]
    HD1 = INNER // HEADS
    TILES0 = 2 * T // P + E
    CAP = -(-5 * T // (4 * E))
    CT = CAP // P
    TILES1 = E * CT
    assert CAP % P == 0

    xn_dram = nc.dram_tensor("xn_scratch", (T, D), F32, kind="Internal").ap()
    y0_dram = nc.dram_tensor("y0_scratch", (TILES0 * P, D), F32, kind="Internal").ap()
    xm_dram = nc.dram_tensor("xm_scratch", (T, 2 * D), F32, kind="Internal").ap()

    top = ExitStack()
    with top:
        x_sb = top.enter_context(nc.sbuf_tensor("x_sb", [P, NT, D], F32))
        ident = top.enter_context(nc.sbuf_tensor("ident", [P, P], F32))
        ctxT = top.enter_context(nc.sbuf_tensor("ctxT", [P, KC, NB * S], F32))
        z_all = top.enter_context(nc.sbuf_tensor("z_all", [P, NT, E], F32))
        sems = RouteSemaphores()
        (sems.consts_ready, sems.pool_chain, sems.exp_ready, sems.exp_done, sems.hot_ready, sems.ranks_done,
         sems.rows_ready, sems.tokens_done, sems.dve_chain) = (
            top.enter_context(nc.semaphore("route_" + name)) for name in (
                "consts_ready", "pool_chain", "exp_ready", "exp_done", "hot_ready", "ranks_done",
                "rows_ready", "tokens_done", "dve_chain"))
        passed = top.enter_context(nc.semaphore("passed"))
        x4 = x_sb[:, :, :].rearrange("p (n k) d -> p n k d", k=TB)

        attention_0(nc, passed, x, ctx, Wq0, bq0, Wk0, bk0, Wv0, bv0, Wo0, bo0, gate0, x_sb, x4, ident, ctxT,
                    xn_dram, z_all, NB, L, D, S, TB, KC, HEADS, HD0, E)
        with ExitStack() as routes:
            a1 = attention_1_weights(nc, routes, D, KC, INNER)
            r0 = routes_of(nc, "r0", routes, 2, TILES0, None, NT)
            with ExitStack() as expert_weights:
                w0 = experts_0_weights(nc, expert_weights, E, D, H0, KC)
                route(nc, sems, "r0", r0, z_all, 2, E, TILES0, None, NT,
                      lambda sp: load_experts_0(sp, w0, W10, b10, W20, E, D, H0, KC, a1, Wk1))
                experts_0(nc, xn_dram, y0_dram, ident, r0, w0, b20, E, D, H0, KC, TILES0, a1, Wq1, Wv1, Wo1, HD1)
            attention_1(nc, passed, a1, bo1, gq1, betaq1, gk1, betak1, gate1, x_sb, ident, ctxT, y0_dram,
                        r0, z_all, xm_dram, out, NB, L, D, S, NT, KC, HEADS, HD1, INNER, E)
        with ExitStack() as routes:
            r1 = routes_of(nc, "r1", routes, 1, TILES1, CAP, NT)
            w1 = experts_1_weights(nc, routes, x_sb, E, D, H1, KC)
            route(nc, sems, "r1", r1, z_all, 1, E, TILES1, CAP, NT,
                  lambda sp: load_experts_1(sp, w1, W11, b11, W21, b21, E, D, H1, KC),
                  lambda act: split_expert_0_high(act, w1, 2 * D * H1 // P))
            experts_1(nc, passed, xm_dram, out, ident, r1, w1, W11, W21, E, D, H1, KC, CT)


def attention_0(nc, passed, x, ctx, Wq, bq, Wk, bk, Wv, bv, Wo, bo, gate, x_sb, x4, ident, ctxT,
                xn_dram, z_all, NB, L, D, S, TB, KC, HEADS, HD, E):
    HM = P // HD
    JT = -(-HM * S // P)
    PADDED = JT * P
    U = KC * JT
    TH = TB // 2
    SCALE = float(HD) ** -0.5
    with ExitStack() as c:
        def sb(name, shape, dt=F32):
            return c.enter_context(nc.sbuf_tensor("a0_" + name, shape, dt))

        def sem(name):
            return c.enter_context(nc.semaphore("a0_" + name))

        wq, wk, wv, wo = (sb(n, [P, KC, D]) for n in ("wq", "wk", "wv", "wo"))
        bqT, bkT = sb("bqT", [P, KC]), sb("bkT", [P, KC])
        bv_b, bo_b = sb("bv_b", [P, D]), sb("bo_b", [P, D])
        ctx_sb = sb("ctx", [S, NB, D])
        kT = sb("kT", [P, KC, NB, S])
        v_sb = sb("v", [S, NB, D])
        head_mask = sb("head_mask", [P, HM])
        v_blocks = sb("v_blocks", [P, NB, KC, JT, P])
        k_blocks = sb("k_blocks", [P, KC, PADDED])

        xn = sb("xn", [P, TB, D])
        stats, mv = sb("stats", [P, TB, 6]), sb("mv", [P, TB, 2])
        var, rstd, tmp = sb("var", [P, TB]), sb("rstd", [P, TB]), sb("tmp", [P, TB])
        x0_in, dve_chain, xn_ready = sem("x0_in"), sem("dve_chain"), sem("xn_ready")

        x_in, ctx_in, w_in, b_in = (sem(n) for n in ("x_in", "ctx_in", "w_in", "b_in"))
        v_moved = [sem(f"v_moved{m}") for m in range(KC)]
        ident_ready, mask_ready, pads_ready = sem("ident_ready"), sem("mask_ready"), sem("pads_ready")
        pool_chain = sem("pool_chain")
        ctxT_done, ctxT_ready = sem("ctxT_done"), sem("ctxT_ready")
        kv_done, k_ready, v_ready = sem("kv_done"), sem("k_ready"), sem("v_ready")

        pieces = []
        for h in range(HM):
            r, end = h * S, (h + 1) * S
            while r < end:
                n = min(end - r, P - r % P)
                pieces.append((h, r - h * S, n, r // P, r % P))
                r += n

        def tiles(i, h):
            return [x4[:, i, TH * h + t, :] for t in range(TH)]

        def statistics(dve, chain, i, h):
            for t, x_tile in enumerate(tiles(i, h)):
                chain.step(dve.bn_stats(stats[:, TH * h + t, :], x_tile))

        def write(dve, i, h, rows, ready):
            for t, x_tile in enumerate(tiles(i, h)):
                k = TH * h + t
                dve.tensor_scalar(rows[:, k, :], x_tile, mv[:, k, 0:1], rstd[:, k:k + 1],
                                  ALU.subtract, ALU.mult).then_inc(ready, 1)

        with ExitStack() as c2:
            ps = c2.enter_context(nc.psum_tensor("a0_setup", [P, 8, 512], F32))
            block = c2.enter_context(nc.Block())

            @block.sync
            def _(sp):
                sp.dma_start(ctx_sb[:], ctx.rearrange("n s d -> s n d")).then_inc(ctx_in, 16)
                sp.dma_start(x4[:, 0, :, :], x[0].rearrange("(k p) d -> p k d", p=P)).then_inc(x0_in, 16)
                for w, src in ((wk, Wk), (wv, Wv), (wq, Wq), (wo, Wo)):
                    sp.dma_start(w[:], src.rearrange("(k p) n -> p k n", p=P)).then_inc(w_in, 16)
                sp.dma_start(x_sb[:, TB:NB * TB, :], x[1:NB].rearrange("n (k p) d -> p (n k) d", p=P)).then_inc(x_in, 16)

            @block.scalar
            def _(act):
                act.dma_start(bkT[:], bk.rearrange("(m p) -> p m", p=P), allow_slow_non_contiguous=True).then_inc(b_in, 16)
                act.dma_start(bqT[:], bq.rearrange("(m p) -> p m", p=P), allow_slow_non_contiguous=True).then_inc(b_in, 16)
                act.dma_start(bv_b[:], bv.rearrange("(a d) -> a d", a=1).to_broadcast([P, D])).then_inc(b_in, 16)
                act.dma_start(bo_b[:], bo.rearrange("(a d) -> a d", a=1).to_broadcast([P, D])).then_inc(b_in, 16)
                for k in range(KC):
                    act.wait_ge(ctxT_done, k + 1)
                    act.copy(ctxT[:, k, :], ps[:, k, 0:NB * S]).then_inc(ctxT_ready, 1)
                act.wait_ge(b_in, 64)
                for m in range(KC):
                    act.wait_ge(kv_done, m + 1)
                    act.activation(kT[:, m, :, :].rearrange("p n s -> p (n s)"), ps[:, 2 + m, 0:NB * S], ACT.Identity,
                                   bias=bkT[:, m:m + 1]).then_inc(k_ready, 1)

            @block.gpsimd
            def _(pool):
                pool.memset(ident[:], 0.0).then_inc(pool_chain, 1)
                pool.wait_ge(pool_chain, 1)
                pool.affine_select(out=ident[:], in_=ident[:], compare_op=ALU.not_equal, fill=1.0, base=0,
                                   pattern=[[-1, P]], channel_multiplier=1).then_inc(ident_ready, 1)
                pool.memset(head_mask[:], 1.0).then_inc(pool_chain, 1)
                pool.wait_ge(pool_chain, 2)
                pool.affine_select(out=head_mask[:], in_=head_mask[:], compare_op=ALU.is_ge, fill=0.0, base=0,
                                   pattern=[[-HD, HM]], channel_multiplier=1).then_inc(pool_chain, 1)
                pool.wait_ge(pool_chain, 3)
                pool.affine_select(out=head_mask[:], in_=head_mask[:], compare_op=ALU.is_ge, fill=0.0, base=HD - 1,
                                   pattern=[[HD, HM]], channel_multiplier=-1).then_inc(mask_ready, 1)
                pool.memset(v_blocks[:], 0.0).then_inc(pads_ready, 1)

            @block.vector
            def _(dve):
                chain = Chain(dve, dve_chain)
                dve.memset(k_blocks[:], 0.0)
                dve.wait_ge(x0_in, 16)
                for h in range(2):
                    statistics(dve, chain, 0, h)
                dve.wait_ge(chain.sem, chain.base + chain.n)
                moments(dve, chain, stats, mv, var[:], rstd[:], tmp[:], D)
                for h in range(2):
                    write(dve, 0, h, xn, xn_ready)
                dve.wait_ge(b_in, 64)
                for n in range(NB):
                    dve.wait_ge(kv_done, KC + n + 1)
                    dve.tensor_tensor(v_sb[:, n, :], ps[0:S, 4 + n, 0:D], bv_b[0:S, :], ALU.add).then_inc(v_ready, 1)

            @block.tensor
            def _(pe):
                pe.wait_ge(ident_ready, 1)
                pe.wait_ge(ctx_in, 16)
                for k in range(KC):
                    for n in range(NB):
                        last = pe.transpose(ps[:, k, n * S:(n + 1) * S], ctx_sb[:, n, k * P:(k + 1) * P],
                                            ident[0:S, 0:S])
                    last.then_inc(ctxT_done, 1)
                pe.wait_ge(ctxT_ready, KC)
                pe.wait_ge(w_in, 64)
                for m in range(KC):
                    for k in range(KC):
                        last = pe.matmul(ps[:, 2 + m, 0:NB * S], wk[:, k, m * P:(m + 1) * P], ctxT[:, k, :],
                                         start=(k == 0), stop=(k == KC - 1))
                    last.then_inc(kv_done, 1)
                for n in range(NB):
                    for k in range(KC):
                        last = pe.matmul(ps[0:S, 4 + n, 0:D], ctxT[:, k, n * S:(n + 1) * S], wv[:, k, :],
                                         start=(k == 0), stop=(k == KC - 1))
                    last.then_inc(kv_done, 1)

        with ExitStack() as c2:
            def sb2(name, shape, dt=F32):
                return c2.enter_context(nc.sbuf_tensor("a0m_" + name, shape, dt))

            def sem2(name):
                return c2.enter_context(nc.semaphore("a0m_" + name))

            gate_sb = sb2("gate", [P, KC, E])
            xn2 = sb2("xn2", [P, TB, D])
            xT, x2T = sb2("xT", [P, KC, L]), sb2("x2T", [P, KC, L])
            qT = sb2("qT", [P, KC, L])
            e_sb = sb2("e", [P, 2, L])
            v_scaled = sb2("v_scaled", [P, 2, P])
            aT = sb2("aT", [P, KC, L])
            mx, nmx = sb2("mx", [P, U]), sb2("nmx", [P, U])
            sums, rsum = sb2("sums", [P, U]), sb2("rsum", [P, U])
            gate_in, xn_out = sem2("gate_in"), sem2("xn_out")
            xn2_ready, kb_ready = sem2("xn2_ready"), sem2("kb_ready")
            bo_added = sem2("bo_added")
            scores_done, max_ready, exp_done = sem2("scores_done"), sem2("max_ready"), sem2("exp_done")
            vs_ready, pv_done, o_moved = sem2("vs_ready"), sem2("pv_done"), sem2("o_moved")
            work = c2.enter_context(nc.psum_tensor("a0_work", [P, 2, 512], F32))
            scores = c2.enter_context(nc.psum_tensor("a0_scores_ps", [P, 2, L], F32))
            o_ps = c2.enter_context(nc.psum_tensor("a0_out_ps", [P, L], F32))
            HALF = L // 2
            ORDER = [("q1", 0, 0), ("q1", 1, 0), ("out", 0, -1), ("out", 1, -1), ("out", 2, -1), ("out", 3, -1),
                     ("xT", 0, 1), ("xT", 1, 1), ("xT", 2, 1), ("xT", 3, 1), ("q0", 0, 1), ("q0", 1, 1),
                     ("x2", 0, -1), ("x2", 1, -1), ("x2", 2, -1), ("x2", 3, -1), ("z", 0, -1), ("z", 1, -1)]
            per = {kind: u + 1 for kind, u, _ in sorted(ORDER)}
            place = {(kind, u): i for i, (kind, u, _) in enumerate(ORDER)}
            assert len(ORDER) % 2 == 0
            full = {kind: sem2("full_" + kind) for kind in per}
            freed = {kind: sem2("freed_" + kind) for kind in per}
            block = c2.enter_context(nc.Block())

            def has(n):
                return not isinstance(n, int) or 0 <= n < NB

            def wait(eng, sem, value):
                if not isinstance(value, int) or value > 0:
                    eng.wait_ge(sem, value)

            def bank(kind, u):
                return work[:, place[kind, u] % 2, :]

            def take(n, kind, u):
                row, i = n, place[kind, u] - 2
                for _ in range(len(ORDER)):
                    if i < 0:
                        i, row = i + len(ORDER), row - 1
                    kind2, u2, dist2 = ORDER[i]
                    if has(row + dist2):
                        before = per["z"] if kind2 == "z" else 0
                        wait(nc.tensor, freed[kind2], per[kind2] * (row + dist2) + u2 + 1 + before)
                        break
                    i -= 2
                return bank(kind, u)

            def program(eng, row, chain=None, steps=0):
                row(-1)
                row(0)
                with eng.Fori(1, NB - 1) as n:
                    if chain:
                        chain.enter(n - 1, steps)
                    row(n)
                if chain:
                    chain.leave(NB - 2)
                row(NB - 1)
                row(NB)

            @block.sync
            def _(sp):
                sp.wait_ge(v_ready, NB)
                sp.wait_ge(pads_ready, 1)
                for m in range(KC):
                    for h, s0, n, j, p0 in pieces:
                        sp.dma_start(v_blocks[p0:p0 + n, :, m, j, h * HD:(h + 1) * HD],
                                     v_sb[s0:s0 + n, :, m * P + h * HD:m * P + (h + 1) * HD]).then_inc(v_moved[m], 16)
                sp.dma_start(gate_sb[:], gate.rearrange("(k p) e -> p k e", p=P)).then_inc(gate_in, 16)
                sp.sem_inc(xn_out, 1)
                with sp.Fori(0, NB) as n:
                    b = sp.snap(n)
                    sp.wait_ge(xn2_ready, TB * n + TB)
                    sp.dma_start(xn_dram.rearrange("(n k p) d -> n p k d", n=NB, p=P)[b], xn2[:]).then_inc(xn_out, 16)
                sp.wait_ge(xn_out, 16 * NB + 1)

            @block.tensor
            def _(pe):
                def unit_scores(n, u):
                    m, j = divmod(u, JT)
                    if j == 0:
                        pe.wait_ge(kb_ready, KC * n + m + 1)
                        pe.wait_ge(freed["q0" if m == 0 else "q1"], 2 * n + 2)
                    wait(pe, exp_done, U * n + u - 1)
                    for h in range(2):
                        last = pe.matmul(scores[:, u % 2, h * HALF:(h + 1) * HALF], k_blocks[:, m, j * P:(j + 1) * P],
                                         qT[:, m, h * HALF:(h + 1) * HALF], start=True, stop=True)
                    last.then_inc(scores_done, 1)

                def unit_values(n, u):
                    m, j = divmod(u, JT)
                    pe.wait_ge(vs_ready, U * n + u + 1)
                    if j == 0:
                        wait(pe, o_moved, KC * n + m)
                    for h in range(2):
                        last = pe.matmul(o_ps[:, h * HALF:(h + 1) * HALF], v_scaled[:, u % 2, :],
                                         e_sb[:, u % 2, h * HALF:(h + 1) * HALF], start=(j == 0), stop=(j == JT - 1))
                    last.then_inc(pv_done, 1)

                def turn(n, kind, u, rows, ready, i):
                    h, k = divmod(u, KC)
                    pe.wait_ge(ready, TB * i + TH * (h + 1))
                    ps = take(n, kind, u)
                    for t in range(TH):
                        last = pe.transpose(ps[:, t * P:(t + 1) * P], rows[:, TH * h + t, k * P:(k + 1) * P], ident[:])
                    last.then_inc(full[kind], 1)

                def project_q(n, m, h, i):
                    kind = "q0" if m == 0 else "q1"
                    pe.wait_ge(freed["xT"], 4 * i + 2 * h + 2)
                    ps = take(n, kind, h)
                    for k in range(KC):
                        last = pe.matmul(ps, wq[:, k, m * P:(m + 1) * P], xT[:, k, h * HALF:(h + 1) * HALF],
                                         start=(k == 0), stop=(k == KC - 1))
                    last.then_inc(full[kind], 1)

                def output(n, w, i):
                    pe.wait_ge(o_moved, KC * i + KC)
                    ps = take(n, "out", w)
                    for t in range(2):
                        c0 = (2 * w + t) * P
                        for m in range(KC):
                            last = pe.matmul(ps[:, t * D:(t + 1) * D], aT[:, m, c0:c0 + P], wo[:, m, :],
                                             start=(m == 0), stop=(m == KC - 1))
                    last.then_inc(full["out"], 1)

                def logits(n, h, i):
                    pe.wait_ge(freed["x2"], 4 * i + 2 * h + 2)
                    ps = take(n, "z", h)
                    for t in range(TH):
                        for k in range(KC):
                            last = pe.matmul(ps[:, t * E:(t + 1) * E], x2T[:, k, (TH * h + t) * P:(TH * h + t + 1) * P],
                                             gate_sb[:, k, :], start=(k == 0), stop=(k == KC - 1))
                    last.then_inc(full["z"], 1)

                def row(n):
                    for u in range(U):
                        if has(n):
                            unit_scores(n, u)
                            if u:
                                unit_values(n, u - 1)
                            if u == 0:
                                project_q(n, 1, 0, n)
                                project_q(n, 1, 1, n)
                        if 1 <= u <= 4 and has(n - 1):
                            output(n, u - 1, n - 1)
                        if 5 <= u <= 6 and has(n + 1):
                            for k in range(KC):
                                turn(n, "xT", 2 * (u - 5) + k, xn, xn_ready, n + 1)
                        if 7 <= u <= 8 and has(n + 1):
                            project_q(n, 0, u - 7, n + 1)
                        if u == 9 and has(n - 1):
                            for k in range(KC):
                                turn(n, "x2", k, xn2, xn2_ready, n - 1)
                    if has(n):
                        unit_values(n, U - 1)
                    if has(n - 1):
                        for k in range(KC):
                            turn(n, "x2", 2 + k, xn2, xn2_ready, n - 1)
                        for h in range(2):
                            logits(n, h, n - 1)
                    if isinstance(n, int) and n == 0:
                        pe.wait_ge(gate_in, 16)

                program(pe, row)

            @block.scalar
            def _(act):
                def unit_exp(n, u):
                    act.wait_ge(max_ready, U * n + u + 1)
                    wait(act, pv_done, U * n + u - 1)
                    act.activation(e_sb[:, u % 2, :], scores[:, u % 2, :], ACT.Exp, bias=nmx[:, u:u + 1],
                                   scale=SCALE, accum_out=sums[:, u:u + 1]).then_inc(exp_done, 1)

                def move_out(n, m):
                    act.wait_ge(pv_done, U * n + JT * (m + 1))
                    wait(act, full["out"], 4 * n)
                    act.copy(aT[:, m, :], o_ps[:, :]).then_inc(o_moved, 1)

                def take_turned(kind, u, dst, i):
                    h, k = divmod(u, KC)
                    act.wait_ge(full[kind], 4 * i + u + 1)
                    act.copy(dst[:, k, h * HALF:(h + 1) * HALF], bank(kind, u)).then_inc(freed[kind], 1)

                def take_q(m, h, i):
                    kind = "q0" if m == 0 else "q1"
                    act.wait_ge(full[kind], 2 * i + h + 1)
                    act.activation(qT[:, m, h * HALF:(h + 1) * HALF], bank(kind, h), ACT.Identity,
                                   bias=bqT[:, m:m + 1]).then_inc(freed[kind], 1)

                def row(n):
                    for u in range(U):
                        if has(n):
                            unit_exp(n, u)
                            if u == 0:
                                take_q(1, 0, n)
                                take_q(1, 1, n)
                            if u == JT:
                                move_out(n, 0)
                        if 5 <= u <= 6 and has(n + 1):
                            if u == 5 and has(n):
                                act.wait_ge(full["q1"], 2 * n + 2)
                            for k in range(KC):
                                take_turned("xT", 2 * (u - 5) + k, xT, n + 1)
                        if 7 <= u <= 8 and has(n + 1):
                            if has(n):
                                act.wait_ge(scores_done, U * n + JT)
                            take_q(0, u - 7, n + 1)
                        if u == 9 and has(n - 1):
                            for k in range(KC):
                                take_turned("x2", k, x2T, n - 1)
                    if has(n):
                        move_out(n, KC - 1)
                    if has(n - 1):
                        for k in range(KC):
                            take_turned("x2", 2 + k, x2T, n - 1)

                program(act, row)

            @block.gpsimd
            def _(pool):
                with pool.Fori(0, NB) as n:
                    for k in range(TB):
                        if k == 0:
                            pool.wait_ge(xn_ready, TB * n + TB)
                            alone(pool, passed)
                        pool.tensor_tensor(x4[:, n, k, :], x4[:, n, k, :], bo_b[:], ALU.add).then_inc(bo_added, 1)

            @block.vector
            def _(dve):
                chain = Chain(dve, dve_chain)
                chain.n = TB + MOMENTS_STEPS

                def unit_max(n, u):
                    dve.wait_ge(scores_done, U * n + u + 1)
                    chain.link(dve.tensor_reduce(mx[:, u:u + 1], scores[:, u % 2, :], AX.X, ALU.max))
                    dve.tensor_scalar(nmx[:, u:u + 1], mx[:, u:u + 1], -SCALE, None, ALU.mult).then_inc(max_ready, 1)

                def unit_scale(n, u):
                    m, j = divmod(u, JT)
                    dve.wait_ge(exp_done, U * n + u + 1)
                    chain.link(dve.reciprocal(rsum[:, u:u + 1], sums[:, u:u + 1]))
                    wait(dve, pv_done, U * n + u - 1)
                    dve.tensor_scalar(v_scaled[:, u % 2, :], v_blocks[:, n, m, j, :], rsum[:, u:u + 1], None,
                                      ALU.mult).then_inc(vs_ready, 1)

                def place_keys(n, m):
                    dve.tensor_tensor(k_blocks[:, m, 0:HM * S].rearrange("p (h s) -> p h s", s=S),
                                      kT[:, m, n, :].rearrange("p (a s) -> p a s", a=1).to_broadcast([P, HM, S]),
                                      head_mask[:, :].rearrange("p (h a) -> p h a", a=1).to_broadcast([P, HM, S]),
                                      ALU.mult).then_inc(kb_ready, 1)

                def add_output(w, i):
                    dve.wait_ge(full["out"], 4 * i + w + 1)
                    if w == 0:
                        dve.wait_ge(bo_added, TB * i + TB)
                    dve.tensor_tensor(x4[:, i, 2 * w:2 * w + 2, :], bank("out", w).rearrange("p (t d) -> p t d", t=2),
                                      x4[:, i, 2 * w:2 * w + 2, :], ALU.add).then_inc(freed["out"], 1)

                def take_logits(h, i):
                    dve.wait_ge(full["z"], 2 * i + h + 1)
                    dve.tensor_copy(z_all[:, :, :].rearrange("p (n h k) e -> p n h (k e)", h=2, k=TH)[:, i, h, :],
                                    bank("z", h)[:, 0:TH * E]).then_inc(freed["z"], 1)

                def row(n):
                    for u in range(U):
                        if has(n):
                            if isinstance(n, int) and n == 0 and u % JT == 1:
                                dve.wait_ge(v_moved[u // JT], 16 * len(pieces))
                                if u == 1:
                                    dve.wait_ge(x_in, 16)
                            if u:
                                unit_scale(n, u - 1)
                            unit_max(n, u)
                            if u == 0:
                                place_keys(n, 1)
                        if 1 <= u <= 2 and has(n + 1) and has(n):
                            statistics(dve, chain, n + 1, u - 1)
                        if 2 <= u <= 5 and has(n - 1):
                            add_output(u - 2, n - 1)
                        if u == 3 and has(n + 1) and has(n):
                            dve.wait_ge(chain.sem, chain.base + chain.n)
                            moments(dve, chain, stats, mv, var[:], rstd[:], tmp[:], D)
                        if 4 <= u <= 5 and has(n + 1) and has(n):
                            wait(dve, full["xT"], 4 * (n + 1))
                            write(dve, n + 1, u - 4, xn, xn_ready)
                        if 5 <= u <= 6 and has(n - 1):
                            if u == 5:
                                dve.wait_ge(freed["out"], 4 * (n - 1) + 4)
                                if has(n + 1):
                                    dve.wait_ge(xn_ready, TB * (n + 1) + TB)
                                alone(dve, passed)
                            statistics(dve, chain, n - 1, u - 5)
                        if u == 6 and has(n + 1):
                            place_keys(n + 1, 0)
                        if u == 7 and has(n - 1):
                            dve.wait_ge(chain.sem, chain.base + chain.n)
                            moments(dve, chain, stats, mv, var[:], rstd[:], tmp[:], D)
                        if 8 <= u <= 9 and has(n - 1):
                            dve.wait_ge(xn_out, 16 * (n - 1) + 1)
                            write(dve, n - 1, u - 8, xn2, xn2_ready)
                    if has(n):
                        unit_scale(n, U - 1)
                    if has(n - 1):
                        for h in range(2):
                            take_logits(h, n - 1)

                dve.sem_inc(freed["z"], per["z"])
                program(dve, row, chain, 2 * (TB + MOMENTS_STEPS) + 2 * U)


def alone(eng, passed):
    eng.sem_inc(passed, 1)


class RouteSemaphores:
    turn = 0
    rows = 0
    steps = 0


class Routes:
    pass


def routes_of(nc, tag, keep, K, TILES, CAP, NT):
    r = Routes()

    def kept(name, shape, dt=F32):
        return keep.enter_context(nc.sbuf_tensor(f"{tag}_{name}", shape, dt))

    r.gates = [kept(f"gate{k}", [P, NT]) for k in range(K)]
    r.slot = [kept(f"slot{k}", [P, NT + 1], I32) for k in range(K)]
    r.token = kept("token", [P, TILES + 1], I32)
    r.expert = kept("expert", [P, TILES], I32)
    if CAP is not None:
        r.target = kept("target", [P, TILES], I32)
        r.slot_gate = kept("slot_gate", [P, TILES])
    return r


def route(nc, sems, tag, r, z, K, E, TILES, CAP, NT, load, prepare=None):
    GROUPS = 2 if CAP is None else 6
    with ExitStack() as c:
        def sb(name, shape, dt=F32):
            return c.enter_context(nc.sbuf_tensor(f"{tag}_{name}", shape, dt))

        p, p2 = sb("p", [P, NT, E]), sb("p2", [P, NT, E])
        t1, t2 = sb("t1", [P, NT, E]), sb("t2", [P, NT, E])
        hot = [sb(f"hot{k}", [P, NT, E]) for k in range(K)]
        hot_all = sb("hot_all", [P, NT, E], BF16)
        m1, m2, m3 = sb("m1", [P, NT]), sb("m2", [P, NT]), sb("m3", [P, NT])
        mi, ti, bi = sb("mi", [P, NT], I32), sb("ti", [P, NT], I32), sb("bi", [P, NT], I32)
        tf, bf = sb("tf", [P, NT], BF16), sb("bf", [P, NT], BF16)
        slots_f = sb("slots_f", [P, NT, E])
        iota_e = sb("iota_e", [P, E])
        iota_p = sb("iota_p", [P, P], BF16)
        iota_t = sb("iota_t", [P, TILES], BF16)
        iota_i = sb("iota_i", [P, NT], BF16)
        own_p = sb("own_p", [P, 1])
        gate_part = sb("gate_part", [P, NT], BF16)
        lower = sb("lower", [P, P], BF16)
        ones = sb("ones", [P, P], BF16)
        count_i, count_t = sb("count_i", [P, E], I32), sb("count_t", [P, E], I32)
        tiles_f, ones_e, upto, first = sb("tiles_f", [P, E]), sb("ones_e", [P, E]), sb("upto", [P, E]), sb("first", [P, E])
        in_row = [sb(f"in_row{k}", [P, NT, P], BF16) for k in range(K)]
        in_tile = [sb(f"in_tile{k}", [P, NT, GROUPS, TILES], BF16) for k in range(K)]
        in_tile_f = sb("in_tile_f", [P, NT, TILES], BF16)
        token_f = sb("token_f", [P, TILES])
        tile_e = sb("tile_e", [P, TILES, E], BF16)
        tile_s = sb("tile_s", [P, TILES])

        consts_ready, pool_chain, exp_ready, exp_done = sems.consts_ready, sems.pool_chain, sems.exp_ready, sems.exp_done
        hot_ready, ranks_done, rows_ready, tokens_done = sems.hot_ready, sems.ranks_done, sems.rows_ready, sems.tokens_done
        sems.turn += 1
        turn = sems.turn
        rows_before = sems.rows
        sems.rows += K
        rank_ps = c.enter_context(nc.psum_tensor(f"{tag}_rank_ps", [P, 512], F32))
        count_ps = c.enter_context(nc.psum_tensor(f"{tag}_count_ps", [P, 512], F32))
        token_ps = c.enter_context(nc.psum_tensor(f"{tag}_token_ps", [P, 512], F32))
        block = c.enter_context(nc.Block())

        @block.sync
        def _(sp):
            load(sp)

        @block.gpsimd
        def _(pool):
            pool.iota(iota_e[:], [[1, E]], base=-E, channel_multiplier=0, allow_small_or_imprecise_dtypes=True)
            pool.iota(iota_p[:], [[1, P]], base=0, channel_multiplier=0, allow_small_or_imprecise_dtypes=True)
            pool.iota(iota_t[:], [[1, TILES]], base=0, channel_multiplier=0, allow_small_or_imprecise_dtypes=True)
            pool.iota(iota_i[:], [[1, NT]], base=0, channel_multiplier=0, allow_small_or_imprecise_dtypes=True)
            pool.iota(own_p[:], [[0, 1]], base=0, channel_multiplier=1, allow_small_or_imprecise_dtypes=True)
            pool.memset(ones_e[:], 1.0)
            pool.memset(r.token[:, TILES:TILES + 1], 0)
            for k in range(K):
                pool.memset(r.slot[k][:, NT:NT + 1], 0)
            pool.memset(ones[:], 1.0)
            pool.memset(lower[:], 1.0).then_inc(pool_chain, 1)
            pool.wait_ge(pool_chain, turn)
            pool.affine_select(out=lower[:], in_=lower[:], compare_op=ALU.is_gt, fill=0.0, base=0,
                               pattern=[[1, P]], channel_multiplier=-1).then_inc(consts_ready, 1)

        @block.tensor
        def _(pe):
            pe.wait_ge(consts_ready, turn)
            pe.wait_ge(hot_ready, turn)
            h2 = hot_all[:, :, :].rearrange("p i e -> p (i e)")
            for s in range(1, NT):
                pe.matmul(rank_ps[:, s * E:NT * E], ones[:], h2[:, 0:(NT - s) * E], start=(s == 1), stop=False,
                          skip_group_check=True)
            pe.matmul(rank_ps[:, 0:NT * E], lower[:], h2, start=False, stop=True, skip_group_check=True)
            for i in range(NT):
                last = pe.matmul(count_ps[:, 0:E], ones[:], hot_all[:, i, :], start=(i == 0), stop=(i == NT - 1))
            last.then_inc(ranks_done, 1)
            for k in range(K):
                pe.wait_ge(rows_ready, rows_before + k + 1)
                for i in range(NT):
                    last = pe.matmul(token_ps[:, 0:GROUPS * TILES], in_row[k][:, i, :],
                                     in_tile[k][:, i, :, :].rearrange("p a t -> p (a t)"),
                                     start=(k == 0 and i == 0), stop=(k == K - 1 and i == NT - 1))
            last.then_inc(tokens_done, 1)

        @block.scalar
        def _(act):
            act.wait_ge(exp_ready, turn)
            act.activation(t1[:], t2[:], ACT.Exp).then_inc(exp_done, 1)
            if prepare:
                prepare(act)

        @block.vector
        def _(dve):
            chain = Chain(dve, sems.dve_chain, sems.steps)
            link = chain.link

            def per_token(a):
                return a.rearrange("p (i a) -> p i a", a=1).to_broadcast([P, NT, E])

            def per_expert(a):
                return a.rearrange("p (a e) -> p a e", a=1).to_broadcast([P, NT, E])

            dve.wait_ge(consts_ready, turn)
            link(dve.tensor_reduce(m1[:], z[:], AX.X, ALU.max))
            dve.tensor_tensor(t2[:], z[:], per_token(m1[:]), ALU.subtract).then_inc(exp_ready, 1)
            dve.wait_ge(exp_done, turn)
            link(dve.tensor_reduce(m2[:], t1[:], AX.X, ALU.add))
            link(dve.reciprocal(m3[:], m2[:]))
            link(dve.tensor_tensor(p[:], t1[:], per_token(m3[:]), ALU.mult))
            left = p
            for k in range(K):
                link(dve.tensor_reduce(r.gates[k][:], left[:], AX.X, ALU.max))
                link(dve.tensor_tensor(t1[:], left[:], per_token(r.gates[k][:]), ALU.is_equal))
                link(dve.tensor_tensor(t2[:], t1[:], per_expert(iota_e[:]), ALU.mult))
                link(dve.tensor_reduce(m1[:], t2[:], AX.X, ALU.min))
                link(dve.tensor_tensor(hot[k][:], per_expert(iota_e[:]), per_token(m1[:]), ALU.is_equal))
                if k + 1 < K:
                    link(dve.scalar_tensor_tensor(p2[:], hot[k][:], -2.0, left[:], ALU.mult, ALU.add))
                    left = p2
            if K == 2:
                link(dve.tensor_tensor(m1[:], r.gates[0][:], r.gates[1][:], ALU.add))
                link(dve.tensor_scalar(m2[:], m1[:], 1e-12, None, ALU.max))
                link(dve.reciprocal(m3[:], m2[:]))
                for k in range(K):
                    link(dve.tensor_tensor(r.gates[k][:], r.gates[k][:], m3[:], ALU.mult))
                dve.tensor_tensor(hot_all[:], hot[0][:], hot[1][:], ALU.add).then_inc(hot_ready, 1)
            else:
                dve.tensor_copy(hot_all[:], hot[0][:]).then_inc(hot_ready, 1)
            dve.wait_ge(ranks_done, turn)
            ranks = rank_ps[:, 0:NT * E].rearrange("p (i e) -> p i e", e=E)
            if CAP is None:
                link(dve.tensor_scalar(count_i[:], count_ps[:, 0:E], float(P - 1), None, ALU.add))
                link(dve.tensor_scalar(count_t[:], count_i[:], P.bit_length() - 1, None, ALU.logical_shift_right))
                link(dve.tensor_copy(tiles_f[:], count_t[:]))
                link(dve.tensor_tensor_scan(upto[:], ones_e[:], tiles_f[:], 0.0, ALU.mult, ALU.add))
                link(dve.tensor_tensor(first[:], upto[:], tiles_f[:], ALU.subtract))
                link(dve.tensor_scalar(first[:], first[:], float(P), None, ALU.mult))
            else:
                link(dve.tensor_scalar(first[:], iota_e[:], float(E), float(CAP), ALU.add, ALU.mult))
                link(dve.tensor_scalar(upto[:], first[:], float(CAP), 1.0 / P, ALU.add, ALU.mult))
            link(dve.tensor_tensor(slots_f[:], ranks, per_expert(first[:]), ALU.add))
            for k in range(K):
                link(dve.tensor_tensor(t1[:], hot[k][:], slots_f[:], ALU.mult))
                link(dve.tensor_reduce(m1[:], t1[:], AX.X, ALU.add))
                if CAP is not None:
                    link(dve.tensor_tensor(t2[:], hot[k][:], ranks, ALU.mult))
                    link(dve.tensor_reduce(m2[:], t2[:], AX.X, ALU.add))
                    link(dve.tensor_scalar(m3[:], m2[:], float(CAP), None, ALU.is_lt))
                    link(dve.tensor_tensor(r.gates[k][:], r.gates[k][:], m3[:], ALU.mult))
                    link(dve.tensor_tensor(m1[:], m1[:], m3[:], ALU.mult))
                    link(dve.tensor_copy(r.slot[k][:, 0:NT], m1[:]))
                    link(dve.tensor_scalar(m3[:], m3[:], -FAR, FAR, ALU.mult, ALU.add))
                    link(dve.tensor_tensor(m1[:], m1[:], m3[:], ALU.add))
                else:
                    link(dve.tensor_copy(r.slot[k][:, 0:NT], m1[:]))
                link(dve.tensor_copy(mi[:], m1[:]))
                link(dve.tensor_scalar(ti[:], mi[:], P.bit_length() - 1, None, ALU.logical_shift_right))
                link(dve.tensor_scalar(bi[:], mi[:], P - 1, None, ALU.bitwise_and))
                link(dve.tensor_copy(tf[:], ti[:]))
                link(dve.tensor_copy(bf[:], bi[:]))
                link(dve.tensor_tensor(in_row[k][:], bf[:, :].rearrange("p (i a) -> p i a", a=1).to_broadcast([P, NT, P]),
                                       iota_p[:, :].rearrange("p (a q) -> p a q", a=1).to_broadcast([P, NT, P]),
                                       ALU.is_equal))
                link(dve.tensor_tensor(in_tile_f[:],
                                       tf[:, :].rearrange("p (i a) -> p i a", a=1).to_broadcast([P, NT, TILES]),
                                       iota_t[:, :].rearrange("p (a q) -> p a q", a=1).to_broadcast([P, NT, TILES]),
                                       ALU.is_equal))
                link(dve.tensor_tensor(in_tile[k][:, :, 0, :], in_tile_f[:],
                                       iota_i[:, :].rearrange("p (i a) -> p i a", a=1).to_broadcast([P, NT, TILES]),
                                       ALU.mult))
                link(dve.tensor_scalar(in_tile[k][:, :, 1, :], in_tile_f[:], own_p[:, 0:1], None, ALU.mult))
                if CAP is None:
                    dve.sem_inc(rows_ready, 1)
                else:
                    chain.step(dve.tensor_copy(in_tile[k][:, :, 2, :], in_tile_f[:]))
                    link(dve.tensor_copy(m1[:], r.gates[k][:]))
                    for part in range(3):
                        link(dve.tensor_copy(gate_part[:], m1[:]))
                        chain.step(dve.tensor_tensor(m1[:], m1[:], gate_part[:], ALU.subtract))
                        link(dve.tensor_tensor(in_tile[k][:, :, 3 + part, :], in_tile_f[:],
                                               gate_part[:, :].rearrange("p (i a) -> p i a", a=1)
                                               .to_broadcast([P, NT, TILES]), ALU.mult))
                    dve.sem_inc(rows_ready, 1)
            link(dve.tensor_tensor(tile_e[:], upto[:, :].rearrange("p (a e) -> p a e", a=1).to_broadcast([P, TILES, E]),
                                   iota_t[:, :].rearrange("p (t a) -> p t a", a=1).to_broadcast([P, TILES, E]),
                                   ALU.is_le))
            link(dve.tensor_reduce(tile_s[:], tile_e[:], AX.X, ALU.add))
            link(dve.tensor_scalar(r.expert[:], tile_s[:], float(E - 1), None, ALU.min))
            dve.wait_ge(tokens_done, turn)
            link(dve.tensor_copy(token_f[:], token_ps[:, TILES:2 * TILES]))
            link(dve.scalar_tensor_tensor(r.token[:, 0:TILES], token_ps[:, 0:TILES], float(P), token_f[:],
                                          ALU.mult, ALU.add))
            if CAP is not None:
                link(dve.tensor_scalar(token_f[:], token_ps[:, 2 * TILES:3 * TILES], -FAR, FAR, ALU.mult, ALU.add))
                chain.step(dve.tensor_tensor(r.target[:], r.token[:, 0:TILES], token_f[:], ALU.add))
                link(dve.tensor_copy(r.slot_gate[:], token_ps[:, 3 * TILES:4 * TILES]))
                for part in (4, 5):
                    link(dve.tensor_tensor(r.slot_gate[:], r.slot_gate[:],
                                           token_ps[:, part * TILES:(part + 1) * TILES], ALU.add))
            sems.steps = chain.base + chain.n


class Weights:
    pass


def experts_0_weights(nc, keep, E, D, H, KC):
    w = Weights()
    HC = H // P

    def kept(name, shape):
        return keep.enter_context(nc.sbuf_tensor("e0_" + name, shape, F32))

    w.w1, w.w2 = kept("w1", [P, KC, E, H]), kept("w2", [P, HC, E, D])
    w.b1_b = kept("b1_b", [P, E, H])
    w.w_in = keep.enter_context(nc.semaphore("e0_w_in"))
    w.loads = KC + HC + 1
    return w


def load_experts_0(sp, w, W1, b1, W2, E, D, H, KC, a1, Wk1):
    for k in range(KC):
        sp.dma_start(w.w1[:, k, :, :], W1[:, k * P:(k + 1) * P, :].rearrange("e p h -> p e h")).then_inc(w.w_in, 16)
    sp.dma_start(w.b1_b[:, :, :].rearrange("p e h -> p (e h)"),
                 b1.rearrange("(a e) h -> a (e h)", a=1).to_broadcast([P, E * H])).then_inc(w.w_in, 16)
    for j in range(H // P):
        sp.dma_start(w.w2[:, j, :, :], W2[:, j * P:(j + 1) * P, :].rearrange("e p d -> p e d")).then_inc(w.w_in, 16)
    sp.dma_start(a1.wk[:], Wk1.rearrange("(k p) n -> p k n", p=P)).then_inc(a1.wk_in, 16)


def attention_1_weights(nc, keep, D, KC, INNER):
    w = Weights()

    def kept(name, shape):
        return keep.enter_context(nc.sbuf_tensor("a1_" + name, shape, F32))

    w.wq, w.wk, w.wv = (kept(n, [P, KC, INNER]) for n in ("wq", "wk", "wv"))
    w.wo_hi, w.wo_lo = (keep.enter_context(nc.sbuf_tensor("a1_" + n, [P, INNER // P, D], F32R)) for n in ("wo_hi", "wo_lo"))
    w.wk_in, w.w_in = (keep.enter_context(nc.semaphore("a1_" + n)) for n in ("wk_in", "w_in"))
    return w


def centre(dve, chain, weights, means, HD):
    heads = weights[:, :, :].rearrange("p k (h d) -> p (k h) d", d=HD)
    chain.link(dve.tensor_reduce(means[:], heads, AX.X, ALU.add))
    chain.link(dve.tensor_scalar(means[:], means[:], 1.0 / HD, None, ALU.mult))
    chain.link(dve.tensor_tensor(heads, heads, means[:, :].rearrange("p (h a) -> p h a", a=1)
                                 .to_broadcast([P, heads.shape[1], HD]), ALU.subtract))


def experts_0(nc, xn_dram, y_dram, ident, r, w, b2, E, D, H, KC, TILES, a1, Wq1, Wv1, Wo1, HD1):
    HC = H // P
    w1, w2, b1_b = w.w1, w.w2, w.b1_b
    with ExitStack() as c:
        def sb(name, shape, dt=F32):
            return c.enter_context(nc.sbuf_tensor("e0_" + name, shape, dt))

        def sem(name):
            return c.enter_context(nc.semaphore("e0_" + name))

        index = sb("index", [P, 2], I32)
        xg = sb("xg", [P, 2, D])
        xT = sb("xT", [P, 2, KC * P])
        h_sb = sb("h", [P, 2, H])
        hT = sb("hT", [P, 2, H])
        y_sb = sb("y", [P, 2, D])
        b2_b = sb("b2_b", [P, E, D])
        wo = sb("wo", [P, Wo1.shape[0] // P, D])
        b2_in, wo_in, wo_hi_ready = sem("b2_in"), sem("wo_in"), sem("wo_hi_ready")
        means = sb("means", [P, a1.wq.shape[1] * a1.wq.shape[2] // HD1])
        index_ready, dve_chain = sem("index_ready"), sem("dve_chain")
        gathered = [sem(f"gathered{b}") for b in range(2)]
        stored = [sem(f"stored{b}") for b in range(2)]
        x_turned, xT_ready, h_done, h_ready, h_turned, hT_ready, y_done, y_ready = (
            sem(s) for s in ("x_turned", "xT_ready", "h_done", "h_ready", "h_turned", "hT_ready", "y_done", "y_ready"))
        x_ps = c.enter_context(nc.psum_tensor("e0_x_ps", [P, 2, 512], F32))
        h_ps = c.enter_context(nc.psum_tensor("e0_h_ps", [P, 2, 512], F32))
        hT_ps = c.enter_context(nc.psum_tensor("e0_hT_ps", [P, 2, 512], F32))
        y_ps = c.enter_context(nc.psum_tensor("e0_y_ps", [P, 2, 512], F32))
        block = c.enter_context(nc.Block())
        PAIRS = TILES // 2
        assert TILES % 2 == 0

        def pairs(eng, pair, then=None):
            pair(0)
            if then:
                then()
            with eng.Fori(1, PAIRS - 1) as i:
                pair(i)
            pair(PAIRS - 1)

        def later(i):
            return not isinstance(i, int) or i > 0

        def has_next(i):
            return not isinstance(i, int) or i + 1 < PAIRS

        @block.sync
        def _(sp):
            sp.dma_start(b2_b[:, :, :].rearrange("p e h -> p (e h)"),
                         b2.rearrange("(a e) h -> a (e h)", a=1).to_broadcast([P, E * D])).then_inc(b2_in, 16)
            sp.dma_start(wo[:], Wo1.rearrange("(k p) n -> p k n", p=P)).then_inc(wo_in, 16)
            for dst, src in ((a1.wv, Wv1), (a1.wq, Wq1)):
                sp.dma_start(dst[:], src.rearrange("(k p) n -> p k n", p=P)).then_inc(a1.w_in, 16)

            def pair(i):
                for b in range(2):
                    t = sp.snap(2 * i + b) if not isinstance(i, int) else 2 * i + b
                    sp.wait_ge(y_ready, 2 * i + b + 1)
                    sp.dma_start(y_dram.rearrange("(t p) d -> t p d", p=P)[t], y_sb[:, b, :]).then_inc(stored[b], 16)

            pairs(sp, pair)
            for b in range(2):
                sp.wait_ge(stored[b], 16 * PAIRS)

        @block.gpsimd
        def _(pool):
            pool.tensor_copy(index[:, 0:1], r.token[:, 0:1]).then_inc(index_ready, 1)

            def pair(i):
                for b in range(2):
                    after = pool.snap(2 * i + b + 1) if not isinstance(i, int) else 2 * i + b + 1
                    if later(i) or b:
                        pool.wait_ge(gathered[1 - b], 16 * i + 16 * b)
                    if later(i):
                        pool.wait_ge(x_turned, 2 * i + b - 1)
                    pool.wait_ge(index_ready, 2 * i + b + 1)
                    pool.tensor_copy(index[:, 1 - b:2 - b], r.token[:, bass.ds(after, 1)]).then_inc(index_ready, 1)
                    pool.indirect_dma_start(xg[:, b, :], None, xn_dram,
                                            bass.IndirectOffsetOnAxis(ap=index[:, b:b + 1], axis=0)
                                            ).then_inc(gathered[b], 16)

            pairs(pool, pair)

        @block.tensor
        def _(pe):
            def turn_x(i, b):
                pe.wait_ge(gathered[b], 16 * i + 16)
                if later(i):
                    pe.wait_ge(xT_ready, 2 * i + b - 1)
                for k in range(KC):
                    last = pe.transpose(x_ps[:, b, k * P:(k + 1) * P], xg[:, b, k * P:(k + 1) * P], ident[:])
                last.then_inc(x_turned, 1)

            def turn_h(i, b):
                pe.wait_ge(h_ready, 2 * i + b + 1)
                for j in range(HC):
                    last = pe.transpose(hT_ps[:, b, j * P:(j + 1) * P], h_sb[:, b, j * P:(j + 1) * P], ident[:])
                last.then_inc(h_turned, 1)

            def pair(i):
                es = [pe.value_load(r.expert[0:1, bass.ds(2 * i + b, 1)], min_val=0, max_val=E - 1) for b in range(2)]
                for b in range(2):
                    pe.wait_ge(xT_ready, 2 * i + b + 1)
                    for k in range(KC):
                        last = pe.matmul(h_ps[:, b, :], xT[:, b, k * P:(k + 1) * P],
                                         w1[:, k, es[b], :], start=(k == 0), stop=(k == KC - 1))
                    last.then_inc(h_done, 1)
                turn_h(i, 0)
                if has_next(i):
                    for b in range(2):
                        turn_x(i + 1, b)
                turn_h(i, 1)
                for b in range(2):
                    pe.wait_ge(hT_ready, 2 * i + b + 1)
                    if later(i):
                        pe.wait_ge(y_ready, 2 * i + b - 1)
                    for j in range(HC):
                        last = pe.matmul(y_ps[:, b, 0:D], hT[:, b, j * P:(j + 1) * P], w2[:, j, es[b], :],
                                         start=(j == 0), stop=(j == HC - 1))
                    last.then_inc(y_done, 1)

            for b in range(2):
                turn_x(0, b)
            pe.wait_ge(w.w_in, 16 * w.loads)
            pairs(pe, pair)

        @block.scalar
        def _(act):
            def take_x(i, b):
                act.wait_ge(x_turned, 2 * i + b + 1)
                if later(i):
                    act.wait_ge(h_done, 2 * i + b - 1)
                act.copy(xT[:, b, :], x_ps[:, b, 0:KC * P]).then_inc(xT_ready, 1)

            def take_h(i, b):
                act.wait_ge(h_turned, 2 * i + b + 1)
                if later(i):
                    act.wait_ge(y_done, 2 * i + b - 1)
                act.activation(hT[:, b, :], hT_ps[:, b, :], ACT.Relu).then_inc(hT_ready, 1)

            def pair(i):
                take_h(i, 0)
                if has_next(i):
                    for b in range(2):
                        take_x(i + 1, b)
                take_h(i, 1)

            def split_wo():
                act.wait_ge(wo_in, 16)
                act.copy(a1.wo_hi[:], wo[:]).then_inc(wo_hi_ready, 1)

            for b in range(2):
                take_x(0, b)
            pairs(act, pair, split_wo)

        @block.vector
        def _(dve):
            chain = Chain(dve, dve_chain)

            def pair(i):
                es = [dve.value_load(r.expert[0:1, bass.ds(2 * i + b, 1)], min_val=0, max_val=E - 1) for b in range(2)]
                for b in range(2):
                    dve.wait_ge(h_done, 2 * i + b + 1)
                    if later(i):
                        dve.wait_ge(h_turned, 2 * i + b - 1)
                    dve.tensor_tensor(h_sb[:, b, :], h_ps[:, b, :], b1_b[:, es[b], :], ALU.add).then_inc(h_ready, 1)
                for b in range(2):
                    dve.wait_ge(y_done, 2 * i + b + 1)
                    if later(i):
                        dve.wait_ge(stored[b], 16 * i)
                    dve.tensor_tensor(y_sb[:, b, :], y_ps[:, b, 0:D], b2_b[:, es[b], :], ALU.add).then_inc(y_ready, 1)

            dve.wait_ge(a1.wk_in, 16)
            centre(dve, chain, a1.wk, means, HD1)
            def split_wo():
                dve.wait_ge(wo_hi_ready, 1)
                dve.tensor_tensor(a1.wo_lo[:], wo[:], a1.wo_hi[:].bitcast(F32), ALU.subtract)

            dve.wait_ge(w.w_in, 16 * w.loads)
            dve.wait_ge(b2_in, 16)
            pairs(dve, pair, split_wo)


def attention_1(nc, passed, a1, bo, gq, betaq, gk, betak, gate, x_sb, ident, ctxT, y0_dram, r0, z_all,
                xm_dram, out, NB, L, D, S, NT, KC, HEADS, HD, INNER, E):
    PAIR = 2
    G = HEADS // PAIR
    TB = NT // NB
    SCALE = float(HD) ** -0.5
    WC = PAIR * S
    ROWS = HEADS * S
    JT = -(-ROWS // P)
    OH = 512 // HD
    OB = -(-HEADS // OH)
    SB = -(-G // 3)
    IC = INNER // P
    K0 = len(r0.gates)
    first_head = [j * P // S for j in range(JT)]
    last_head = [min(((j + 1) * P - 1) // S, HEADS - 1) for j in range(JT)]
    v_at, total = [], 0
    for j in range(JT):
        v_at.append(total)
        total += (last_head[j] - first_head[j] + 1) * HD
    pieces = []
    for h in range(HEADS):
        r, end = h * S, (h + 1) * S
        while r < end:
            n = min(end - r, P - r % P)
            pieces.append((h, r - h * S, n, r // P, r % P))
            r += n
    with ExitStack() as c:
        def sb(name, shape, dt=F32):
            return c.enter_context(nc.sbuf_tensor("a1_" + name, shape, dt))

        def sem(name):
            return c.enter_context(nc.semaphore("a1_" + name))

        wq, wk, wv, wo_hi, wo_lo = a1.wq, a1.wk, a1.wv, a1.wo_hi, a1.wo_lo
        bo_b = sb("bo_b", [P, D])
        gate_sb = sb("gate_w", [P, KC, E])
        k_pairs = sb("k_pairs", [P, NB, G, WC])
        v_rows = sb("v_rows", [P, NB, total])
        gq2, betaq2 = sb("gq2", [P, 1]), sb("betaq2", [P, 1])
        b_in = sem("b_in")
        setup_chain, dve_chain = sem("setup_chain"), sem("dve_chain")

        with ExitStack() as c2:
            def sb2(name, shape, dt=F32):
                return c2.enter_context(nc.sbuf_tensor("a1s_" + name, shape, dt))

            def sem2(name):
                return c2.enter_context(nc.semaphore("a1s_" + name))

            gate_rows = sb2("gate_rows", [E, D])
            v_sb = sb2("v", [S, NB, HEADS, HD])
            gk_b, betak_b = sb2("gk_b", [S, HD]), sb2("betak_b", [S, HD])
            k_sb, k_sq = sb2("k", [S, 2, HEADS, HD]), sb2("k_sq", [S, 2, HEADS, HD])
            var, rstd, tmp = sb2("var", [S, HEADS]), sb2("rstd", [S, HEADS]), sb2("tmp", [S, HEADS])
            means = sb2("means", [P, KC * HEADS])
            kn_ready, k_done, v_done, k_taken, v_taken, v_moved = (
                sem2(s) for s in ("kn_ready", "k_done", "v_done", "k_taken", "v_taken", "v_moved"))
            k_turned, k_placed, pads, gate_turned = (sem2(s) for s in ("k_turned", "k_placed", "pads", "gate_turned"))
            k_squared, k_scaled, k_by_gamma = (sem2(s) for s in ("k_squared", "k_scaled", "k_by_gamma"))
            k_ps = c2.enter_context(nc.psum_tensor("a1s_k_ps", [P, 2, 512], F32))
            v_ps = c2.enter_context(nc.psum_tensor("a1s_v_ps", [P, 2, 512], F32))
            kT_ps = c2.enter_context(nc.psum_tensor("a1s_kT_ps", [P, 2, 512], F32))
            gate_ps = c2.enter_context(nc.psum_tensor("a1s_gate_ps", [P, 512], F32))
            block = c2.enter_context(nc.Block())
            kT4 = kT_ps[:, :, :].rearrange("p b (g s) -> p b g s", g=4)

            @block.sync
            def _(sp):
                for dst, src in ((gk_b, gk), (betak_b, betak)):
                    sp.dma_start(dst[:], src.rearrange("(a d) -> a d", a=1).to_broadcast([S, HD])).then_inc(b_in, 16)
                for dst, src in ((gq2, gq), (betaq2, betaq)):
                    for h in range(PAIR):
                        sp.dma_start(dst[h * HD:(h + 1) * HD, :], src.rearrange("(d a) -> d a", a=1),
                                     allow_slow_non_contiguous=True).then_inc(b_in, 16)
                sp.dma_start(bo_b[:], bo.rearrange("(a d) -> a d", a=1).to_broadcast([P, D])).then_inc(b_in, 16)
                sp.dma_start(gate_rows[:], gate).then_inc(b_in, 16)
                sp.wait_ge(v_taken, 2 * NB)
                sp.wait_ge(pads, 2)
                for h, s0, n, j, p0 in pieces:
                    at = v_at[j] + (h - first_head[j]) * HD
                    sp.dma_start(v_rows[p0:p0 + n, :, at:at + HD], v_sb[s0:s0 + n, :, h, :]).then_inc(v_moved, 16)
                sp.wait_ge(v_moved, 16 * len(pieces))

            @block.gpsimd
            def _(pool):
                pool.memset(k_pairs[:], 0.0).then_inc(pads, 1)
                pool.memset(v_rows[:], 0.0).then_inc(pads, 1)

                def per_column(a):
                    return a.rearrange("s (a d) -> s a d", a=1).to_broadcast([S, HEADS, HD])

                pool.wait_ge(b_in, 16 * 8)
                for n in range(NB):
                    keys = k_sb[:, n % 2, :, :]
                    pool.wait_ge(k_scaled, n + 1)
                    pool.tensor_tensor(keys, keys, per_column(gk_b[:]), ALU.mult).then_inc(k_by_gamma, 1)
                    pool.wait_ge(k_by_gamma, n + 1)
                    pool.tensor_tensor(keys, keys, per_column(betak_b[:]), ALU.add).then_inc(kn_ready, 1)

            def turn_keys(pe, n):
                pe.wait_ge(kn_ready, n + 1)
                if n:
                    pe.wait_ge(k_placed, 4 * n)
                kf = k_sb[:, n % 2, :, :].rearrange("s h d -> s (h d)")
                for g in range(G):
                    last = pe.transpose(kT4[:, g // 4, g % 4, 0:S], kf[:, g * P:(g + 1) * P], ident[0:S, 0:S])
                last.then_inc(k_turned, 1)

            @block.tensor
            def _(pe):
                for n in range(NB):
                    for h in range(2):
                        if n:
                            pe.wait_ge(k_taken, 2 * n)
                        for k in range(KC):
                            last = pe.matmul(k_ps[0:S, h, :], ctxT[:, k, n * S:(n + 1) * S],
                                             wk[:, k, h * 512:(h + 1) * 512], start=(k == 0), stop=(k == KC - 1))
                        last.then_inc(k_done, 1)
                    for h in range(2):
                        if n:
                            pe.wait_ge(v_taken, 2 * n - 1 + h)
                        for k in range(KC):
                            last = pe.matmul(v_ps[0:S, h, :], ctxT[:, k, n * S:(n + 1) * S],
                                             wv[:, k, h * 512:(h + 1) * 512], start=(k == 0), stop=(k == KC - 1))
                        last.then_inc(v_done, 1)
                    if n:
                        turn_keys(pe, n - 1)
                pe.wait_ge(b_in, 16 * 8)
                for k in range(KC):
                    last = pe.transpose(gate_ps[:, k * E:(k + 1) * E], gate_rows[:, k * P:(k + 1) * P], ident[0:E, 0:E])
                last.then_inc(gate_turned, 1)
                turn_keys(pe, NB - 1)

            @block.scalar
            def _(act):
                for n in range(NB):
                    for h in range(2):
                        act.wait_ge(k_done, 2 * n + h + 1)
                        if n >= 2:
                            act.wait_ge(k_turned, n - 1)
                        ps = k_ps[0:S, h, :].rearrange("s (h d) -> s h d", d=HD)
                        act.activation(k_sq[:, n % 2, 8 * h:8 * h + 8, :], ps, ACT.Square).then_inc(k_squared, 1)
                        act.copy(k_sb[:, n % 2, 8 * h:8 * h + 8, :], ps).then_inc(k_taken, 1)
                    for h in range(2):
                        act.wait_ge(v_done, 2 * n + h + 1)
                        act.copy(v_sb[:, n, 8 * h:8 * h + 8, 0:HD],
                                 v_ps[0:S, h, :].rearrange("s (h d) -> s h d", d=HD)).then_inc(v_taken, 1)
                act.wait_ge(gate_turned, 1)
                act.copy(gate_sb[:, :, :].rearrange("p k e -> p (k e)"), gate_ps[:, 0:KC * E])

            @block.vector
            def _(dve):
                chain = Chain(dve, setup_chain)
                link = chain.link

                def per_head(a):
                    return a.rearrange("s (h a) -> s h a", a=1).to_broadcast([S, HEADS, HD])

                def place_keys(n):
                    dve.wait_ge(k_turned, n + 1)
                    dve.wait_ge(pads, 2)
                    for h in range(PAIR):
                        for b in range(2):
                            dve.tensor_copy(k_pairs[h * HD:(h + 1) * HD, n, 4 * b:4 * b + 4, h * S:(h + 1) * S],
                                            kT4[h * HD:(h + 1) * HD, b, :, 0:S]).then_inc(k_placed, 1)

                for n in range(NB):
                    keys = k_sb[:, n % 2, :, :]
                    dve.wait_ge(k_squared, 2 * n + 2)
                    link(dve.tensor_reduce(var[:], k_sq[:, n % 2, :, :], AX.X, ALU.add))
                    link(dve.tensor_scalar(var[:], var[:], 1.0 / HD, EPS, ALU.mult, ALU.add))
                    rsqrt(dve, chain, rstd[:], var[:], tmp[:])
                    dve.wait_ge(k_taken, 2 * n + 2)
                    dve.tensor_tensor(keys, keys, per_head(rstd[:]), ALU.mult).then_inc(k_scaled, 1)
                    if n:
                        place_keys(n - 1)
                dve.wait_ge(a1.w_in, 32)
                centre(dve, chain, wq, means, HD)
                place_keys(NB - 1)

        with ExitStack() as c2:
            def sb3(name, shape, dt=F32):
                return c2.enter_context(nc.sbuf_tensor("a1m_" + name, shape, dt))

            def sem3(name):
                return c2.enter_context(nc.semaphore("a1m_" + name))

            YR = 4
            index = sb3("index", [P, YR, K0], I32)
            yg = sb3("yg", [P, YR, K0, D])
            stats, mv, tmp2, var2 = sb3("stats", [P, 2, 6]), sb3("mv", [P, 2, 2]), sb3("tmp2", [P, 2]), sb3("var2", [P, 2])
            VN = 2 + HEADS
            var, rstd, tmp = sb3("var", [P, VN]), sb3("rstd", [P, VN]), sb3("tmp", [P, VN])
            xn, xn2 = sb3("xn", [P, 2, D]), sb3("xn2", [P, 2, D])
            xT, x2T = sb3("xT", [P, KC * P]), sb3("x2T", [P, 2, KC * P])
            q_sb, q_sq = sb3("q", [P, 2, INNER]), sb3("q_sq", [P, 2, INNER])
            qn = sb3("qn", [P, 2, INNER])
            qT = sb3("qT", [P, G, P])
            s_sb, e_sb = sb3("s", [P, ROWS]), sb3("e", [P, 2, JT * P])
            mx, rsum = sb3("mx", [P, HEADS]), sb3("rsum", [P, HEADS])
            eT = sb3("eT", [P, JT, P])
            o_sb = sb3("o", [P, 2, INNER])
            oT = sb3("oT", [P, IC, P])
            oT_hi, oT_lo = sb3("oT_hi", [P, IC, P], F32R), sb3("oT_lo", [P, IC, P], F32R)
            o_hi_ready, o_lo_ready = sem3("o_hi_ready"), sem3("o_lo_ready")
            y_sb = sb3("y", [P, 2, D])
            work = c2.enter_context(nc.psum_tensor("a1_work", [P, 3, 512], F32))
            s_ps = c2.enter_context(nc.psum_tensor("a1_s_ps", [P, SB, 512], F32))
            o_ps = c2.enter_context(nc.psum_tensor("a1_o_ps", [P, OB, 512], F32))
            index_ready, combined, xn_ready, qn_ready, xn2_ready = (
                sem3(s) for s in ("index_ready", "combined", "xn_ready", "qn_ready", "xn2_ready"))
            s_done, max_ready, s_taken, e_ready, o_done, o_taken = (
                sem3(s) for s in ("s_done", "max_ready", "s_taken", "e_ready", "o_done", "o_taken"))
            bo_added, x_added, x_out, sq_ready, e_pads = (
                sem3(s) for s in ("bo_added", "x_added", "x_out", "sq_ready", "e_pads"))
            gathered = [sem3(f"gathered{b}") for b in range(YR)]
            xn2_out = [sem3(f"xn2_out{b}") for b in range(2)]
            ORDER = [("xT", 0, 3, 2), ("qT", 0, 1, 0), ("qT", 1, 1, 1), ("oT", 0, -1, 2), ("oT", 1, -1, 0),
                     ("eT", 0, 0, 1), ("q", 0, 3, 2), ("eT", 1, 0, 0), ("q", 1, 3, 1), ("eT", 2, 0, 2),
                     ("z", 0, -5, 0), ("x2", 0, -4, 2), ("y", 0, -1, 1)]
            per = {kind: u + 1 for kind, u, _, _ in sorted(ORDER)}
            place = {(kind, u): i for i, (kind, u, _, _) in enumerate(ORDER)}
            assert per["eT"] == -(-JT // 4) and per["oT"] == IC // 4
            full = {kind: sem3("full_" + kind) for kind in per}
            freed = {kind: sem3("freed_" + kind) for kind in per}
            block = c2.enter_context(nc.Block())
            AHEAD, BEHIND = 5, 5

            def has(n, k):
                return not isinstance(n, int) or 0 <= TB * n + k < NT

            def wait(eng, sem, n, k, times=1, add=1):
                value = times * (TB * n + k) + add
                if not isinstance(n, int) or value > 0:
                    eng.wait_ge(sem, value)

            def bank_of(kind, u):
                return ORDER[place[kind, u]][3]

            def take(n, k, kind, u):
                slot, i = k, place[kind, u] - 1
                while slot > k - 12:
                    if i < 0:
                        i, slot = i + len(ORDER), slot - 1
                    kind2, u2, dist2, bank2 = ORDER[i]
                    if bank2 == bank_of(kind, u) and has(n, slot + dist2):
                        wait(nc.tensor, freed[kind2], n, slot + dist2, per[kind2], u2 + 1)
                        break
                    i -= 1
                return work[:, bank_of(kind, u), :]

            def program(eng, slot, chain=None, per_row=0):
                for k in range(TB - AHEAD, TB):
                    slot(-1, k)
                for k in range(TB):
                    slot(0, k)
                with eng.Fori(1, NB - 1) as n:
                    if chain:
                        chain.enter(n - 1, per_row)
                    for k in range(TB):
                        slot(n, k)
                if chain:
                    chain.leave(NB - 2)
                for k in range(TB):
                    slot(NB - 1, k)
                for k in range(BEHIND):
                    slot(NB, k)

            @block.gpsimd
            def _(pool):
                def copy_index(n, k):
                    for j in range(K0):
                        pool.tensor_copy(index[:, k % YR, j:j + 1], r0.slot[j][:, bass.ds(TB * n + k, 1)]
                                         ).then_inc(index_ready, 1)

                def slot(n, k):
                    if has(n, k - 1):
                        t = k - 1
                        for u in range(2):
                            wait(pool, o_hi_ready, n, t, 2, u + 1)
                            wait(pool, full["y"], n, t - 1)
                            at = slice(4 * u, 4 * u + 4)
                            pool.tensor_tensor(oT_lo[:, at, :], oT[:, at, :], oT_hi[:, at, :].bitcast(F32), ALU.subtract
                                               ).then_inc(o_lo_ready, 1)
                    if has(n, k + AHEAD):
                        t = k + AHEAD
                        if isinstance(n, int) and TB * n + t == 0:
                            copy_index(0, 0)
                        wait(pool, combined, n, t - YR)
                        wait(pool, index_ready, n, t, K0, K0)
                        alone(pool, passed)
                        for j in range(K0):
                            pool.indirect_dma_start(yg[:, t % YR, j, :], None, y0_dram,
                                                    bass.IndirectOffsetOnAxis(ap=index[:, t % YR, j:j + 1], axis=0)
                                                    ).then_inc(gathered[t % YR], 16)
                        if has(n, t + 1):
                            wait(pool, combined, n, t + 1 - YR)
                            alone(pool, passed)
                            copy_index(n, t + 1)
                    if has(n, k - 1):
                        t = k - 1
                        wait(pool, freed["y"], n, t)
                        pool.tensor_tensor(y_sb[:, t % 2, :], y_sb[:, t % 2, :], bo_b[:], ALU.add).then_inc(bo_added, 1)
                        wait(pool, bo_added, n, t)
                        alone(pool, passed)
                        pool.tensor_tensor(x_sb[:, TB * n + t, :], x_sb[:, TB * n + t, :], y_sb[:, t % 2, :], ALU.add
                                           ).then_inc(x_added, 1)

                program(pool, slot)

            @block.sync
            def _(sp):
                xm_rows = xm_dram.rearrange("(t p) (a d) -> t a p d", p=P, a=2)
                out_rows = out.rearrange("n (k p) d -> (n k) p d", p=P)

                def slot(n, k):
                    if has(n, k - 3):
                        t = sp.snap(TB * n + k - 3) if not isinstance(n, int) else TB * n + k - 3
                        wait(sp, xn2_ready, n, k - 3)
                        sp.dma_start(xm_rows[t, 0], xn2[:, (k - 3) % 2, :]).then_inc(xn2_out[(k - 3) % 2], 16)
                        sp.dma_start(xm_rows[t, 1], x_sb[:, t, :]).then_inc(x_out, 16)
                        sp.dma_start(out_rows[t], x_sb[:, t, :]).then_inc(x_out, 16)

                program(sp, slot)
                sp.wait_ge(x_out, 32 * NT)
                for b in range(2):
                    sp.wait_ge(xn2_out[b], 16 * (NT // 2))

            @block.tensor
            def _(pe):
                def turn(n, k, kind, u, rows, count):
                    bank = take(n, k, kind, u)
                    for j in range(count):
                        last = pe.transpose(bank[:, j * P:(j + 1) * P],
                                            rows[:, (4 * u + j) * P:(4 * u + j + 1) * P], ident[:])
                    last.then_inc(full[kind], 1)

                def turn_x(n, k, t):
                    wait(pe, xn_ready, n, t)
                    turn(n, k, "xT", 0, xn[:, t % 2, :], KC)

                def turn_q(n, k, t, u):
                    wait(pe, qn_ready, n, t)
                    turn(n, k, "qT", u, qn[:, t % 2, :], 4)

                def product(ps, a_hi, a_lo, b_hi, b_lo, start, stop):
                    pe.matmul(ps, a_hi, b_hi, start=start, stop=False)
                    pe.matmul(ps, a_hi, b_lo, start=False, stop=False)
                    return pe.matmul(ps, a_lo, b_hi, start=False, stop=stop)

                def project_q(n, k, t, u):
                    wait(pe, freed["xT"], n, t)
                    bank = take(n, k, "q", u)
                    for j in range(KC):
                        last = pe.matmul(bank, xT[:, j * P:(j + 1) * P], wq[:, j, u * 512:(u + 1) * 512],
                                         start=(j == 0), stop=(j == KC - 1))
                    last.then_inc(full["q"], 1)

                def scores(n, k, t):
                    wait(pe, freed["qT"], n, t, 2, 2)
                    wait(pe, s_taken, n, t - 1)
                    for g in range(G):
                        last = pe.matmul(s_ps[:, g // 3, (g % 3) * WC:(g % 3 + 1) * WC], qT[:, g, :],
                                         k_pairs[:, n + t // TB, g, :], start=True, stop=True)
                    last.then_inc(s_done, 1)

                def turn_e(n, k, t, u):
                    wait(pe, e_ready, n, t)
                    turn(n, k, "eT", u, e_sb[:, t % 2, :], min(4, JT - 4 * u))

                def values(n, k, t):
                    wait(pe, freed["eT"], n, t, per["eT"], per["eT"])
                    wait(pe, o_taken, n, t - 1)
                    opened = set()
                    for j in range(JT):
                        h = first_head[j]
                        while h <= last_head[j]:
                            b = h // OH
                            h1 = min(last_head[j], b * OH + OH - 1)
                            at = v_at[j] + (h - first_head[j]) * HD
                            last = pe.matmul(o_ps[:, b, (h - b * OH) * HD:(h1 - b * OH + 1) * HD], eT[:, j, :],
                                             v_rows[:, n, at:at + (h1 - h + 1) * HD], start=b not in opened,
                                             stop=True, skip_group_check=True)
                            opened.add(b)
                            h = h1 + 1
                    last.then_inc(o_done, 1)

                def turn_o(n, k, t, u):
                    wait(pe, o_taken, n, t)
                    turn(n, k, "oT", u, o_sb[:, t % 2, :], 4)

                def output(n, k, t):
                    wait(pe, o_lo_ready, n, t, per["oT"], per["oT"])
                    bank = take(n, k, "y", 0)
                    for j in range(IC):
                        last = product(bank[:, 0:D], oT_hi[:, j, :], oT_lo[:, j, :], wo_hi[:, j, :], wo_lo[:, j, :],
                                       j == 0, j == IC - 1)
                    last.then_inc(full["y"], 1)

                def turn_x2(n, k, t):
                    wait(pe, xn2_ready, n, t)
                    turn(n, k, "x2", 0, xn2[:, t % 2, :], KC)

                def logits(n, k, t):
                    wait(pe, freed["x2"], n, t)
                    bank = take(n, k, "z", 0)
                    for j in range(KC):
                        last = pe.matmul(bank[:, 0:E], x2T[:, t % 2, j * P:(j + 1) * P], gate_sb[:, j, :],
                                         start=(j == 0), stop=(j == KC - 1))
                    last.then_inc(full["z"], 1)

                def slot(n, k):
                    if has(n, k + 3):
                        turn_x(n, k, k + 3)
                    if has(n, k + 1):
                        turn_q(n, k, k + 1, 0)
                        turn_q(n, k, k + 1, 1)
                    if has(n, k - 1):
                        turn_o(n, k, k - 1, 0)
                        turn_o(n, k, k - 1, 1)
                    if has(n, k):
                        turn_e(n, k, k, 0)
                    if has(n, k + 3):
                        project_q(n, k, k + 3, 0)
                    if has(n, k):
                        turn_e(n, k, k, 1)
                    if has(n, k + 3):
                        project_q(n, k, k + 3, 1)
                    if has(n, k + 1):
                        scores(n, k, k + 1)
                    if has(n, k):
                        turn_e(n, k, k, 2)
                    if has(n, k - 5):
                        logits(n, k, k - 5)
                    if has(n, k - 4):
                        turn_x2(n, k, k - 4)
                    if has(n, k):
                        values(n, k, k)
                    if has(n, k - 1):
                        output(n, k, k - 1)

                program(pe, slot)

            @block.scalar
            def _(act):
                def take_x(n, t):
                    wait(act, full["xT"], n, t)
                    act.copy(xT[:], work[:, bank_of("xT", 0), 0:KC * P]).then_inc(freed["xT"], 1)

                def high_o(n, t, u):
                    wait(act, freed["oT"], n, t, 2, u + 1)
                    wait(act, full["y"], n, t - 1)
                    at = slice(4 * u, 4 * u + 4)
                    act.copy(oT_hi[:, at, :], oT[:, at, :]).then_inc(o_hi_ready, 1)

                def take_qT(n, t, u):
                    wait(act, full["qT"], n, t, 2, u + 1)
                    act.activation(qT[:, 4 * u:4 * u + 4, :].rearrange("p g q -> p (g q)"),
                                   work[:, bank_of("qT", u), :], ACT.Identity, bias=betaq2[:, 0:1],
                                   scale=gq2[:, 0:1]).then_inc(freed["qT"], 1)

                def take_q(n, t, u):
                    wait(act, full["q"], n, t, 2, u + 1)
                    wait(act, qn_ready, n, t - 2)
                    act.copy(q_sb[:, t % 2, u * 512:(u + 1) * 512], work[:, bank_of("q", u), :]).then_inc(freed["q"], 1)

                def squares(n, t):
                    wait(act, freed["q"], n, t, 2, 2)
                    act.activation(q_sq[:, t % 2, :], q_sb[:, t % 2, :], ACT.Square).then_inc(sq_ready, 1)

                def take_rows(n, t, kind, u, dst, count):
                    wait(act, full[kind], n, t, per[kind], u + 1)
                    if kind == "oT":
                        wait(act, o_lo_ready, n, t - 1, per[kind], u + 1)
                    act.copy(dst[:, 4 * u:4 * u + count, :].rearrange("p j q -> p (j q)"),
                             work[:, bank_of(kind, u), 0:count * P]).then_inc(freed[kind], 1)

                def take_y(n, t):
                    wait(act, full["y"], n, t)
                    wait(act, x_added, n, t - 2)
                    act.copy(y_sb[:, t % 2, :], work[:, bank_of("y", 0), 0:D]).then_inc(freed["y"], 1)

                def take_x2(n, t):
                    wait(act, full["x2"], n, t)
                    act.copy(x2T[:, t % 2, :], work[:, bank_of("x2", 0), 0:KC * P]).then_inc(freed["x2"], 1)

                def take_z(n, t):
                    wait(act, full["z"], n, t)
                    alone(act, passed)
                    act.copy(z_all[:, TB * n + t, :], work[:, bank_of("z", 0), 0:E]).then_inc(freed["z"], 1)

                def exponentials(n, t):
                    wait(act, s_taken, n, t)
                    if isinstance(n, int) and TB * n + t == 0:
                        act.wait_ge(e_pads, 1)
                    act.activation(e_sb[:, t % 2, 0:ROWS], s_sb[:], ACT.Exp, scale=SCALE).then_inc(e_ready, 1)

                def slot(n, k):
                    if has(n, k + 3):
                        take_x(n, k + 3)
                    if has(n, k + 1):
                        take_qT(n, k + 1, 0)
                    if has(n, k + 1):
                        take_qT(n, k + 1, 1)
                    if has(n, k - 1):
                        take_rows(n, k - 1, "oT", 0, oT, 4)
                        take_rows(n, k - 1, "oT", 1, oT, 4)
                        high_o(n, k - 1, 0)
                    if has(n, k):
                        take_rows(n, k, "eT", 0, eT, min(4, JT - 0))
                    if has(n, k - 1):
                        high_o(n, k - 1, 1)
                    if has(n, k + 3):
                        take_q(n, k + 3, 0)
                    if has(n, k):
                        take_rows(n, k, "eT", 1, eT, min(4, JT - 4))
                    if has(n, k + 3):
                        take_q(n, k + 3, 1)
                        squares(n, k + 3)
                    if has(n, k):
                        take_rows(n, k, "eT", 2, eT, min(4, JT - 8))
                    if has(n, k - 5):
                        take_z(n, k - 5)
                    if has(n, k - 4):
                        take_x2(n, k - 4)
                    if has(n, k + 1):
                        exponentials(n, k + 1)
                    if has(n, k - 1):
                        take_y(n, k - 1)

                program(act, slot)

            @block.vector
            def _(dve):
                chain = Chain(dve, dve_chain)
                dve.memset(e_sb[:, :, ROWS:JT * P], 0.0).then_inc(e_pads, 1)
                dve.memset(stats[:], 0.0)
                chain.link(dve.memset(var[:], 1.0))
                s_parts = [(0, 6 * (SB - 1), 6), (6 * (SB - 1), HEADS, HEADS - 6 * (SB - 1))]

                def scores(part):
                    h0, h1, nh = part
                    b0 = h0 // 6
                    return s_ps[:, b0:b0 + (h1 - h0) // nh, 0:nh * S].rearrange("p b (h s) -> p b h s", s=S)

                def slot(n, k):
                    enters, leaves, queries = has(n, k + 4), has(n, k - 3), has(n, k + 2)
                    if enters:
                        t = k + 4
                        for j in range(K0):
                            if j == 0:
                                dve.wait_ge(gathered[t % YR], 16 * K0 * ((TB // YR) * n + t // YR + 1))
                            ins = dve.scalar_tensor_tensor(x_sb[:, TB * n + t, :], yg[:, t % YR, j, :],
                                                           r0.gates[j][:, bass.ds(TB * n + t, 1)], x_sb[:, TB * n + t, :],
                                                           ALU.mult, ALU.add)
                            if j + 1 < K0:
                                chain.link(ins)
                            else:
                                ins.then_inc(combined, 1)
                                wait(dve, combined, n, t)
                                alone(dve, passed)
                        chain.step(dve.bn_stats(stats[:, 0, :], x_sb[:, TB * n + t, :]))
                    if leaves:
                        wait(dve, x_added, n, k - 3)
                        alone(dve, passed)
                        chain.step(dve.bn_stats(stats[:, 1, :], x_sb[:, TB * n + k - 3, :]))
                    if enters or leaves:
                        dve.wait_ge(chain.sem, chain.base + chain.n)
                        m0, v0, m1, v1 = (stats[:, :, c] for c in (1, 2, 4, 5))
                        chain.step(dve.tensor_tensor(mv[:, :, 0], m0, m1, ALU.add))
                        chain.step(dve.tensor_tensor(mv[:, :, 1], v0, v1, ALU.add))
                        chain.link(dve.tensor_tensor(tmp2[:], m0, m1, ALU.subtract))
                        chain.step(dve.tensor_tensor(var2[:], tmp2[:], tmp2[:], ALU.mult))
                        chain.step(dve.tensor_scalar(mv[:, :, 0], mv[:, :, 0], 0.5, None, ALU.mult))
                        chain.link(dve.tensor_scalar(mv[:, :, 1], mv[:, :, 1], 1.0 / D, EPS, ALU.mult, ALU.add))
                        chain.step(dve.scalar_tensor_tensor(var[:, 0:2], var2[:], 0.25, mv[:, :, 1], ALU.mult, ALU.add))
                    if queries:
                        wait(dve, sq_ready, n, k + 2)
                        chain.link(dve.tensor_reduce(var[:, 2:VN], q_sq[:, k % 2, :].rearrange("p (h d) -> p h d", d=HD),
                                                     AX.X, ALU.add))
                        chain.step(dve.tensor_scalar(var[:, 2:VN], var[:, 2:VN], 1.0 / HD, EPS, ALU.mult, ALU.add))
                    if enters or leaves or queries:
                        dve.wait_ge(chain.sem, chain.base + chain.n)
                        rsqrt(dve, chain, rstd[:], var[:], tmp[:])
                    if enters:
                        t = k + 4
                        wait(dve, full["xT"], n, t - 2)
                        dve.tensor_scalar(xn[:, t % 2, :], x_sb[:, TB * n + t, :], mv[:, 0, 0:1], rstd[:, 0:1],
                                          ALU.subtract, ALU.mult).then_inc(xn_ready, 1)
                    if queries:
                        t = k + 2
                        wait(dve, freed["q"], n, t, 2, 2)
                        wait(dve, full["qT"], n, t - 2, 2, 2)
                        dve.tensor_tensor(qn[:, t % 2, :].rearrange("p (h d) -> p h d", d=HD),
                                          q_sb[:, t % 2, :].rearrange("p (h d) -> p h d", d=HD),
                                          rstd[:, 2:VN].rearrange("p (h a) -> p h a", a=1).to_broadcast([P, HEADS, HD]),
                                          ALU.mult).then_inc(qn_ready, 1)
                    if leaves:
                        t = k - 3
                        rounds = (TB // 2) * n + (t - 2) // 2 + 1
                        if not isinstance(n, int) or rounds > 0:
                            dve.wait_ge(xn2_out[t % 2], 16 * rounds)
                        wait(dve, full["x2"], n, t - 2)
                        dve.tensor_scalar(xn2[:, t % 2, :], x_sb[:, TB * n + t, :], mv[:, 1, 0:1], rstd[:, 1:2],
                                          ALU.subtract, ALU.mult).then_inc(xn2_ready, 1)
                    if has(n, k):
                        wait(dve, e_ready, n, k)
                        chain.link(dve.tensor_reduce(rsum[:], e_sb[:, k % 2, 0:ROWS].rearrange("p (h s) -> p h s", s=S),
                                                     AX.X, ALU.add))
                        chain.step(dve.reciprocal(rsum[:], rsum[:]))
                    if has(n, k + 1):
                        t = k + 1
                        wait(dve, s_done, n, t)
                        chain.step(dve.tensor_reduce(mx[:, 0:s_parts[0][1]].rearrange("p (b h) -> p b h", h=6),
                                                     scores(s_parts[0]), AX.X, ALU.max))
                        dve.tensor_reduce(mx[:, s_parts[1][0]:HEADS].rearrange("p (b h) -> p b h", b=1),
                                          scores(s_parts[1]), AX.X, ALU.max).then_inc(max_ready, 1)
                        wait(dve, max_ready, n, t)
                        wait(dve, e_ready, n, t - 1)
                        for part in s_parts:
                            h0, h1, nh = part
                            nb = (h1 - h0) // nh
                            ins = dve.tensor_tensor(
                                s_sb[:, h0 * S:h1 * S].rearrange("p (b h s) -> p b h s", h=nh, s=S), scores(part),
                                mx[:, h0:h1].rearrange("p (b h a) -> p b h a", h=nh, a=1).to_broadcast([P, nb, nh, S]),
                                ALU.subtract)
                            if h0 == 0:
                                chain.step(ins)
                            else:
                                ins.then_inc(s_taken, 1)
                    if has(n, k):
                        dve.wait_ge(chain.sem, chain.base + chain.n)
                        wait(dve, o_done, n, k)
                        wait(dve, full["oT"], n, k - 2, per["oT"], per["oT"])
                        dve.tensor_tensor(o_sb[:, k % 2, :].rearrange("p (h d) -> p h d", d=HD),
                                          o_ps[:, :, :].rearrange("p b (h d) -> p (b h) d", d=HD),
                                          rsum[:, :].rearrange("p (h a) -> p h a", a=1).to_broadcast([P, HEADS, HD]),
                                          ALU.mult).then_inc(o_taken, 1)

                SLOT = (K0 - 1) + 2 + 7 + 2 + RSQRT_STEPS + 1 + 1 + 1 + 1
                program(dve, slot, chain, TB * SLOT)


def experts_1_weights(nc, keep, x_sb, E, D, H, KC):
    w = Weights()
    HC = H // P
    SIZE = KC * H + HC * D
    space = x_sb[:, :, :].rearrange("p t d -> p (t d)")
    assert 2 * SIZE <= space.shape[1]

    def kept(name, shape):
        return keep.enter_context(nc.sbuf_tensor("e1_" + name, shape, F32))

    w.raw = [space[:, b * SIZE:(b + 1) * SIZE] for b in range(2)]
    w.w1 = [w.raw[b][:, 0:KC * H].rearrange("p (k h) -> p k h", k=KC) for b in range(2)]
    w.w2 = [w.raw[b][:, KC * H:SIZE].rearrange("p (j d) -> p j d", j=HC) for b in range(2)]
    w.b1_rows, w.b2_b = kept("b1_rows", [E * HC, P]), kept("b2_b", [P, E, D])
    w.w_hi = keep.enter_context(nc.sbuf_tensor("e1_w_hi", [P, 2, SIZE], F32R))
    w.CHUNKS = 4
    w.w_hi_ready = keep.enter_context(nc.semaphore("e1_w_hi_ready"))
    w.b_in = keep.enter_context(nc.semaphore("e1_b_in"))
    w.w_in = [keep.enter_context(nc.semaphore(f"e1_w_in{b}")) for b in range(2)]
    return w


def load_expert_1(sp, w, W1, W2, e, b):
    sp.dma_start(w.w1[b], W1.rearrange("e (k p) h -> e p k h", p=P)[e]).then_inc(w.w_in[b], 16)
    sp.dma_start(w.w2[b], W2.rearrange("e (j p) d -> e p j d", p=P)[e]).then_inc(w.w_in[b], 16)


def split_high(act, w, b, q, CHUNK):
    at = slice(q * CHUNK, (q + 1) * CHUNK)
    act.copy(w.w_hi[:, b, at], w.raw[b][:, at]).then_inc(w.w_hi_ready, 1)


def split_expert_0_high(act, w, SIZE):
    act.wait_ge(w.w_in[0], 32)
    for q in range(w.CHUNKS):
        split_high(act, w, 0, q, SIZE // w.CHUNKS)


def load_experts_1(sp, w, W1, b1, W2, b2, E, D, H, KC):
    sp.dma_start(w.b1_rows[:], b1.rearrange("e (j p) -> (e j) p", p=P)).then_inc(w.b_in, 16)
    for b in range(2):
        load_expert_1(sp, w, W1, W2, b, b)
    sp.dma_start(w.b2_b[:, :, :].rearrange("p e h -> p (e h)"),
                 b2.rearrange("(a e) h -> a (e h)", a=1).to_broadcast([P, E * D])).then_inc(w.b_in, 16)


def experts_1(nc, passed, xm_dram, out, ident, r, w, W1, W2, E, D, H, KC, CT):
    HC = H // P
    CAP = CT * P
    HALVES = [(0, CAP // 2), (CAP // 2, CAP)]
    PASSES = E // 2
    HU = 2 * HC
    SIZE = KC * H + HC * D
    CHUNKS, CHUNK = w.CHUNKS, SIZE // w.CHUNKS
    EARLY = 2
    assert CHUNK * CHUNKS // 2 >= KC * H
    with ExitStack() as c:
        def sb(name, shape, dt=F32):
            return c.enter_context(nc.sbuf_tensor("e1_" + name, shape, dt))

        def sem(name):
            return c.enter_context(nc.semaphore("e1_" + name))

        b1_rows, b2_b = w.b1_rows, w.b2_b
        w_hi, w_hi_ready = w.w_hi, w.w_hi_ready
        w_lo = sb("w_lo", [P, 2, SIZE], F32R)
        b1T, b1_now = sb("b1T", [P, E, HC]), sb("b1_now", [P, 2, HC])
        source, target = sb("source", [P, 2, CT], I32), sb("target", [P, 2, CT], I32)
        xg = sb("xg", [P, 2, CT, 2 * D])
        x_kept = sb("x_kept", [P, 2, CT, D])
        xT_hi, xT_lo = sb("xT_hi", [P, KC, CAP], F32R), sb("xT_lo", [P, KC, CAP], F32R)
        h_sb = sb("h", [P, 4, CAP // 2])
        hT_hi, hT_lo = sb("hT_hi", [P, HC, CAP], F32R), sb("hT_lo", [P, HC, CAP], F32R)
        biased = sb("biased", [P, 2, D])
        y_sb = sb("y", [P, 2, CT, D])
        b1_turned, b1_ready = sem("b1_turned"), sem("b1_ready")
        source_ready, target_ready = sem("source_ready"), sem("target_ready")
        b1_copied, kept = sem("b1_copied"), sem("kept")
        w_in = w.w_in
        gathered = [sem(f"gathered{b}") for b in range(2)]
        scattered = [sem(f"scattered{b}") for b in range(2)]
        x_turned, xT_hi_ready, xT_lo_ready, w_lo_ready = (
            sem(s) for s in ("x_turned", "xT_hi_ready", "xT_lo_ready", "w_lo_ready"))
        h_done, h_ready, hT_hi_ready, hT_lo_ready, y_done, y_taken, y_ready = (
            sem(s) for s in ("h_done", "h_ready", "hT_hi_ready", "hT_lo_ready", "y_done", "y_taken", "y_ready"))
        x_ps = c.enter_context(nc.psum_tensor("e1_x_ps", [P, 2, 512], F32))
        h_ps = c.enter_context(nc.psum_tensor("e1_h_ps", [P, 4, 512], F32))
        y_ps = c.enter_context(nc.psum_tensor("e1_y_ps", [P, 2, 512], F32))
        block = c.enter_context(nc.Block())

        def experts(eng, one):
            for b in range(2):
                one(0, b)
            with eng.Fori(1, PASSES - 1) as i:
                for b in range(2):
                    one(i, b)
            for b in range(2):
                one(PASSES - 1, b)

        def later(i):
            return not isinstance(i, int) or i > 0

        def has_next(i, b):
            return not isinstance(i, int) or 2 * i + b + 1 < E

        def following(i, b):
            return (i, 1) if b == 0 else (i + 1, 0)

        @block.sync
        def _(sp):
            with sp.Fori(1, PASSES) as i:
                for b in range(2):
                    e = sp.snap(2 * i + b)
                    sp.wait_ge(w_lo_ready, CHUNKS * (2 * i + b - 1))
                    load_expert_1(sp, w, W1, W2, e, b)

        @block.gpsimd
        def _(pool):
            out_rows = out.rearrange("n l d -> (n l) d")

            def gather(i, b):
                e = 2 * i + b
                if later(i):
                    pool.wait_ge(gathered[b], 16 * CT * i)
                    pool.wait_ge(x_turned, CT * (2 * i + b - 1))
                    pool.wait_ge(kept, CT * (2 * i + b - 1))
                    alone(pool, passed)
                pool.tensor_copy(source[:, b, :], r.token[:, bass.ds(CT * e, CT)]).then_inc(source_ready, 1)
                pool.wait_ge(source_ready, e + 1)
                alone(pool, passed)
                for t in range(CT):
                    pool.indirect_dma_start(xg[:, b, t, :], None, xm_dram,
                                            bass.IndirectOffsetOnAxis(ap=source[:, b, t:t + 1], axis=0)
                                            ).then_inc(gathered[b], 16)

            def scatter(i, b, first):
                e = 2 * i + b
                if not first:
                    pool.wait_ge(scattered[b], 16 * CT * i)
                    alone(pool, passed)
                pool.tensor_copy(target[:, b, :], r.target[:, bass.ds(CT * e, CT)]).then_inc(target_ready, 1)
                pool.wait_ge(target_ready, e + 1)
                for t in range(CT):
                    pool.wait_ge(y_ready, CT * e + t + 1)
                    alone(pool, passed)
                    pool.indirect_dma_start(out_rows, bass.IndirectOffsetOnAxis(ap=target[:, b, t:t + 1], axis=0),
                                            y_sb[:, b, t, :], None, bounds_check=out_rows.shape[0] - 1,
                                            oob_is_err=False).then_inc(scattered[b], 16)

            for b in range(2):
                gather(0, b)
            for b in range(2):
                gather(1, b)
                scatter(0, b, True)
            with pool.Fori(2, PASSES) as i:
                for b in range(2):
                    gather(i, b)
                    scatter(i - 1, b, False)
            for b in range(2):
                scatter(PASSES - 1, b, False)
            for b in range(2):
                pool.wait_ge(scattered[b], 16 * CT * PASSES)

        @block.tensor
        def _(pe):
            def product(ps, a_hi, a_lo, b_hi, b_lo, start, stop):
                pe.matmul(ps, a_hi, b_hi, start=start, stop=False)
                pe.matmul(ps, a_hi, b_lo, start=False, stop=False)
                return pe.matmul(ps, a_lo, b_hi, start=False, stop=stop)

            def turn_x(i, b, tiles):
                e = 2 * i + b
                pe.wait_ge(gathered[b], 16 * (CT * i + CT))
                for t in tiles:
                    if later(i) or b or t >= 2:
                        pe.wait_ge(xT_lo_ready, CT * e + max(t - 1, 0))
                    for k in range(KC):
                        last = pe.transpose(x_ps[:, t % 2, k * P:(k + 1) * P], xg[:, b, t, k * P:(k + 1) * P], ident[:])
                    last.then_inc(x_turned, 1)

            def one(i, b):
                e = 2 * i + b
                pe.wait_ge(xT_lo_ready, CT * e + CT)
                pe.wait_ge(w_hi_ready, CHUNKS * e + CHUNKS // 2)
                pe.wait_ge(w_lo_ready, CHUNKS * e + CHUNKS // 2)
                for u in range(HU):
                    j, s = divmod(u, 2)
                    if u >= 4:
                        pe.wait_ge(h_ready, HU * e + u - 3)
                    c0, c1 = HALVES[s]
                    for k in range(KC):
                        at = k * H + j * P
                        last = product(h_ps[:, u % 4, 0:c1 - c0], w_hi[:, b, at:at + P], w_lo[:, b, at:at + P],
                                       xT_hi[:, k, c0:c1], xT_lo[:, k, c0:c1], k == 0, k == KC - 1)
                    last.then_inc(h_done, 1)
                if has_next(i, b):
                    turn_x(*following(i, b), range(EARLY))
                pe.wait_ge(hT_lo_ready, HU * e + HU)
                pe.wait_ge(w_hi_ready, CHUNKS * (e + 1))
                pe.wait_ge(w_lo_ready, CHUNKS * (e + 1))
                for t in range(CT):
                    if later(i) or b or t >= 2:
                        pe.wait_ge(y_taken, CT * e + max(t - 1, 0))
                    for j in range(HC):
                        at = KC * H + j * D
                        last = product(y_ps[:, t % 2, 0:D], hT_hi[:, j, t * P:(t + 1) * P], hT_lo[:, j, t * P:(t + 1) * P],
                                       w_hi[:, b, at:at + D], w_lo[:, b, at:at + D], j == 0, j == HC - 1)
                    last.then_inc(y_done, 1)
                    if has_next(i, b) and EARLY + t < CT:
                        turn_x(*following(i, b), [EARLY + t])

            pe.wait_ge(w.b_in, 32)
            pe.transpose(x_ps[:, 0, 0:E * HC], b1_rows[:], ident[0:E * HC, 0:E * HC]).then_inc(b1_turned, 1)
            pe.wait_ge(b1_ready, 1)
            turn_x(0, 0, range(CT))
            experts(pe, one)

        @block.scalar
        def _(act):
            def high_part(e, u):
                j, s = divmod(u, 2)
                c0, c1 = HALVES[s]
                act.wait_ge(h_ready, HU * e + u + 1)
                act.copy(hT_hi[:, j, c0:c1], h_sb[:, u % 4, 0:c1 - c0]).then_inc(hT_hi_ready, 1)

            def take_x(i, b, tiles):
                for t in tiles:
                    act.wait_ge(x_turned, CT * (2 * i + b) + t + 1)
                    act.copy(xT_hi[:, :, t * P:(t + 1) * P],
                             x_ps[:, t % 2, 0:KC * P].rearrange("p (k q) -> p k q", k=KC)).then_inc(xT_hi_ready, 1)

            def one(i, b):
                e = 2 * i + b
                act.copy(b1_now[:, b, :], b1T[:, e, :]).then_inc(b1_copied, 1)
                act.wait_ge(b1_copied, e + 1)
                for u in range(HU):
                    j, s = divmod(u, 2)
                    c0, c1 = HALVES[s]
                    act.wait_ge(h_done, HU * e + u + 1)
                    if u >= 4:
                        act.wait_ge(hT_lo_ready, HU * e + u - 3)
                    act.activation(h_sb[:, u % 4, 0:c1 - c0], h_ps[:, u % 4, 0:c1 - c0], ACT.Relu,
                                   bias=b1_now[:, b, j:j + 1]).then_inc(h_ready, 1)
                    if u:
                        high_part(e, u - 1)
                high_part(e, HU - 1)
                if has_next(i, b):
                    i2, b2 = following(i, b)
                    take_x(i2, b2, range(EARLY))
                    act.wait_ge(w_in[b2], 32 * i2 + 32)
                    if later(i2):
                        act.wait_ge(y_done, CT * (2 * i2 + b2 - 1))
                    for q in range(CHUNKS):
                        split_high(act, w, b2, q, CHUNK)
                        if EARLY + q < CT:
                            take_x(i2, b2, [EARLY + q])

            act.wait_ge(b1_turned, 1)
            act.copy(b1T[:, :, :].rearrange("p e j -> p (e j)"), x_ps[:, 0, 0:E * HC]).then_inc(b1_ready, 1)
            act.wait_ge(b1_ready, 1)
            take_x(0, 0, range(CT))
            experts(act, one)

        @block.vector
        def _(dve):
            def split(i, b, q):
                e = 2 * i + b
                dve.wait_ge(w_hi_ready, CHUNKS * e + q + 1)
                at = slice(q * CHUNK, (q + 1) * CHUNK)
                dve.tensor_tensor(w_lo[:, b, at], w.raw[b][:, at], w_hi[:, b, at].bitcast(F32), ALU.subtract
                                  ).then_inc(w_lo_ready, 1)

            def take_x(i, b, tiles):
                e = 2 * i + b
                for t in tiles:
                    dve.wait_ge(xT_hi_ready, CT * e + t + 1)
                    at = slice(t * P, (t + 1) * P)
                    dve.tensor_tensor(xT_lo[:, :, at], x_ps[:, t % 2, 0:KC * P].rearrange("p (k q) -> p k q", k=KC),
                                      xT_hi[:, :, at].bitcast(F32), ALU.subtract).then_inc(xT_lo_ready, 1)

            def keep_x(i, b):
                dve.wait_ge(gathered[b], 16 * (CT * i + CT))
                if later(i):
                    dve.wait_ge(y_ready, CT * (2 * i + b - 1))
                dve.tensor_copy(x_kept[:, b, :, :], xg[:, b, :, D:2 * D]).then_inc(kept, CT)

            def low_part(e, u):
                j, s = divmod(u, 2)
                c0, c1 = HALVES[s]
                dve.wait_ge(hT_hi_ready, HU * e + u + 1)
                dve.tensor_tensor(hT_lo[:, j, c0:c1], h_sb[:, u % 4, 0:c1 - c0], hT_hi[:, j, c0:c1].bitcast(F32),
                                  ALU.subtract).then_inc(hT_lo_ready, 1)

            def one(i, b):
                e = 2 * i + b
                for u in range(HU):
                    low_part(e, u)
                if has_next(i, b):
                    take_x(*following(i, b), range(EARLY))
                for t in range(CT):
                    dve.wait_ge(y_done, CT * e + t + 1)
                    dve.tensor_tensor(biased[:, (CT * b + t) % 2, :], y_ps[:, t % 2, 0:D], b2_b[:, e, :], ALU.add
                                      ).then_inc(y_taken, 1)
                    dve.wait_ge(y_taken, CT * e + t + 1)
                    if t == 0:
                        dve.wait_ge(kept, CT * (e + 1))
                        if later(i):
                            dve.wait_ge(scattered[b], 16 * CT * i)
                    dve.scalar_tensor_tensor(y_sb[:, b, t, :], biased[:, (CT * b + t) % 2, :],
                                             r.slot_gate[:, bass.ds(CT * e + t, 1)], x_kept[:, b, t, :],
                                             ALU.mult, ALU.add).then_inc(y_ready, 1)
                    if has_next(i, b):
                        if t < CHUNKS:
                            split(*following(i, b), t)
                        if EARLY + t < CT:
                            take_x(*following(i, b), [EARLY + t])
                        if t == CT - 1:
                            keep_x(*following(i, b))

            dve.wait_ge(w.b_in, 32)
            for q in range(CHUNKS // 2):
                split(0, 0, q)
            take_x(0, 0, range(CT))
            for q in range(CHUNKS // 2, CHUNKS):
                split(0, 0, q)
            keep_x(0, 0)
            experts(dve, one)


_INS = ['x', 'ctx_1024', 'L0_xattn_Wq', 'L0_xattn_bq', 'L0_xattn_Wk', 'L0_xattn_bk', 'L0_xattn_Wv', 'L0_xattn_bv',
        'L0_xattn_Wo', 'L0_xattn_bo', 'L0_ffn_gate', 'L0_ffn_W1', 'L0_ffn_b1', 'L0_ffn_W2', 'L0_ffn_b2',
        'L1_xattn_Wq', 'L1_xattn_Wk', 'L1_xattn_Wv', 'L1_xattn_Wo', 'L1_xattn_bo', 'L1_xattn_q_gamma',
        'L1_xattn_q_beta', 'L1_xattn_k_gamma', 'L1_xattn_k_beta', 'L1_ffn_gate_w', 'L1_ffn_w1', 'L1_ffn_b1',
        'L1_ffn_w2', 'L1_ffn_b2']
_OUTS = [((4, 1024, 256), 'float32')]


def kernel(**inputs):
    import numpy as _np
    import concourse.bacc as _bacc
    from concourse import mybir as _mybir
    from concourse.bass_utils import run_bass_kernel_spmd as _run

    nc = _bacc.Bacc("TRN2", target_bir_lowering=False, num_devices=1)
    arrays, args = {}, []
    for name in _INS:
        a = _np.ascontiguousarray(inputs[name])
        arrays[f"in_{name}_dram"] = a
        args.append(nc.dram_tensor(f"in_{name}_dram", a.shape, _mybir.dt.from_np(a.dtype), kind="ExternalInput").ap())
    for i, (shape, dtype) in enumerate(_OUTS):
        dt = _mybir.dt.from_np(_np.dtype(dtype))
        args.append(nc.dram_tensor(f"out_{i}_dram", shape, dt, kind="ExternalOutput").ap())
    build_layers(nc, *args)
    r = _run(nc, [arrays], core_ids=[0])
    got = tuple(r.results[0][f"out_{i}_dram"] for i in range(len(_OUTS)))
    return got[0]
```
